# Optimizing a Trainium2 kernel written in Bass

```python
import numpy as np
import jax
import jax.numpy as jnp

def _softmax(x, axis=-1):
    return jax.nn.softmax(x, axis=axis)

def _gelu(x):
    return jax.nn.gelu(x, approximate=True)

def _silu(x):
    return jax.nn.silu(x)

def _sigmoid(x):
    return jax.nn.sigmoid(x)

def _layernorm(x, axis=-1, eps=1e-05):
    m = jnp.mean(x, axis=axis, keepdims=True)
    v = jnp.var(x, axis=axis, keepdims=True)
    return (x - m) / jnp.sqrt(v + eps)

def _scatter_add(tgt, idx, src, axis=0):
    return tgt.at[idx].add(src)

def _segment_sum(src, seg, n):
    return jax.ops.segment_sum(src, seg, n)
kernel_name = 'mk_adaln_ffn_d4_seqx_r8_c4186f'

def setup_inputs(seed: int=0):
    np.random.seed(seed)
    _w = jnp.asarray

    def _rec_inputs():
        import jax
        import jax.numpy as jnp
        _rk = jax.random.key(seed)
        x = -0.0002928 + 1 * jax.random.normal(jax.random.fold_in(_rk, 1), (8, 128, 128), jnp.float32)
        _lenS = 128 - jax.random.randint(jax.random.fold_in(_rk, 7), (8,), 0, max(1, 128 // 4) + 1, jnp.int32)
        _lenS2 = 128 - jax.random.randint(jax.random.fold_in(_rk, 8), (8,), 0, max(1, 128 // 4) + 1, jnp.int32)
        cond_1024 = 0.0061147 + 1.02565 * jax.random.normal(jax.random.fold_in(_rk, 11), (8, 128), jnp.float32)
        fside_Bx1x1024x16_0 = 0.00222621 + 0.99962 * jax.random.normal(jax.random.fold_in(_rk, 12), (8, 1, 128, 16), jnp.float32)
        return (x, cond_1024, fside_Bx1x1024x16_0)
    x, cond_1024, fside_Bx1x1024x16_0 = _rec_inputs()

    def _L0_cond_setup():
        import jax, jax.numpy as jnp
        import numpy as np
        D, HS, HE, E, K = (128, 256, 128, 8, 2)
        B, T = (4, 128)
        N_SHARED = 1
        key = jax.random.key(seed)
        ks = jax.random.split(key, 9)
        g = lambda k, shape, s: jax.random.normal(k, shape, jnp.float32) * s
        return {'x': g(ks[0], (B, T, D), 1.0), 't_emb': g(ks[1], (B, D), 1.0), 'router_W': g(ks[2], (2 * D, E), 0.01), 'router_bias': jnp.zeros((E,), jnp.float32), 'w1': g(ks[3], (D, HS), 0.02), 'w3': g(ks[4], (D, HS), 0.02), 'w2': g(ks[5], (HS, D), 0.02), 'W1e': g(ks[6], (E, D, HE), 0.02), 'W2e': g(ks[7], (E, HE, D), 0.02)}
    _L0_cond_all = _L0_cond_setup()
    _L0_cond_in = {k: v for k, v in _L0_cond_all.items() if k in ('router_W', 'router_bias', 'w1', 'w3', 'w2', 'W1e', 'W2e')}
    del _L0_cond_all

    def _L0_ffn_setup():
        import jax, jax.numpy as jnp
        import numpy as np
        N_EMBD = 128
        EXPERT_SIZES = [(4, 128), (4, 256)]
        TOP_K = 2
        B, S = (1, 256)
        WIDTHS = []
        for count, size in EXPERT_SIZES:
            WIDTHS += [size] * count
        OFFSETS = np.concatenate([[0], np.cumsum(WIDTHS)]).astype(np.int64)
        E = len(WIDTHS)
        TOTAL_W = int(OFFSETS[-1])
        MAX_W = max(WIDTHS)

        def _stack_experts(w1, w2):
            W1e, W2e = ([], [])
            for e in range(E):
                off, wd = (int(OFFSETS[e]), WIDTHS[e])
                pad = MAX_W - wd
                W1e.append(jnp.pad(w1[:, off:off + wd], ((0, 0), (0, pad))))
                W2e.append(jnp.pad(w2[off:off + wd, :], ((0, pad), (0, 0))))
            return (jnp.stack(W1e), jnp.stack(W2e))
        key = jax.random.key(seed)
        k1, k2, k3, k4 = jax.random.split(key, 4)
        x = jax.random.normal(k1, (B, S, N_EMBD), jnp.float32)
        router_w = jax.random.normal(k2, (E, N_EMBD), jnp.float32) * 0.02
        w1 = jax.random.truncated_normal(k3, -3.0, 3.0, (N_EMBD, TOTAL_W), jnp.float32) * 0.02
        w2 = jax.random.truncated_normal(k4, -3.0, 3.0, (TOTAL_W, N_EMBD), jnp.float32) * 0.02
        return {'x': x, 'router_w': router_w, 'w1': w1, 'w2': w2}
    _L0_ffn_all = _L0_ffn_setup()
    _L0_ffn_in = {k: v for k, v in _L0_ffn_all.items() if k in ('router_w', 'w1', 'w2')}
    del _L0_ffn_all

    def _L1_cond_setup():
        import jax, jax.numpy as jnp
        import numpy as np
        B, T, D_IN, V_IN, E = (64, 128, 128, 128, 128)
        key = jax.random.key(seed)
        ks = jax.random.split(key, 16)
        s = 0.01
        return {'video': jax.random.normal(ks[0], (B, V_IN), jnp.float32), 'seq': jax.random.normal(ks[1], (B, T, D_IN), jnp.float32), 'W_z': jax.random.normal(ks[2], (D_IN, E), jnp.float32) * s, 'U_z': jax.random.normal(ks[3], (E, E), jnp.float32) * s, 'C_z': jax.random.normal(ks[4], (V_IN, E), jnp.float32) * s, 'b_z': jnp.zeros((E,), jnp.float32), 'W_r': jax.random.normal(ks[5], (D_IN, E), jnp.float32) * s, 'U_r': jax.random.normal(ks[6], (E, E), jnp.float32) * s, 'C_r': jax.random.normal(ks[7], (V_IN, E), jnp.float32) * s, 'b_r': jnp.zeros((E,), jnp.float32), 'W': jax.random.normal(ks[8], (D_IN, E), jnp.float32) * s, 'U': jax.random.normal(ks[9], (E, E), jnp.float32) * s, 'C': jax.random.normal(ks[10], (V_IN, E), jnp.float32) * s, 'b': jnp.zeros((E,), jnp.float32)}
    _L1_cond_all = _L1_cond_setup()
    _L1_cond_in = {k: v for k, v in _L1_cond_all.items() if k in ('W_z', 'U_z', 'C_z', 'b_z', 'W_r', 'U_r', 'C_r', 'b_r', 'W', 'U', 'C', 'b')}
    del _L1_cond_all

    def _L1_ffn_setup():
        import jax, jax.numpy as jnp
        import numpy as np
        TOP_K = 2
        key = jax.random.key(seed)
        ks = jax.random.split(key, 8)
        B, S, D, E = (4, 256, 128, 8)
        H = 4 * D
        x = jax.random.normal(ks[0], (B, S, D), dtype=jnp.float32)
        W1 = jax.random.normal(ks[1], (E, D, H), dtype=jnp.float32) * np.sqrt(2.0 / (D + H))
        b1 = jax.random.normal(ks[2], (E, H), dtype=jnp.float32) * 1e-06
        W2 = jax.random.normal(ks[3], (E, H, D), dtype=jnp.float32) * np.sqrt(2.0 / (H + D))
        b2 = jax.random.normal(ks[4], (E, D), dtype=jnp.float32) * 1e-06
        gate_w = jax.random.normal(ks[5], (D, E), dtype=jnp.float32) * np.sqrt(1.0 / D)
        gate_b = jnp.zeros((E,), dtype=jnp.float32)
        temperature = jnp.asarray(1.0, dtype=jnp.float32)
        return {'x': x, 'W1': W1, 'b1': b1, 'W2': W2, 'b2': b2, 'gate_w': gate_w, 'gate_b': gate_b, 'temperature': temperature}
    _L1_ffn_all = _L1_ffn_setup()
    _L1_ffn_in = {k: v for k, v in _L1_ffn_all.items() if k in ('W1', 'b1', 'W2', 'b2', 'gate_w', 'gate_b', 'temperature')}
    del _L1_ffn_all

    def _L2_cond_setup():
        import jax, jax.numpy as jnp
        import numpy as np
        B, F_, IN, OUT, R = (32, 64, 128, 128, 16)
        key = jax.random.key(seed)
        ks = jax.random.split(key, 6)
        x = jax.random.normal(ks[0], (B, F_, IN), dtype=jnp.float32)
        u = jax.random.normal(ks[1], (B, 1, OUT, R), dtype=jnp.float32)
        v = jax.random.normal(ks[2], (B, 1, IN, R), dtype=jnp.float32)
        b = jax.random.normal(ks[3], (B, 1, OUT), dtype=jnp.float32)
        lim = 1.0 / np.sqrt(IN)
        W = jax.random.uniform(ks[4], (OUT, IN), minval=-lim, maxval=lim, dtype=jnp.float32)
        fc_bias = jax.random.uniform(ks[5], (OUT,), minval=-lim, maxval=lim, dtype=jnp.float32)
        return {'x': x, 'u': u, 'v': v, 'b': b, 'W': W, 'fc_bias': fc_bias}
    _L2_cond_all = _L2_cond_setup()
    _L2_cond_in = {k: v for k, v in _L2_cond_all.items() if k in ('W', 'fc_bias')}
    del _L2_cond_all

    def _L2_ffn_setup():
        import jax, jax.numpy as jnp
        import numpy as np
        H = 128
        E = 8
        TOP_K = 2
        F = 512
        B, S = (4, 256)
        key = jax.random.key(seed)
        ks = jax.random.split(key, 8)
        sc = 0.02
        return {'x': jax.random.normal(ks[0], (B, S, H), dtype=jnp.float32), 'gate_w': jax.random.normal(ks[1], (H, E), dtype=jnp.float32) * sc, 'gate_b': jnp.zeros((E,), dtype=jnp.float32), 'w1': jax.random.normal(ks[2], (E, H, F), dtype=jnp.float32) * sc, 'b1': jnp.zeros((E, F), dtype=jnp.float32), 'w2': jax.random.normal(ks[3], (E, F, H), dtype=jnp.float32) * sc, 'b2': jnp.zeros((E, H), dtype=jnp.float32)}
    _L2_ffn_all = _L2_ffn_setup()
    _L2_ffn_in = {k: v for k, v in _L2_ffn_all.items() if k in ('gate_w', 'gate_b', 'w1', 'b1', 'w2', 'b2')}
    del _L2_ffn_all

    def _L3_cond_setup():
        import jax, jax.numpy as jnp
        import numpy as np
        N, T, D, H = (64, 64, 128, 128)
        key = jax.random.key(seed)
        k1, k2, k3, k4 = jax.random.split(key, 4)
        x = jax.random.normal(k1, (N, T, D), dtype=jnp.float32)
        h0 = jax.random.normal(k2, (N, H), dtype=jnp.float32)
        Wx = jax.random.normal(k3, (D, H), dtype=jnp.float32) / jnp.sqrt(jnp.float32(D))
        Wh = jax.random.normal(k4, (H, H), dtype=jnp.float32) / jnp.sqrt(jnp.float32(H))
        b = jnp.zeros((H,), dtype=jnp.float32)
        return {'x': x, 'h0': h0, 'Wx': Wx, 'Wh': Wh, 'b': b}
    _L3_cond_all = _L3_cond_setup()
    _L3_cond_in = {k: v for k, v in _L3_cond_all.items() if k in ('Wx', 'Wh', 'b')}
    del _L3_cond_all

    def _L3_ffn_setup():
        import jax, jax.numpy as jnp
        import numpy as np
        K = 3
        TAU = 1.0
        EPS = 1e-08

        def _route_dense(z, k, tau):
            topi = jax.lax.top_k(z, k)[1]
            topv = jnp.take_along_axis(z, topi, axis=1)
            w = jax.nn.softmax(topv / (tau + EPS), axis=1)
            N, L = z.shape
            dw = jnp.zeros((N, L), z.dtype)
            dw = dw.at[jnp.arange(N)[:, None], topi].add(w)
            return dw

        def _apply_mixture(x, dw, W):
            y = jnp.zeros((x.shape[0], W.shape[1]), x.dtype)
            for e in range(W.shape[0]):
                y = y + x @ W[e].T * dw[:, e:e + 1]
            return y
        key = jax.random.key(seed)
        ks = jax.random.split(key, 8)
        B, T, D_in, H, D_out, L, d_addr = (4, 256, 128, 512, 128, 12, 64)

        def unitize(U):
            U = U - U.mean(axis=1, keepdims=True)
            return U / (jnp.linalg.norm(U, axis=1, keepdims=True) + EPS)
        x = jax.random.normal(ks[0], (B, T, D_in), jnp.float32)
        P_w = jax.random.normal(ks[1], (d_addr, D_in), jnp.float32) / np.sqrt(D_in)
        U1 = unitize(jax.random.normal(ks[2], (L, d_addr), jnp.float32))
        U2 = unitize(jax.random.normal(ks[3], (L, d_addr), jnp.float32))
        U3 = unitize(jax.random.normal(ks[4], (L, d_addr), jnp.float32))
        W1 = jax.random.normal(ks[5], (L, H, D_in), jnp.float32)
        W1 = W1 / jnp.linalg.norm(W1.reshape(L, -1), axis=1)[:, None, None]
        W2 = jax.random.normal(ks[6], (L, D_out, H), jnp.float32)
        W2 = W2 / jnp.linalg.norm(W2.reshape(L, -1), axis=1)[:, None, None]
        b2 = jax.random.normal(ks[7], (L, D_out), jnp.float32)
        b2 = b2 / jnp.linalg.norm(b2, axis=1, keepdims=True)
        return {'x': x, 'P_w': P_w, 'U1': U1, 'U2': U2, 'U3': U3, 'W1': W1, 'W2': W2, 'b2': b2}
    _L3_ffn_all = _L3_ffn_setup()
    _L3_ffn_in = {k: v for k, v in _L3_ffn_all.items() if k in ('P_w', 'U1', 'U2', 'U3', 'W1', 'W2', 'b2')}
    del _L3_ffn_all
    return {'x': x, 'cond_1024': cond_1024, 'fside_Bx1x1024x16_0': fside_Bx1x1024x16_0, 'L0_cond_router_W': _L0_cond_in['router_W'], 'L0_cond_router_bias': _L0_cond_in['router_bias'], 'L0_cond_w1': _L0_cond_in['w1'], 'L0_cond_w3': _L0_cond_in['w3'], 'L0_cond_w2': _L0_cond_in['w2'], 'L0_cond_W1e': _L0_cond_in['W1e'], 'L0_cond_W2e': _L0_cond_in['W2e'], 'L0_ffn_router_w': _L0_ffn_in['router_w'], 'L0_ffn_w1': _L0_ffn_in['w1'], 'L0_ffn_w2': _L0_ffn_in['w2'], 'L1_cond_W_z': _L1_cond_in['W_z'], 'L1_cond_U_z': _L1_cond_in['U_z'], 'L1_cond_C_z': _L1_cond_in['C_z'], 'L1_cond_b_z': _L1_cond_in['b_z'], 'L1_cond_W_r': _L1_cond_in['W_r'], 'L1_cond_U_r': _L1_cond_in['U_r'], 'L1_cond_C_r': _L1_cond_in['C_r'], 'L1_cond_b_r': _L1_cond_in['b_r'], 'L1_cond_W': _L1_cond_in['W'], 'L1_cond_U': _L1_cond_in['U'], 'L1_cond_C': _L1_cond_in['C'], 'L1_cond_b': _L1_cond_in['b'], 'L1_ffn_W1': _L1_ffn_in['W1'], 'L1_ffn_b1': _L1_ffn_in['b1'], 'L1_ffn_W2': _L1_ffn_in['W2'], 'L1_ffn_b2': _L1_ffn_in['b2'], 'L1_ffn_gate_w': _L1_ffn_in['gate_w'], 'L1_ffn_gate_b': _L1_ffn_in['gate_b'], 'L1_ffn_temperature': _L1_ffn_in['temperature'], 'L2_cond_W': _L2_cond_in['W'], 'L2_cond_fc_bias': _L2_cond_in['fc_bias'], 'L2_ffn_gate_w': _L2_ffn_in['gate_w'], 'L2_ffn_gate_b': _L2_ffn_in['gate_b'], 'L2_ffn_w1': _L2_ffn_in['w1'], 'L2_ffn_b1': _L2_ffn_in['b1'], 'L2_ffn_w2': _L2_ffn_in['w2'], 'L2_ffn_b2': _L2_ffn_in['b2'], 'L3_cond_Wx': _L3_cond_in['Wx'], 'L3_cond_Wh': _L3_cond_in['Wh'], 'L3_cond_b': _L3_cond_in['b'], 'L3_ffn_P_w': _L3_ffn_in['P_w'], 'L3_ffn_U1': _L3_ffn_in['U1'], 'L3_ffn_U2': _L3_ffn_in['U2'], 'L3_ffn_U3': _L3_ffn_in['U3'], 'L3_ffn_W1': _L3_ffn_in['W1'], 'L3_ffn_W2': _L3_ffn_in['W2'], 'L3_ffn_b2': _L3_ffn_in['b2']}

def reference(x, cond_1024, fside_Bx1x1024x16_0, L0_cond_router_W, L0_cond_router_bias, L0_cond_w1, L0_cond_w3, L0_cond_w2, L0_cond_W1e, L0_cond_W2e, L0_ffn_router_w, L0_ffn_w1, L0_ffn_w2, L1_cond_W_z, L1_cond_U_z, L1_cond_C_z, L1_cond_b_z, L1_cond_W_r, L1_cond_U_r, L1_cond_C_r, L1_cond_b_r, L1_cond_W, L1_cond_U, L1_cond_C, L1_cond_b, L1_ffn_W1, L1_ffn_b1, L1_ffn_W2, L1_ffn_b2, L1_ffn_gate_w, L1_ffn_gate_b, L1_ffn_temperature, L2_cond_W, L2_cond_fc_bias, L2_ffn_gate_w, L2_ffn_gate_b, L2_ffn_w1, L2_ffn_b1, L2_ffn_w2, L2_ffn_b2, L3_cond_Wx, L3_cond_Wh, L3_cond_b, L3_ffn_P_w, L3_ffn_U1, L3_ffn_U2, L3_ffn_U3, L3_ffn_W1, L3_ffn_W2, L3_ffn_b2):
    import jax
    import jax.numpy as jnp

    def _L0_cond_ref(x, t_emb, router_W, router_bias, w1, w3, w2, W1e, W2e):
        import jax, jax.numpy as jnp
        import numpy as np
        D, HS, HE, E, K = (128, 256, 128, 8, 2)
        B, T = (4, 128)
        N_SHARED = 1
        Bb, Tt, C = x.shape
        xf = x.reshape(-1, C)
        tf = jnp.broadcast_to(t_emb[:, None, :], (Bb, Tt, C)).reshape(-1, C)
        N = xf.shape[0]
        shared = jax.nn.silu(xf @ w1) * (xf @ w3) @ w2
        s = jax.nn.sigmoid((jnp.concatenate([xf, tf], axis=-1) @ router_W).astype(jnp.float32))
        sel_scores = s + router_bias
        _, topk_idx = jax.lax.top_k(sel_scores, K)
        s_sel = jnp.take_along_axis(s, topk_idx, axis=1)
        denom = s_sel.sum(axis=1, keepdims=True)
        gates = jnp.where(denom > 1e-09, s_sel / (denom + 1e-09), 1.0 / K).astype(x.dtype)
        combine = jnp.zeros((N, E), x.dtype).at[jnp.arange(N)[:, None], topk_idx].add(gates)
        h = jax.nn.gelu(jnp.einsum('nc,ech->enh', xf, W1e), approximate=False)
        y = jnp.einsum('enh,ehc->enc', h, W2e)
        routed = jnp.einsum('ne,enc->nc', combine, y)
        return ((shared + routed) / (N_SHARED + K)).reshape(Bb, Tt, C)

    def _L0_ffn_ref(x, router_w, w1, w2):
        import jax, jax.numpy as jnp
        import numpy as np
        N_EMBD = 128
        EXPERT_SIZES = [(4, 128), (4, 256)]
        TOP_K = 2
        B, S = (1, 256)
        WIDTHS = []
        for count, size in EXPERT_SIZES:
            WIDTHS += [size] * count
        OFFSETS = np.concatenate([[0], np.cumsum(WIDTHS)]).astype(np.int64)
        E = len(WIDTHS)
        TOTAL_W = int(OFFSETS[-1])
        MAX_W = max(WIDTHS)

        def _stack_experts(w1, w2):
            W1e, W2e = ([], [])
            for e in range(E):
                off, wd = (int(OFFSETS[e]), WIDTHS[e])
                pad = MAX_W - wd
                W1e.append(jnp.pad(w1[:, off:off + wd], ((0, 0), (0, pad))))
                W2e.append(jnp.pad(w2[off:off + wd, :], ((0, pad), (0, 0))))
            return (jnp.stack(W1e), jnp.stack(W2e))
        b, s, d = x.shape
        xf = x.reshape(-1, d)
        logits = xf @ router_w.T
        probs = jax.nn.sigmoid(logits.astype(jnp.float32))
        topw, sel = jax.lax.top_k(probs, TOP_K)
        topw = topw / (topw.sum(-1, keepdims=True) + 1e-20)
        topw = topw.astype(x.dtype)
        onehot = sel[:, :, None] == jnp.arange(E)[None, None, :]
        combine = jnp.sum(topw[:, :, None] * onehot, axis=1)
        W1e, W2e = _stack_experts(w1, w2)
        h = jnp.einsum('td,edw->tew', xf, W1e)
        h = jnp.square(jax.nn.relu(h))
        y = jnp.einsum('tew,ewd->ted', h, W2e)
        out = jnp.einsum('ted,te->td', y, combine)
        return out.reshape(b, s, d)

    def _L1_cond_ref(video, seq, W_z, U_z, C_z, b_z, W_r, U_r, C_r, b_r, W, U, C, b):
        import jax, jax.numpy as jnp
        import numpy as np
        B, T, D_IN, V_IN, E = (64, 128, 128, 128, 128)
        vz = video @ C_z + b_z
        vr = video @ C_r + b_r
        vh = video @ C + b
        xz = jnp.einsum('btd,de->bte', seq, W_z)
        xr = jnp.einsum('btd,de->bte', seq, W_r)
        xh = jnp.einsum('btd,de->bte', seq, W)

        def step(h, xs):
            xzt, xrt, xht = xs
            z = jax.nn.sigmoid(xzt + h @ U_z + vz)
            r = jax.nn.sigmoid(xrt + h @ U_r + vr)
            hh = jnp.tanh(xht + r * h @ U + vh)
            h_new = (1.0 - z) * h + z * hh
            return (h_new, h_new)
        h0 = jnp.zeros((seq.shape[0], U.shape[0]), seq.dtype)
        xs = (jnp.swapaxes(xz, 0, 1), jnp.swapaxes(xr, 0, 1), jnp.swapaxes(xh, 0, 1))
        _, out_t = jax.lax.scan(step, h0, xs)
        return jnp.swapaxes(out_t, 0, 1)

    def _L1_ffn_ref(x, W1, b1, W2, b2, gate_w, gate_b, temperature):
        import jax, jax.numpy as jnp
        import numpy as np
        TOP_K = 2
        gates = (jnp.einsum('bsd,de->bse', x, gate_w) + gate_b) / temperature
        weights, indices = jax.lax.top_k(gates, TOP_K)
        weights = jax.nn.softmax(weights, axis=-1)
        h = jnp.einsum('bsd,edf->bsef', x, W1) + b1
        h = jax.nn.gelu(h, approximate=False)
        all_out = jnp.einsum('bsef,efd->bsed', h, W2) + b2
        expert_out = jnp.take_along_axis(all_out, indices[..., None], axis=2)
        out = jnp.sum(expert_out * weights[..., None], axis=2)
        return out

    def _L2_cond_ref(x, u, v, b, W, fc_bias):
        import jax, jax.numpy as jnp
        import numpy as np
        B, F_, IN, OUT, R = (32, 64, 128, 128, 16)
        inch = x.shape[-1]
        r = v.shape[-1]
        z1 = jnp.einsum('bfi,bir->bfr', x, v[:, 0]) / inch
        z = jnp.einsum('bfr,bor->bfo', z1, u[:, 0]) / r
        y = jnp.einsum('bfi,oi->bfo', x, W) + fc_bias + z + b
        return jax.nn.gelu(y, approximate=False)

    def _L2_ffn_ref(x, gate_w, gate_b, w1, b1, w2, b2):
        import jax, jax.numpy as jnp
        import numpy as np
        H = 128
        E = 8
        TOP_K = 2
        F = 512
        B, S = (4, 256)
        bsz, seq, h = x.shape
        flat = x.reshape(-1, h)
        T = flat.shape[0]
        logits = flat @ gate_w + gate_b
        weights = jax.nn.softmax(logits, axis=-1)
        top_w, top_i = jax.lax.top_k(weights, TOP_K)
        top_w = top_w / jnp.clip(top_w.sum(axis=-1, keepdims=True), 1e-06)
        comb = jnp.zeros((T, weights.shape[-1]), dtype=flat.dtype)
        comb = comb.at[jnp.arange(T)[:, None], top_i].add(top_w)
        out = jnp.zeros_like(flat)
        for e in range(w1.shape[0]):
            hdn = jax.nn.gelu(flat @ w1[e] + b1[e], approximate=False)
            out = out + (hdn @ w2[e] + b2[e]) * comb[:, e:e + 1]
        return out.reshape(bsz, seq, h)

    def _L3_cond_ref(x, h0, Wx, Wh, b):
        import jax, jax.numpy as jnp
        import numpy as np
        N, T, D, H = (64, 64, 128, 128)
        xw = jnp.einsum('ntd,dh->nth', x, Wx) + b

        def step(prev_h, xw_t):
            next_h = jnp.tanh(xw_t + prev_h @ Wh)
            return (next_h, next_h)
        _, hs = jax.lax.scan(step, h0, jnp.swapaxes(xw, 0, 1))
        return jnp.swapaxes(hs, 0, 1)

    def _L3_ffn_ref(x, P_w, U1, U2, U3, W1, W2, b2):
        import jax, jax.numpy as jnp
        import numpy as np
        K = 3
        TAU = 1.0
        EPS = 1e-08

        def _route_dense(z, k, tau):
            topi = jax.lax.top_k(z, k)[1]
            topv = jnp.take_along_axis(z, topi, axis=1)
            w = jax.nn.softmax(topv / (tau + EPS), axis=1)
            N, L = z.shape
            dw = jnp.zeros((N, L), z.dtype)
            dw = dw.at[jnp.arange(N)[:, None], topi].add(w)
            return dw

        def _apply_mixture(x, dw, W):
            y = jnp.zeros((x.shape[0], W.shape[1]), x.dtype)
            for e in range(W.shape[0]):
                y = y + x @ W[e].T * dw[:, e:e + 1]
            return y
        B, T, D = x.shape
        x_flat = x.reshape(B * T, D)
        x_addr = x_flat @ P_w.T
        dw1 = _route_dense(x_addr @ U1.T, K, TAU)
        dw2 = _route_dense(x_addr @ U2.T, K, TAU)
        dw3 = _route_dense(x_addr @ U3.T, K, TAU)
        h = _apply_mixture(x_flat, dw1, W1)
        h = jax.nn.gelu(h, approximate=False)
        y = _apply_mixture(h, dw2, W2)
        y = y + dw3 @ b2
        return y.reshape(B, T, -1)
    x = x + _L0_ffn_ref(_L0_cond_ref(x, cond_1024, L0_cond_router_W, L0_cond_router_bias, L0_cond_w1, L0_cond_w3, L0_cond_w2, L0_cond_W1e, L0_cond_W2e), L0_ffn_router_w, L0_ffn_w1, L0_ffn_w2)
    x = x + _L1_ffn_ref(_L1_cond_ref(cond_1024, x, L1_cond_W_z, L1_cond_U_z, L1_cond_C_z, L1_cond_b_z, L1_cond_W_r, L1_cond_U_r, L1_cond_C_r, L1_cond_b_r, L1_cond_W, L1_cond_U, L1_cond_C, L1_cond_b), L1_ffn_W1, L1_ffn_b1, L1_ffn_W2, L1_ffn_b2, L1_ffn_gate_w, L1_ffn_gate_b, L1_ffn_temperature)
    x = x + _L2_ffn_ref(_L2_cond_ref(x, fside_Bx1x1024x16_0, fside_Bx1x1024x16_0, cond_1024[:, None, :], L2_cond_W, L2_cond_fc_bias), L2_ffn_gate_w, L2_ffn_gate_b, L2_ffn_w1, L2_ffn_b1, L2_ffn_w2, L2_ffn_b2)
    x = x + _L3_ffn_ref(_L3_cond_ref(x, cond_1024, L3_cond_Wx, L3_cond_Wh, L3_cond_b), L3_ffn_P_w, L3_ffn_U1, L3_ffn_U2, L3_ffn_U3, L3_ffn_W1, L3_ffn_W2, L3_ffn_b2)
    return x

_drawn_inputs = setup_inputs


def setup_inputs(seed=0):
    import zlib

    import numpy as np

    out = dict(_drawn_inputs(seed))
    spreads = {'L0_cond_router_bias': (0.0, 0.8),
     'L1_cond_b_z': (0.0, 2.0),
     'L1_cond_b_r': (0.0, 2.0),
     'L1_cond_b': (0.0, 0.8),
     'L1_ffn_gate_b': (0.0, 0.8),
     'L2_ffn_gate_b': (0.0, 0.8),
     'L2_ffn_b1': (0.0, 2.0),
     'L2_ffn_b2': (0.0, 0.8),
     'L3_cond_b': (0.0, 2.0)}
    factors = {'fside_Bx1x1024x16_0': 6.233,
     'L0_cond_router_W': 8.0,
     'L0_cond_w1': 8.0,
     'L0_cond_w3': 8.0,
     'L0_cond_w2': 8.0,
     'L0_cond_W1e': 8.0,
     'L0_cond_W2e': 8.0,
     'L0_ffn_router_w': 8.0,
     'L0_ffn_w1': 8.0,
     'L0_ffn_w2': 8.0,
     'L1_cond_W_z': 44.168,
     'L1_cond_U_z': 64.0,
     'L1_cond_C_z': 64.0,
     'L1_cond_W_r': 64.0,
     'L1_cond_U_r': 64.0,
     'L1_cond_C_r': 64.0,
     'L1_cond_U': 47.792,
     'L1_ffn_b1': 64.0,
     'L1_ffn_b2': 64.0,
     'L2_cond_fc_bias': 33.384,
     'L3_ffn_U1': 64.0,
     'L3_ffn_U2': 64.0,
     'L3_ffn_W1': 64.0,
     'L3_ffn_W2': 64.0,
     'L1_cond_W': 5.157,
     'L1_cond_C': 8.0,
     'L1_ffn_W1': 5.333,
     'L1_ffn_W2': 5.109,
     'L1_ffn_gate_w': 5.79,
     'L3_cond_Wx': 8.0,
     'L3_cond_Wh': 8.0,
     'L3_ffn_P_w': 8.0,
     'L3_ffn_U3': 8.0,
     'L3_ffn_b2': 8.0}
    for name, (base, spread) in spreads.items():
        noise = np.random.default_rng([zlib.crc32(name.encode()), seed]).standard_normal(out[name].shape)
        drawn = base * np.exp(spread * noise) if base else spread * noise
        out[name] = jnp.asarray(drawn.astype(out[name].dtype))
    for name, factor in factors.items():
        out[name] = (out[name] * factor).astype(out[name].dtype)
    return out
```

```python
from contextlib import ExitStack

import concourse.bass as bass
from concourse import mybir

F32 = mybir.dt.float32
ALU = mybir.AluOpType
ACT = mybir.ActivationFunctionType
AX = mybir.AxisListType

P = 128
B, T, D = 8, 128, 128
CT = 32
CHUNKS = T // CT
N = CT * B
TILES = N // P
E = 8
E3 = 12
NR3 = 3
F = 512
Q = F // P
R = 16
DA = 64
LU = E * Q // 2
RSQRT2 = 0.5 ** 0.5

U_X, U_PREP, U_L0, U_L12, U_L3 = 2, 2 * E3, 12, 2 * LU, 2
Y_L0, Y_L12, Y_L3 = 11, 2 * E, E3 // 2 + TILES * E3 // 4
M_PRO, M_L0, M_L12, M_L3 = 4, 4, 10, 4
GA_L0, GD_L0 = 4, 7
U0_L0 = U_X
U0_PREP = U0_L0 + CHUNKS * U_L0
U0_L12 = U0_PREP + U_PREP
U0_L3 = U0_L12 + CHUNKS * U_L12
Y0_L12 = CHUNKS * Y_L0
Y0_L3 = Y0_L12 + CHUNKS * Y_L12
M0_L0 = M_PRO
M0_L12 = M0_L0 + CHUNKS * M_L0
M0_L3 = M0_L12 + CHUNKS * M_L12


class OwnOrder:

    def __init__(self, engine, sem):
        self.engine, self.sem, self.base, self.n = engine, sem, 0, 0

    def __call__(self, instruction):
        instruction.then_inc(self.sem, 1)
        self.n += 1
        self.engine.wait_ge(self.sem, self.base + self.n)

    def enter(self, k, per):
        self.start = self.base + self.n
        self.base, self.n = self.start + k * per, 0

    def leave(self, count, per):
        assert self.n == per, (self.n, per)
        self.base, self.n = self.start + count * per, 0


def adaln_ffn_program(nc, a, out):
    with ExitStack() as ctx:
        def sb(name, shape):
            return ctx.enter_context(nc.sbuf_tensor(name, shape, F32))

        def psum(name):
            return ctx.enter_context(nc.psum_tensor(name, [P, 512], F32))

        def sem(name):
            return ctx.enter_context(nc.semaphore(name))

        ident = sb("ident", [P, P])
        sel_batch = sb("sel_batch", [B, N])
        rank_mask = sb("rank_mask", [P, B])
        earlier8 = sb("earlier8", [P, E, E])
        earlier12 = sb("earlier12", [P, E3, E3])
        ones_row = sb("ones_row", [1, N])
        rows = sb("rows", [1, 3 * E + 1])
        gru_b_row = sb("gru_b_row", [1, 3 * D])
        rnn_b_row = sb("rnn_b_row", [1, D])
        cond = sb("cond", [B, D])
        l0_rw = sb("l0_rw", [P, 2, E])
        l0f_rw_in = sb("l0f_rw_in", [E, D])
        l0_w13 = sb("l0_w13", [P, 2, 2 * P])
        l0_w2 = sb("l0_w2", [P, 2, D])
        l0_up = sb("l0_up", [P, E, P])
        l0_dn = sb("l0_dn", [P, E, D])
        l0f_up = sb("l0f_up", [P, 12 * P])
        l0f_dn = sb("l0f_dn", [P, 12, D])
        gru_w = sb("gru_w", [P, 3, D])
        gru_u = sb("gru_u", [P, 3, D])
        gru_c = sb("gru_c", [P, 3 * D])
        up = [sb(f"l{l}_up", [P, E, F]) for l in (1, 2)]
        dn = [sb(f"l{l}_dn", [P, E, Q, D]) for l in (1, 2)]
        b1_in = sb("b1_in", [2 * E * Q, P])
        b2 = [sb(f"l{l}_b2", [E, D]) for l in (1, 2)]
        gate_w = sb("gate_w", [P, 2, E])
        l2_v = sb("l2_v", [P, B * R])
        l2_w_in = sb("l2_w_in", [P, P])
        fc_bias = sb("fc_bias", [P, 1])
        rnn_w = sb("rnn_w", [P, 2, D])
        l3_p_in = sb("l3_p_in", [DA, D])
        l3_u_in = sb("l3_u_in", [NR3 * E3, DA])
        l3_b2 = sb("l3_b2", [E3, D])
        l3_up = sb("l3_up", [P, E3, F])
        l3_dn = sb("l3_dn", [P, Q, E3, D])
        stage = sb("stage", [P, E3 * F])

        condT = sb("condT", [D, B])
        cond_tok = sb("cond_tok", [D, P])
        bc = sb("bc", [P, 3 * E + 1])
        inv_temp = sb("inv_temp", [P, 1])
        b1T = sb("b1T", [P, 2 * E * Q])
        l2_uT = sb("l2_uT", [B * R, P])
        l2_wT = sb("l2_wT", [P, P])
        l0f_rw = sb("l0f_rw", [P, E])
        l3_pT = sb("l3_pT", [P, DA])
        l3_uT = sb("l3_uT", [DA, NR3 * E3])
        gru_vb = sb("gru_vb", [B, 3 * D])
        l2_fb = sb("l2_fb", [P, B])

        h3 = sb("h3", [P, B + T * B])
        xT = h3[:, B:]
        x3 = sb("x3", [P, T * B])
        x_in = x3[:, :].rearrange("p (b d) -> p b d", b=B)
        x1 = sb("x1", [P, T * B])
        h_gru = sb("h_gru", [P, (CT + 1) * B])
        l1_in = sb("l1_in", [P, N])
        x2 = sb("x2", [P, N])
        l2_in = sb("l2_in", [P, N])
        x_c, c0 = l2_in, l1_in
        z1m = sb("z1m", [P, N])
        l2_pre = sb("l2_pre", [P, N])
        silu = sb("silu", [P, 512])
        act = sb("act", [P, 2, 512])
        gated = sb("gated", [P, 4, 512])
        acc = sb("acc", [P, TILES, D])
        zr_s = sb("zr_s", [P, 2, B])
        rh = sb("rh", [P, B])
        zh = sb("zh", [P, B])
        keep = sb("keep", [P, B])
        cand = sb("cand", [P, B])
        fresh = sb("fresh", [P, B])
        l3_in = l0f_up[:, 0:N]
        x3_c = l0f_up[:, N:2 * N]
        addr = l0f_up[0:DA, 2 * N:3 * N]
        dwT = l0f_up[0:E3, 3 * N:5 * N]
        sel_expert = l0f_dn[0:E3, :, :]
        l3_cmp_a = l0_up[:, :, :].rearrange("p e h -> p (e h)")
        l3_cmp_b = l0_dn[:, :, :].rearrange("p e h -> p (e h)")
        scaled = stage[:, 0:E3 * N].rearrange("p (e n) -> p e n", e=E3)

        NG = TILES * NR3 * E3
        score = sb("score", [P, NG])
        sig_a = sb("sig_a", [P, NG])
        sig_b = sb("sig_b", [P, NG])
        cmp_a = sb("cmp_a", [P, TILES * E * E])
        cmp_b = sb("cmp_b", [P, TILES * E * E])
        rank = sb("rank", [P, NG])
        mask = sb("mask", [P, NG])
        gap = sb("gap", [P, NG])
        comb = sb("comb", [P, NG])
        top = sb("top", [P, TILES * NR3])
        den = sb("den", [P, TILES * NR3])
        okay = sb("okay", [P, TILES * NR3])
        combT = sb("combT", [E, N])

        U = [psum("U0"), psum("U1")]
        Y = [psum("Y0"), psum("Y1")]
        M = [psum("M0"), psum("M1")]
        ZR = psum("ZR")
        HH = psum("HH")

        consts = sem("consts")
        ld_x, ld_small, ld_l0, ld_gru = sem("ld_x"), sem("ld_small"), sem("ld_l0"), sem("ld_gru")
        ld_l1, ld_l2, ld_w1, ld_w2 = sem("ld_l1"), sem("ld_l2"), sem("ld_w1"), sem("ld_w2")
        u_full, u_free = sem("u_full"), sem("u_free")
        y_full, y_free = sem("y_full"), sem("y_free")
        m_full, m_free = sem("m_full"), sem("m_free")
        e_full, ga_full, gd_full = sem("e_full"), sem("ga_full"), sem("gd_full")
        hid_full, l3_hid = sem("hid_full"), sem("l3_hid")
        set_up = sem("set_up")
        xc_ready, acc_third = sem("xc_ready"), sem("acc_third")
        l0_sig, silu_done = sem("l0_sig"), sem("silu_done")
        gru_zr, gru_gates, gru_rh = sem("gru_zr"), sem("gru_gates"), sem("gru_rh")
        gru_hh, gru_cand, gru_h = sem("gru_hh"), sem("gru_cand"), sem("gru_h")
        h_moved = sem("h_moved")
        soft_gap, soft_tanh, comb_ready = sem("soft_gap"), sem("soft_tanh"), sem("comb_ready")
        l2_ready = sem("l2_ready")
        rnn_pre, rnn_h = sem("rnn_pre"), sem("rnn_h")
        l3_consts, l3_ready, out_done = sem("l3_consts"), sem("l3_ready"), sem("out_done")
        dve_own, pool_own = sem("dve_own"), sem("pool_own")

        SMALL, L0_LOADS, GRU_LOADS, L12_LOADS = 0, 8, 6, 2
        small_loads = [
            (cond[:, :], a["cond_1024"]),
            (rows[:, 0:E], a["L0_cond_router_bias"].unsqueeze(0)),
            (rows[:, E:2 * E], a["L1_ffn_gate_b"].unsqueeze(0)),
            (rows[:, 2 * E:3 * E], a["L2_ffn_gate_b"].unsqueeze(0)),
            (rows[:, 3 * E:], a["L1_ffn_temperature"].unsqueeze(0)),
            (gru_b_row[:, 0:D], a["L1_cond_b_z"].unsqueeze(0)),
            (gru_b_row[:, D:2 * D], a["L1_cond_b_r"].unsqueeze(0)),
            (gru_b_row[:, 2 * D:], a["L1_cond_b"].unsqueeze(0)),
            (rnn_b_row[:, :], a["L3_cond_b"].unsqueeze(0)),
            (fc_bias[:, :], a["L2_cond_fc_bias"].unsqueeze(1)),
            (gru_c[:, 0:D], a["L1_cond_C_z"]),
            (gru_c[:, D:2 * D], a["L1_cond_C_r"]),
            (gru_c[:, 2 * D:], a["L1_cond_C"]),
            (l0f_rw_in[:, :], a["L0_ffn_router_w"]),
            (b1_in[0:E * Q, :], a["L1_ffn_b1"].rearrange("e (q p) -> (e q) p", p=P)),
            (b1_in[E * Q:, :], a["L2_ffn_b1"].rearrange("e (q p) -> (e q) p", p=P)),
            (b2[0][:, :], a["L1_ffn_b2"]),
            (b2[1][:, :], a["L2_ffn_b2"]),
            (gate_w[:, 0, :], a["L1_ffn_gate_w"]),
            (gate_w[:, 1, :], a["L2_ffn_gate_w"]),
            (l2_v[:, :].rearrange("i (b r) -> i b r", b=B), a["fside_Bx1x1024x16_0"].rearrange("b o i r -> (o i) b r")),
            (l2_w_in[:, :], a["L2_cond_W"]),
            (l3_p_in[:, :], a["L3_ffn_P_w"]),
            (l3_u_in[0:E3, :], a["L3_ffn_U1"]),
            (l3_u_in[E3:2 * E3, :], a["L3_ffn_U2"]),
            (l3_u_in[2 * E3:, :], a["L3_ffn_U3"]),
            (l3_b2[:, :], a["L3_ffn_b2"]),
            (rnn_w[:, 0, :], a["L3_cond_Wx"]),
            (rnn_w[:, 1, :], a["L3_cond_Wh"]),
        ]
        SMALL = len(small_loads)

        block = ctx.enter_context(nc.Block())

        @block.sync
        def _(sp):
            sp.dma_start(x_in, a["x"].rearrange("b t d -> t b d")).then_inc(ld_x, 16)
            for dst, src in small_loads:
                sp.dma_start(dst, src).then_inc(ld_small, 16)
            sp.dma_start(l0_rw[:, :, :], a["L0_cond_router_W"].rearrange("(h d) e -> d h e", h=2)).then_inc(ld_l0, 16)
            sp.dma_start(l0_w13[:, 0, :], a["L0_cond_w1"]).then_inc(ld_l0, 16)
            sp.dma_start(l0_w13[:, 1, :], a["L0_cond_w3"]).then_inc(ld_l0, 16)
            sp.dma_start(l0_w2[:, :, :], a["L0_cond_w2"].rearrange("(q p) d -> p q d", p=P)).then_inc(ld_l0, 16)
            sp.dma_start(l0_up[:, :, :], a["L0_cond_W1e"].rearrange("e c h -> c e h")).then_inc(ld_l0, 16)
            sp.dma_start(l0_dn[:, :, :], a["L0_cond_W2e"].rearrange("e h c -> h e c")).then_inc(ld_l0, 16)
            sp.dma_start(l0f_up[:, :], a["L0_ffn_w1"]).then_inc(ld_l0, 16)
            sp.dma_start(l0f_dn[:, :, :], a["L0_ffn_w2"].rearrange("(q p) d -> p q d", p=P)).then_inc(ld_l0, 16)
            for g, s in enumerate(("_z", "_r", "")):
                sp.dma_start(gru_w[:, g, :], a["L1_cond_W" + s]).then_inc(ld_gru, 16)
                sp.dma_start(gru_u[:, g, :], a["L1_cond_U" + s]).then_inc(ld_gru, 16)
            sp.dma_start(stage[:, :].rearrange("p (e q d) -> p e q d", e=E3, q=Q),
                         a["L3_ffn_W1"].rearrange("e (q p) d -> p e q d", p=P)).then_inc(ld_w1, 16)
            sp.dma_start(up[0][:, :, :], a["L1_ffn_W1"].rearrange("e d f -> d e f")).then_inc(ld_l1, 16)
            sp.dma_start(dn[0][:, :, :, :], a["L1_ffn_W2"].rearrange("e (q p) d -> p e q d", p=P)).then_inc(ld_l1, 16)
            sp.dma_start(up[1][:, :, :], a["L2_ffn_w1"].rearrange("e d f -> d e f")).then_inc(ld_l2, 16)
            sp.dma_start(dn[1][:, :, :, :], a["L2_ffn_w2"].rearrange("e (q p) d -> p e q d", p=P)).then_inc(ld_l2, 16)
            sp.wait_ge(u_full, U0_PREP + E3)
            sp.dma_start(stage[:, :].rearrange("o (e h) -> o e h", e=E3),
                         a["L3_ffn_W2"].rearrange("e o h -> o e h")).then_inc(ld_w2, 16)
            with sp.Fori(0, CHUNKS) as c:
                for i in range(TILES):
                    sp.wait_ge(y_free, Y0_L3 + c * Y_L3 + E3 // 2 + (i + 1) * E3 // 4)
                    for b in range(P // CT):
                        sp.dma_start(out[i * (P // CT) + b, bass.ds(c * CT, CT), :],
                                     acc[b * CT:(b + 1) * CT, i, :]).then_inc(out_done, 16)
            sp.wait_ge(out_done, CHUNKS * B * 16)

        @block.gpsimd
        def _(pool):
            own = OwnOrder(pool, pool_own)
            own(pool.memset(ident[:, :], 0.0))
            own(pool.memset(sel_batch[:, :], 0.0))
            own(pool.memset(rank_mask[:, :], 1.0 / (D * R)))
            own(pool.memset(earlier8[:, :, :], 1.0))
            own(pool.memset(earlier12[:, :, :], 1.0))
            pool.memset(ones_row[:, :], 1.0).then_inc(consts, 1)
            pool.memset(h_gru[:, 0:B], 0.0).then_inc(consts, 1)
            pool.affine_select(out=ident[:, :], in_=ident[:, :], compare_op=ALU.not_equal, fill=1.0,
                               base=0, pattern=[[-1, P]], channel_multiplier=1).then_inc(consts, 1)
            sbv = sel_batch[:, :].rearrange("p (t b) -> p t b", b=B)
            pool.affine_select(out=sbv, in_=sbv, compare_op=ALU.not_equal, fill=1.0,
                               base=0, pattern=[[0, CT], [-1, B]], channel_multiplier=1).then_inc(consts, 1)
            rm = rank_mask[:, 0:B]
            own(pool.affine_select(out=rm, in_=rm, compare_op=ALU.is_ge, fill=0.0,
                                   base=0, pattern=[[-R, B]], channel_multiplier=1))
            pool.affine_select(out=rm, in_=rm, compare_op=ALU.is_ge, fill=0.0,
                               base=R - 1, pattern=[[R, B]], channel_multiplier=-1).then_inc(consts, 1)
            for t, n in ((earlier8, E), (earlier12, E3)):
                pool.affine_select(out=t[:, :, :], in_=t[:, :, :], compare_op=ALU.is_gt, fill=0.0,
                                   base=0, pattern=[[1, n], [-1, n]], channel_multiplier=0).then_inc(consts, 1)

            pool.wait_ge(h_moved, 1)
            own(pool.memset(sel_expert, 0.0))
            pool.affine_select(out=sel_expert, in_=sel_expert, compare_op=ALU.not_equal, fill=1.0,
                               base=0, pattern=[[-1, E3], [0, P]], channel_multiplier=1).then_inc(l3_consts, 1)

        @block.scalar
        def _(sc):
            def l0_router(k, second):
                sc.wait_ge(m_free, M0_L0 + k * M_L0 + (3 if second else 1))
                nc.scalar.activation(sig_a[:, 0:TILES * E], score[:, 0:TILES * E], ACT.Sigmoid).then_inc(l0_sig, 1)

            with sc.Fori(0, CHUNKS) as k:
                u0, ga0, gd0, y0 = U0_L0 + k * U_L0, k * GA_L0, k * GD_L0, k * Y_L0
                l0_router(k, False)
                sc.wait_ge(u_full, u0 + 1)
                nc.scalar.activation(act[:, 0, :], U[0][:, :], ACT.Sigmoid).then_inc(e_full, 1)
                for j in range(1, 5):
                    sc.wait_ge(u_full, u0 + j + 2)
                    if j == 4:
                        sc.wait_ge(y_full, y0 + 1)
                    nc.scalar.activation(gated[:, j % 4, :], U[(j + 1) % 2][:, :], ACT.Gelu).then_inc(ga_full, 1)
                l0_router(k, True)
                for n in range(1, GD_L0):
                    sc.wait_ge(u_full, u0 + n + 6)
                    if n > 1:
                        sc.wait_ge(gd_full, gd0 + n - 1)
                    nc.scalar.activation(act[:, n % 2, :], U[(n + 1) % 2][:, :], ACT.Relu).then_inc(e_full, 1)

            def gru_gates_of(chunk, t):
                sc.wait_ge(gru_zr, chunk * CT + t + 1)
                zr = ZR[:, :].rearrange("p (g n) -> p g n", g=2)[:, :, t * B:(t + 1) * B]
                nc.scalar.activation(zr_s[:, :, :], zr, ACT.Tanh, scale=0.5).then_inc(gru_gates, 1)

            def gru_cand_of(chunk, t):
                sc.wait_ge(gru_hh, chunk * CT + t + 1)
                nc.scalar.activation(cand[:, :], HH[:, t * B:(t + 1) * B], ACT.Tanh).then_inc(gru_cand, 1)

            def rnn_step(chunk, t):
                step = chunk * CT + t
                sc.wait_ge(rnn_pre, step + 1)
                nc.scalar.activation(h3[:, bass.ds((step + 1) * B, B)], ZR[:, t * B:(t + 1) * B],
                                     ACT.Tanh).then_inc(rnn_h, 1)

            def softmax_tanh(count, n):
                sc.wait_ge(soft_gap, count)
                nc.scalar.activation(sig_a[:, 0:n], gap[:, 0:n], ACT.Tanh, scale=0.5).then_inc(soft_tanh, 1)

            def l12(k, first, second):
                for l in range(2):
                    y0 = Y0_L12 + k * Y_L12 + l * E

                    def hidden(u):
                        sc.wait_ge(u_full, U0_L12 + k * U_L12 + l * LU + u + 1)
                        sc.wait_ge(y_full, y0 + max(u // 2 - 1, 0))
                        for h in range(2):
                            col = l * E * Q + 2 * u + h
                            last = nc.scalar.activation(gated[:, u % 4, h * N:(h + 1) * N], U[u % 2][:, h * N:(h + 1) * N],
                                                        ACT.Gelu, bias=b1T[:, col:col + 1])
                        last.then_inc(hid_full, 1)

                    for u in range(LU):
                        first(l * LU + u)
                        if u:
                            hidden(u - 1)
                        if u == 1:
                            softmax_tanh(2 * k + l + 1, TILES * E)
                        second(l * LU + u)
                    hidden(LU - 1)
                    if l == 0:
                        sc.wait_ge(m_free, M0_L12 + k * M_L12 + 6)
                        nc.scalar.activation(l2_in[:, :], l2_pre[:, :], ACT.Gelu).then_inc(l2_ready, 1)

            for t in range(CT):
                gru_gates_of(0, t)
                gru_cand_of(0, t)
            with sc.Fori(0, CHUNKS - 1) as k:
                l12(k, lambda s: gru_gates_of(k + 1, s), lambda s: gru_cand_of(k + 1, s))
            l12(CHUNKS - 1, lambda s: rnn_step(2 * s // CT, 2 * s % CT), lambda s: rnn_step((2 * s + 1) // CT, (2 * s + 1) % CT))

            def l3(c, step):
                softmax_tanh(2 * CHUNKS + c + 1, TILES * NR3 * E3)
                for half in range(2):
                    for s in range(8):
                        step(half * 8 + s)
                    sc.wait_ge(u_full, U0_L3 + c * U_L3 + half + 1)
                    sc.wait_ge(y_full, Y0_L3 + c * Y_L3)
                    nc.scalar.activation(gated[:, half, :], U[half][:, :], ACT.Gelu).then_inc(l3_hid, 1)
                for s in range(16, CT):
                    step(s)

            with sc.Fori(0, 2) as c:
                l3(c, lambda s: rnn_step(c + 2, s))
            with sc.Fori(2, CHUNKS) as c:
                l3(c, lambda s: None)

        @block.vector
        def _(dve):
            own = OwnOrder(dve, dve_own)
            v = nc.vector

            def tt(out, in0, in1, op):
                return v.tensor_tensor(out=out, in0=in0, in1=in1, op=op)

            def ts(out, in0, s1, op0, s2=None, op1=None):
                if op1 is None:
                    return v.tensor_scalar(out, in0, s1, None, op0)
                return v.tensor_scalar(out, in0, s1, s2, op0, op1)

            def stt(out, in0, scalar, in1, op0, op1):
                return v.scalar_tensor_tensor(out=out, in0=in0, scalar=scalar, in1=in1, op0=op0, op1=op1)

            def grp(t, g, n):
                return t[:, 0:g * n].rearrange("p (g n) -> p g n", g=g)

            def over(t, g, n):
                return t[:, 0:g].unsqueeze(2).to_broadcast([P, g, n])

            def top_mask(scores, g, n, k):
                s = grp(scores, g, n)
                ca, cb = [t[:, 0:g * n * n].rearrange("p (g a b) -> p g a b", g=g, a=n)
                          for t in ((cmp_a, cmp_b) if n == E else (l3_cmp_a, l3_cmp_b))]
                other = s.unsqueeze(2).to_broadcast([P, g, n, n])
                mine = s.unsqueeze(3).to_broadcast([P, g, n, n])
                earlier = earlier8 if n == E else earlier12
                tt(ca, other, mine, ALU.is_gt)
                own(tt(cb, other, mine, ALU.is_equal))
                own(tt(cb, cb, earlier[:, :, :].unsqueeze(1).to_broadcast([P, g, n, n]), ALU.mult))
                own(tt(ca, ca, cb, ALU.add))
                own(v.tensor_reduce(out=grp(rank, g, n), in_=ca, axis=AX.X, op=ALU.add))
                own(ts(mask[:, 0:g * n], rank[:, 0:g * n], k - 0.5, ALU.is_lt))

            def softmax_gaps(g, n):
                own(v.tensor_reduce(out=top[:, 0:g], in_=grp(score, g, n), axis=AX.X, op=ALU.max))
                tt(grp(gap, g, n), grp(score, g, n), over(top, g, n), ALU.subtract).then_inc(soft_gap, 1)

            def softmax_combine(count, g, n):
                m = g * n
                dve.wait_ge(soft_tanh, count)
                own(ts(sig_b[:, 0:m], sig_a[:, 0:m], -1.0, ALU.mult, 1.0, ALU.add))
                own(v.reciprocal(sig_b[:, 0:m], sig_b[:, 0:m]))
                own(stt(sig_a[:, 0:m], sig_a[:, 0:m], 1.0, sig_b[:, 0:m], ALU.add, ALU.mult))
                own(tt(sig_a[:, 0:m], sig_a[:, 0:m], mask[:, 0:m], ALU.mult))
                own(v.tensor_reduce(out=den[:, 0:g], in_=grp(sig_a, g, n), axis=AX.X, op=ALU.add))
                own(v.reciprocal(den[:, 0:g], den[:, 0:g]))
                tt(grp(comb, g, n), grp(sig_a, g, n), over(den, g, n), ALU.mult).then_inc(comb_ready, 1)

            def gru_reset(chunk, t):
                step = chunk * CT + t
                h = h_gru[:, t * B:(t + 1) * B]
                dve.wait_ge(gru_gates, step + 1)
                if not isinstance(step, int) or step:
                    dve.wait_ge(gru_h, step)
                stt(rh[:, :], zr_s[:, 1, :], 1.0, h, ALU.add, ALU.mult).then_inc(gru_rh, 1)
                own(stt(zh[:, :], zr_s[:, 0, :], 1.0, h, ALU.add, ALU.mult))
                own(stt(keep[:, :], zh[:, :], -0.5, h, ALU.mult, ALU.add))

            def gru_update(chunk, t):
                dve.wait_ge(gru_cand, chunk * CT + t + 1)
                own(stt(fresh[:, :], zr_s[:, 0, :], 1.0, cand[:, :], ALU.add, ALU.mult))
                stt(h_gru[:, (t + 1) * B:(t + 2) * B], fresh[:, :], 0.5, keep[:, :], ALU.mult, ALU.add).then_inc(gru_h, 1)

            for i in range(2):
                dve.wait_ge(u_full, i + 1)
                v.tensor_copy(xT.rearrange("d (t b) -> d b t", b=B)[:, 4 * i:4 * i + 4, :],
                              U[i][:, :].rearrange("d (b t) -> d b t", b=4)).then_inc(u_free, 1)
            dve.wait_ge(m_full, 1)
            own(v.tensor_copy(condT[:, :], M[0][:, 0:B]))
            own(v.tensor_copy(bc[:, :], M[0][:, B:B + 3 * E + 1]))
            v.tensor_copy(b1T[:, :], M[0][:, 64:64 + 2 * E * Q]).then_inc(m_free, 1)
            v.tensor_copy(cond_tok[:, :].rearrange("d (t b) -> d t b", b=B),
                          condT[:, :].unsqueeze(1).to_broadcast([P, P // B, B])).then_inc(set_up, 1)
            v.tensor_copy(h3[:, 0:B], condT[:, :]).then_inc(set_up, 1)
            own(v.reciprocal(inv_temp[:, :], bc[:, 3 * E:]))
            dve.wait_ge(ld_small, 16 * SMALL)
            own(ts(l2_fb[:, :], condT[:, :], fc_bias[:, 0:1], ALU.add))
            dve.wait_ge(m_full, 2)
            v.tensor_copy(l2_uT[:, :], M[1][:, 0:P])
            v.tensor_copy(l2_wT[:, :], M[1][:, P:2 * P]).then_inc(m_free, 1)
            dve.wait_ge(m_full, 3)
            v.tensor_copy(gru_vb[:, :], M[0][0:B, 0:3 * D]).then_inc(m_free, 1)
            dve.wait_ge(m_full, 4)
            v.tensor_copy(l0f_rw[:, :], M[1][:, 0:E])
            v.tensor_copy(l3_pT[:, :], M[1][:, E:E + DA])
            v.tensor_copy(l3_uT[:, :], M[1][0:DA, 128:128 + NR3 * E3]).then_inc(m_free, 1)
            dve.wait_ge(ld_gru, 16 * GRU_LOADS)
            ts(gru_u[:, 2, :], gru_u[:, 2, :], 0.5, ALU.mult).then_inc(set_up, 1)
            dve.wait_ge(consts, 7)

            def add_experts(j_full, j_free, bank, pieces, first=False):
                dve.wait_ge(y_full, j_full)
                for n, (col, i, e) in enumerate(pieces):
                    src = Y[bank][:, col:col + D]
                    last = n == len(pieces) - 1
                    if first and n < TILES:
                        ins = ts(acc[:, i, :], src, comb[:, i * E + e:i * E + e + 1], ALU.mult)
                    else:
                        ins = stt(acc[:, i, :], src, comb[:, i * E + e:i * E + e + 1], acc[:, i, :], ALU.mult, ALU.add)
                    if last:
                        ins.then_inc(y_free, 1)
                        dve.wait_ge(y_free, j_free)
                    elif n % TILES == TILES - 1:
                        own(ins)

            L0_OWN = 32
            PAIR = [((i * 2 + e2) * D, i, e2) for e2 in range(2) for i in range(TILES)]
            with dve.Fori(0, CHUNKS) as k:
                own.enter(k, L0_OWN)
                m0, y0, e0, u0 = M0_L0 + k * M_L0, k * Y_L0, k * GD_L0, U0_L0 + k * U_L0
                S = TILES * E
                dve.wait_ge(u_full, u0)
                v.tensor_copy(x_c[:, :], xT[:, bass.ds(k * N, N)]).then_inc(xc_ready, 1)

                dve.wait_ge(m_full, m0 + 1)
                v.tensor_copy(score[:, 0:S], M[0][:, 0:S]).then_inc(m_free, 1)
                dve.wait_ge(l0_sig, 2 * k + 1)
                own(tt(grp(gap, TILES, E), grp(sig_a, TILES, E),
                       bc[:, 0:E].unsqueeze(1).to_broadcast([P, TILES, E]), ALU.add))
                top_mask(gap, TILES, E, 2)
                own(tt(comb[:, 0:S], sig_a[:, 0:S], mask[:, 0:S], ALU.mult))
                own(v.tensor_reduce(out=den[:, 0:TILES], in_=grp(comb, TILES, E), axis=AX.X, op=ALU.add))
                own(ts(okay[:, 0:TILES], den[:, 0:TILES], 1e-9, ALU.is_gt))
                own(ts(den[:, 0:TILES], den[:, 0:TILES], 1e-9, ALU.add))
                own(v.reciprocal(den[:, 0:TILES], den[:, 0:TILES]))
                own(tt(den[:, 0:TILES], den[:, 0:TILES], okay[:, 0:TILES], ALU.mult))
                own(tt(grp(comb, TILES, E), grp(comb, TILES, E), over(den, TILES, E), ALU.mult))
                own(ts(okay[:, 0:TILES], okay[:, 0:TILES], -0.5, ALU.mult, 0.5, ALU.add))
                own(tt(grp(mask, TILES, E), grp(mask, TILES, E), over(okay, TILES, E), ALU.mult))
                own(tt(comb[:, 0:S], comb[:, 0:S], mask[:, 0:S], ALU.add))

                dve.wait_ge(e_full, e0 + 1)
                tt(silu[:, :], act[:, 0, :], U[0][:, :], ALU.mult).then_inc(silu_done, 1)
                dve.wait_ge(u_full, u0 + 2)
                dve.wait_ge(silu_done, k + 1)
                tt(gated[:, 0, :], silu[:, :], U[1][:, :], ALU.mult).then_inc(gd_full, 1)
                for j in range(1, 6):
                    if j == 1:
                        dve.wait_ge(y_full, y0 + 1)
                        v.tensor_copy(acc[:, :, :], Y[0][:, 0:TILES * D].rearrange("p (i d) -> p i d", i=TILES)).then_inc(y_free, 1)
                        dve.wait_ge(y_free, y0 + 1)
                    else:
                        add_experts(y0 + j, y0 + j, (j - 1) % 2,
                                    [(c, i, 2 * (j - 2) + e2) for c, i, e2 in PAIR])
                ts(acc[:, :, :], acc[:, :, :], 1.0 / 3.0, ALU.mult).then_inc(acc_third, 1)
                dve.wait_ge(m_full, m0 + 2)
                v.tensor_copy(c0[:, :], M[1][:, 0:N]).then_inc(m_free, 1)

                dve.wait_ge(m_full, m0 + 3)
                v.tensor_copy(score[:, 0:S], M[0][:, 0:S]).then_inc(m_free, 1)
                dve.wait_ge(l0_sig, 2 * k + 2)
                top_mask(sig_a, TILES, E, 2)
                own(tt(comb[:, 0:S], sig_a[:, 0:S], mask[:, 0:S], ALU.mult))
                own(v.tensor_reduce(out=den[:, 0:TILES], in_=grp(comb, TILES, E), axis=AX.X, op=ALU.add))
                own(ts(den[:, 0:TILES], den[:, 0:TILES], 1e-20, ALU.add))
                own(v.reciprocal(den[:, 0:TILES], den[:, 0:TILES]))
                own(tt(grp(comb, TILES, E), grp(comb, TILES, E), over(den, TILES, E), ALU.mult))
                for j in range(5, 12):
                    if j < 11:
                        dve.wait_ge(e_full, e0 + j - 3)
                        tt(gated[:, j % 4, :], act[:, j % 2, :], U[(j + 1) % 2][:, :], ALU.mult).then_inc(gd_full, 1)
                    if j > 5:
                        n = j - 1
                        if n < 7:
                            pieces = [(c, i, 2 * (n - 5) + e2) for c, i, e2 in PAIR]
                        else:
                            pieces = [(i * D, i, n - 3) for i in range(TILES)]
                        add_experts(y0 + n + 1, y0 + n + 1, n % 2, pieces, first=n == 5)
                dve.wait_ge(m_full, m0 + 4)
                tt(x1[:, bass.ds(k * N, N)], xT[:, bass.ds(k * N, N)], M[1][:, 0:N], ALU.add).then_inc(m_free, 1)
                own.leave(CHUNKS, L0_OWN)

            def copy_l3(w, e):
                dve.wait_ge(u_full, U0_PREP + w * E3 + e + 1)
                if w == 0:
                    v.tensor_copy(l3_up[:, e, :], U[e % 2][:, :]).then_inc(u_free, 1)
                else:
                    v.tensor_copy(l3_dn[:, :, e, :], U[e % 2][:, :].rearrange("p (q d) -> p q d", q=Q)).then_inc(u_free, 1)

            for t in range(CT):
                gru_reset(0, t)
                if t < E3:
                    copy_l3(0, t)
                if t >= CT - E3:
                    copy_l3(1, t - (CT - E3))
                gru_update(0, t)

            def l12(k, first, second):
                S = TILES * E
                dve.wait_ge(gru_h, (k + 1) * CT)
                v.tensor_copy(l1_in[:, :], h_gru[:, B:])
                v.tensor_copy(h_gru[:, 0:B], h_gru[:, CT * B:]).then_inc(h_moved, 1)
                dve.wait_ge(h_moved, k + 1)
                for l in range(2):
                    m0 = M0_L12 + k * M_L12 + 6 * l
                    y0 = Y0_L12 + k * Y_L12 + l * E

                    def add_expert(e):
                        add_experts(y0 + e + 1, y0 + e + 1, e % 2, [(i * D, i, e) for i in range(TILES)])

                    dve.wait_ge(m_full, m0 + 1)
                    tt(grp(score, TILES, E), grp(M[0], TILES, E),
                       bc[:, (1 + l) * E:(2 + l) * E].unsqueeze(1).to_broadcast([P, TILES, E]), ALU.add).then_inc(m_free, 1)
                    dve.wait_ge(m_free, m0 + 1)
                    if l == 0:
                        own(ts(score[:, 0:S], score[:, 0:S], inv_temp[:, 0:1], ALU.mult))
                    softmax_gaps(TILES, E)
                    for u in range(LU):
                        first(l * LU + u)
                        if u == 0:
                            top_mask(score, TILES, E, 2)
                        if u == 2:
                            softmax_combine(2 * k + l + 1, TILES, E)
                        if u == 4:
                            dve.wait_ge(m_full, m0 + 2)
                            v.tensor_copy(combT[:, :], M[1][0:E, 0:N]).then_inc(m_free, 1)
                        if u == 5:
                            dve.wait_ge(m_full, m0 + 3)
                            v.tensor_copy(acc[:, :, :], M[0][:, 0:TILES * D].rearrange("p (i d) -> p i d", i=TILES)).then_inc(m_free, 1)
                            dve.wait_ge(m_free, m0 + 3)
                        if u >= 6 and u % 2 == 0:
                            add_expert((u - 6) // 2)
                        second(l * LU + u)
                    for e in range((LU - 6) // 2, E):
                        add_expert(e)
                    dve.wait_ge(m_full, m0 + 4)
                    if l == 0:
                        tt(x2[:, :], x1[:, bass.ds(k * N, N)], M[1][:, 0:N], ALU.add).then_inc(m_free, 1)
                        dve.wait_ge(m_full, m0 + 5)
                        tt(z1m[:, :].rearrange("p (t b) -> p t b", b=B), M[0][:, 0:N].rearrange("p (t b) -> p t b", b=B),
                           rank_mask[:, 0:B].unsqueeze(1).to_broadcast([P, CT, B]), ALU.mult).then_inc(m_free, 1)
                        dve.wait_ge(m_full, m0 + 6)
                        tt(l2_pre[:, :].rearrange("p (t b) -> p t b", b=B), M[1][:, 0:N].rearrange("p (t b) -> p t b", b=B),
                           l2_fb[:, :].unsqueeze(1).to_broadcast([P, CT, B]), ALU.add).then_inc(m_free, 1)
                    else:
                        tt(x3[:, bass.ds(k * N, N)], x2[:, :], M[1][:, 0:N], ALU.add).then_inc(m_free, 1)

            L12_OWN = 121
            with dve.Fori(0, CHUNKS - 1) as k:
                own.enter(k, L12_OWN)
                l12(k, lambda s: gru_reset(k + 1, s), lambda s: gru_update(k + 1, s))
                own.leave(CHUNKS - 1, L12_OWN)
            l12(CHUNKS - 1, lambda s: None, lambda s: None)

            def l3(c):
                GR = TILES * NR3
                m0, y0 = M0_L3 + c * M_L3, Y0_L3 + c * Y_L3
                dve.wait_ge(rnn_h, (c + 1) * CT)
                v.tensor_copy(l3_in.rearrange("p (b t) -> p b t", b=B),
                              h3[:, bass.ds(c * N + B, N)].rearrange("p (t b) -> p b t", b=B)).then_inc(l3_ready, 1)
                v.tensor_copy(x3_c.rearrange("p (b t) -> p b t", b=B),
                              x3[:, bass.ds(c * N, N)].rearrange("p (t b) -> p b t", b=B)).then_inc(l3_ready, 1)
                dve.wait_ge(m_full, m0 + 1)
                v.tensor_copy(addr, M[0][0:DA, 0:N]).then_inc(m_free, 1)
                dve.wait_ge(m_full, m0 + 2)
                v.tensor_copy(score[:, :], M[1][:, 0:GR * E3]).then_inc(m_free, 1)
                dve.wait_ge(m_free, m0 + 2)
                softmax_gaps(GR, E3)
                top_mask(score, GR, E3, 3)
                softmax_combine(2 * CHUNKS + c + 1, GR, E3)
                dve.wait_ge(m_full, m0 + 3)
                v.tensor_copy(dwT, M[0][0:E3, :]).then_inc(m_free, 1)
                for j in range(E3 // 2):
                    dve.wait_ge(y_full, y0 + j + 1)
                    tt(scaled[:, 2 * j:2 * j + 2, :], Y[j % 2][:, :].rearrange("p (e n) -> p e n", e=2),
                       l3_in.unsqueeze(1).to_broadcast([P, 2, N]), ALU.mult).then_inc(y_free, 1)
                dve.wait_ge(m_full, m0 + 4)
                if not isinstance(c, int):
                    dve.wait_ge(out_done, c * (B * 16))
                v.tensor_copy(acc[:, :, :], M[1][:, 0:TILES * D].rearrange("p (i d) -> p i d", i=TILES)).then_inc(m_free, 1)
                dve.wait_ge(m_free, m0 + 4)
                for i in range(TILES):
                    for g in range(E3 // 4):
                        j = E3 // 2 + i * (E3 // 4) + g
                        dve.wait_ge(y_full, y0 + j + 1)
                        for e4 in range(4):
                            w = i * NR3 * E3 + E3 + 4 * g + e4
                            ins = stt(acc[:, i, :], Y[j % 2][:, e4 * D:(e4 + 1) * D], comb[:, w:w + 1], acc[:, i, :],
                                      ALU.mult, ALU.add)
                            if e4 < 3:
                                own(ins)
                            else:
                                ins.then_inc(y_free, 1)
                                dve.wait_ge(y_free, y0 + j + 1)

            L3_OWN = 30
            l3(0)
            with dve.Fori(1, CHUNKS) as c:
                own.enter(c - 1, L3_OWN)
                l3(c)
                own.leave(CHUNKS - 1, L3_OWN)

        @block.tensor
        def _(pe):
            def mm(out, lhsT, rhs, start=True, stop=True, shared=False):
                return nc.tensor.matmul(out, lhsT, rhs, start=start, stop=stop, skip_group_check=shared)

            pe.wait_ge(consts, 7)
            pe.wait_ge(ld_x, 16)
            for i in range(2):
                for b in range(4):
                    last = nc.tensor.transpose(U[i][:, b * T:(b + 1) * T], x_in[:, 4 * i + b, :], ident[:, :])
                last.then_inc(u_full, 1)
            pe.wait_ge(ld_small, 16 * SMALL)
            mm(M[0][:, 0:B], cond[:, :], ident[0:B, 0:B])
            mm(M[0][:, B:B + 3 * E + 1], ones_row[:, 0:P], rows[:, :])
            mm(M[0][:, 64:64 + 2 * E * Q], b1_in[:, :], ident[0:2 * E * Q, 0:2 * E * Q]).then_inc(m_full, 1)
            nc.tensor.transpose(M[1][:, 0:P], l2_v[:, :], ident[:, :])
            nc.tensor.transpose(M[1][:, P:2 * P], l2_w_in[:, :], ident[:, :]).then_inc(m_full, 1)
            pe.wait_ge(m_free, 1)
            mm(M[0][0:B, 0:3 * D], condT[:, :], gru_c[:, :], stop=False)
            mm(M[0][0:B, 0:3 * D], ones_row[:, 0:B], gru_b_row[:, :], start=False).then_inc(m_full, 1)
            pe.wait_ge(m_free, 2)
            mm(M[1][:, 0:E], l0f_rw_in[:, :], ident[0:E, 0:E])
            mm(M[1][:, E:E + DA], l3_p_in[:, :], ident[0:DA, 0:DA])
            mm(M[1][0:DA, 128:128 + NR3 * E3], l3_u_in[:, :], ident[0:NR3 * E3, 0:NR3 * E3]).then_inc(m_full, 1)
            pe.wait_ge(set_up, 2)
            pe.wait_ge(ld_l0, 16 * L0_LOADS)

            def wait_m(idx):
                pe.wait_ge(m_free, idx - 1)

            def tiles(t):
                return [t[:, i * P:(i + 1) * P] for i in range(TILES)]

            with pe.Fori(0, CHUNKS) as k:
                m0, y0, ga0, gd0 = M0_L0 + k * M_L0, k * Y_L0, k * GA_L0, k * GD_L0

                def project(u):
                    if u == 2:
                        pe.wait_ge(silu_done, k + 1)
                    elif u == 3 or u >= 8:
                        pe.wait_ge(gd_full, gd0 + (1 if u == 3 else u - 6))
                    elif u >= 4:
                        pe.wait_ge(ga_full, ga0 + u - 3)
                    for h in range(2):
                        if u < 2:
                            w = l0_w13[:, u, h * P:(h + 1) * P]
                        elif u < 6:
                            w = l0_up[:, 2 * (u - 2) + h, :]
                        else:
                            w = l0f_up[:, (2 * (u - 6) + h) * P:(2 * (u - 6) + h + 1) * P]
                        last = mm(U[u % 2][:, h * N:(h + 1) * N], w, (x_c if u < 6 else c0)[:, :])
                    last.then_inc(u_full, 1)

                def down(j):
                    if 1 <= j < 5:
                        pe.wait_ge(ga_full, ga0 + j)
                    else:
                        pe.wait_ge(gd_full, gd0 + max(j - 3, 1))
                    if j >= 2:
                        pe.wait_ge(y_free, y0 + j - 1)
                    y, g = Y[j % 2], gated[:, j % 4, :]
                    for i in range(TILES):
                        for h in range(2):
                            hid = g[:, h * N + i * P:h * N + (i + 1) * P]
                            if j == 0:
                                last = mm(y[:, i * D:(i + 1) * D], hid, l0_w2[:, h, :], h == 0, h == 1)
                            elif j < 5:
                                last = mm(y[:, (2 * i + h) * D:(2 * i + h + 1) * D], hid, l0_dn[:, 2 * (j - 1) + h, :])
                            elif j < 7:
                                last = mm(y[:, (2 * i + h) * D:(2 * i + h + 1) * D], hid, l0f_dn[:, 2 * (j - 5) + h, :])
                            else:
                                last = mm(y[:, i * D:(i + 1) * D], hid, l0f_dn[:, 2 * (j - 5) + h, :], h == 0, h == 1)
                    last.then_inc(y_full, 1)

                pe.wait_ge(xc_ready, k + 1)
                wait_m(m0)
                for i, x in enumerate(tiles(x_c)):
                    mm(M[0][:, i * E:(i + 1) * E], x, l0_rw[:, 0, :], True, False)
                    last = mm(M[0][:, i * E:(i + 1) * E], cond_tok[:, :], l0_rw[:, 1, :], False, True)
                last.then_inc(m_full, 1)
                project(0)
                project(1)
                for j in range(5):
                    if j < 4:
                        project(j + 2)
                    down(j)
                pe.wait_ge(acc_third, k + 1)
                wait_m(m0 + 1)
                for i in range(TILES):
                    last = nc.tensor.transpose(M[1][:, i * P:(i + 1) * P], acc[:, i, :], ident[:, :])
                last.then_inc(m_full, 1)
                pe.wait_ge(m_free, m0 + 2)
                for i, x in enumerate(tiles(c0)):
                    last = mm(M[0][:, i * E:(i + 1) * E], x, l0f_rw[:, :])
                last.then_inc(m_full, 1)
                project(6)
                for j in range(5, 11):
                    if j < 10:
                        project(j + 2)
                    down(j)
                pe.wait_ge(y_free, y0 + Y_L0)
                wait_m(m0 + 3)
                for i in range(TILES):
                    last = nc.tensor.transpose(M[1][:, i * P:(i + 1) * P], acc[:, i, :], ident[:, :])
                last.then_inc(m_full, 1)

            pe.wait_ge(ld_gru, 16 * GRU_LOADS)
            pe.wait_ge(set_up, 3)

            def gru_inputs(chunk):
                x = x1[:, bass.ds(chunk * N, N)] if not isinstance(chunk, int) else x1[:, chunk * N:(chunk + 1) * N]
                pe.wait_ge(m_free, M0_L0 + (chunk + 1) * M_L0)
                for g, bank in ((0, ZR[:, 0:N]), (1, ZR[:, N:2 * N]), (2, HH[:, 0:N])):
                    mm(bank, gru_w[:, g, :], x, g != 1, False, True)
                    mm(bank, gru_vb[:, g * D:(g + 1) * D], sel_batch[:, :], False, False, True)

            def gru_gates_of(chunk, t):
                step = chunk * CT + t
                if not isinstance(step, int) or step:
                    pe.wait_ge(gru_h, step)
                h = h_gru[:, t * B:(t + 1) * B]
                for g in range(2):
                    last = mm(ZR[:, g * N + t * B:g * N + (t + 1) * B], gru_u[:, g, :], h, False, False, True)
                last.then_inc(gru_zr, 1)

            def gru_cand_of(chunk, t):
                pe.wait_ge(gru_rh, chunk * CT + t + 1)
                mm(HH[:, t * B:(t + 1) * B], gru_u[:, 2, :], rh[:, :], False, False, True).then_inc(gru_hh, 1)

            def transpose_l3(w, e):
                idx = U_X + w * E3 + e
                pe.wait_ge(u_free, idx - 1)
                for q in range(Q):
                    last = nc.tensor.transpose(U[e % 2][:, q * P:(q + 1) * P],
                                               stage[:, e * F + q * P:e * F + (q + 1) * P], ident[:, :])
                last.then_inc(u_full, 1)

            gru_inputs(0)
            for t in range(CT):
                gru_gates_of(0, t)
                if t == 0:
                    pe.wait_ge(ld_w1, 16)
                if t < E3:
                    transpose_l3(0, t)
                if t == CT - E3:
                    pe.wait_ge(ld_w2, 16)
                if t >= CT - E3:
                    transpose_l3(1, t - (CT - E3))
                gru_cand_of(0, t)
            pe.wait_ge(ld_l1, 16 * L12_LOADS)
            pe.wait_ge(ld_l2, 16 * L12_LOADS)

            def l12(k, first, second):
                for l in range(2):
                    m0 = M0_L12 + k * M_L12 + 6 * l
                    y0 = Y0_L12 + k * Y_L12 + l * E
                    x = l2_in if l else l1_in
                    if l:
                        pe.wait_ge(l2_ready, k + 1)
                    wait_m(m0)
                    for i, xi in enumerate(tiles(x)):
                        last = mm(M[0][:, i * E:(i + 1) * E], xi, gate_w[:, l, :])
                    last.then_inc(m_full, 1)

                    def project(u):
                        if u >= 2:
                            pe.wait_ge(hid_full, (2 * k + l) * LU + u - 1)
                        for h in range(2):
                            col = (2 * u + h) % Q * P
                            last = mm(U[u % 2][:, h * N:(h + 1) * N], up[l][:, u // 2, col:col + P], x[:, :])
                        last.then_inc(u_full, 1)

                    def down(e, i):
                        if i == 0:
                            pe.wait_ge(hid_full, (2 * k + l) * LU + 2 * e + 2)
                            pe.wait_ge(y_free, y0 + e - 1)
                        for q in range(Q):
                            hid = gated[:, (2 * e + q // 2) % 4, (q % 2) * N + i * P:(q % 2) * N + (i + 1) * P]
                            last = mm(Y[e % 2][:, i * D:(i + 1) * D], hid, dn[l][:, e, q, :], q == 0, q == Q - 1)
                        if i == TILES - 1:
                            last.then_inc(y_full, 1)

                    for u in range(LU):
                        first(l * LU + u)
                        project(u)
                        second(l * LU + u)
                        if u >= 3:
                            down((u - 3) // 2, (u - 3) % 2)
                        if u == 3:
                            pe.wait_ge(comb_ready, 2 * k + l + 1)
                            wait_m(m0 + 1)
                            for i in range(TILES):
                                last = mm(M[1][0:E, i * P:(i + 1) * P], comb[:, i * E:(i + 1) * E], ident[:, :])
                            last.then_inc(m_full, 1)
                        if u == 4:
                            pe.wait_ge(m_free, m0 + 2)
                            for i in range(TILES):
                                last = mm(M[0][:, i * D:(i + 1) * D], combT[:, i * P:(i + 1) * P], b2[l][:, :])
                            last.then_inc(m_full, 1)
                    for d in range(LU - 3, LU):
                        down(d // 2, d % 2)
                    pe.wait_ge(y_free, y0 + E)
                    wait_m(m0 + 3)
                    for i in range(TILES):
                        last = nc.tensor.transpose(M[1][:, i * P:(i + 1) * P], acc[:, i, :], ident[:, :])
                    last.then_inc(m_full, 1)
                    if l == 0:
                        pe.wait_ge(m_free, m0 + 4)
                        wait_m(m0 + 4)
                        mm(M[0][:, 0:N], l2_v[:, :], x2[:, :]).then_inc(m_full, 1)
                        wait_m(m0 + 5)
                        mm(M[1][:, 0:N], l2_wT[:, :], x2[:, :], True, False)
                        pe.wait_ge(m_free, m0 + 5)
                        mm(M[1][:, 0:N], l2_uT[:, :], z1m[:, :], False, True).then_inc(m_full, 1)

            def rnn_inputs(c):
                pe.wait_ge(m_free, M0_L12 + (c + 1) * M_L12)
                if not isinstance(c, int) or c:
                    pe.wait_ge(rnn_h, c * CT)
                x = x3[:, bass.ds(c * N, N)]
                mm(ZR[:, 0:N], rnn_w[:, 0, :], x, True, False, True)
                mm(ZR[:, 0:N], rnn_b_row[:, :], ones_row[:, :], False, False, True)

            def rnn_step(c, t):
                step = c * CT + t
                if not isinstance(step, int) or step:
                    pe.wait_ge(rnn_h, step)
                mm(ZR[:, t * B:(t + 1) * B], rnn_w[:, 1, :], h3[:, bass.ds(step * B, B)], False, False, True).then_inc(rnn_pre, 1)

            with pe.Fori(0, CHUNKS - 1) as k:
                pe.wait_ge(h_moved, k + 1)
                gru_inputs(k + 1)
                l12(k, lambda s: gru_gates_of(k + 1, s), lambda s: gru_cand_of(k + 1, s))

            def rnn_early(n):
                if n % CT == 0:
                    rnn_inputs(n // CT)
                rnn_step(n // CT, n % CT)

            pe.wait_ge(h_moved, CHUNKS)
            l12(CHUNKS - 1, lambda s: rnn_early(2 * s), lambda s: rnn_early(2 * s + 1))

            pe.wait_ge(l3_consts, 1)

            def l3(c, step):
                m0, y0 = M0_L3 + c * M_L3, Y0_L3 + c * Y_L3
                pe.wait_ge(l3_ready, 2 * c + 2)
                wait_m(m0)
                mm(M[0][0:DA, 0:N], l3_pT[:, :], l3_in).then_inc(m_full, 1)
                pe.wait_ge(m_free, m0 + 1)
                for i in range(TILES):
                    last = mm(M[1][:, i * NR3 * E3:(i + 1) * NR3 * E3], addr[:, i * P:(i + 1) * P], l3_uT[:, :])
                last.then_inc(m_full, 1)
                pe.wait_ge(comb_ready, 2 * CHUNKS + c + 1)
                wait_m(m0 + 2)
                for half, r in enumerate((0, 2)):
                    for i in range(TILES):
                        w = (i * NR3 + r) * E3
                        last = mm(M[0][0:E3, half * N + i * P:half * N + (i + 1) * P], comb[:, w:w + E3], ident[:, :])
                last.then_inc(m_full, 1)
                pe.wait_ge(m_free, m0 + 3)
                for j in range(E3 // 2):
                    pe.wait_ge(y_free, y0 + max(j - 1, 0))
                    for h in range(2):
                        last = mm(Y[j % 2][:, h * N:(h + 1) * N], sel_expert[:, 2 * j + h, :], dwT[:, 0:N])
                    last.then_inc(y_full, 1)
                n = 0
                for half in range(2):
                    for h in range(2):
                        for e in range(E3):
                            if half == h == 0 and e % 2 == 0:
                                pe.wait_ge(y_free, y0 + e // 2 + 1)
                            q = 2 * half + h
                            last = mm(U[half][:, h * N:(h + 1) * N], l3_up[:, e, q * P:(q + 1) * P], scaled[:, e, :],
                                      e == 0, e == E3 - 1)
                            if h == 1 and e == E3 - 1:
                                last.then_inc(u_full, 1)
                            n += 1
                            if n % 3 == 0:
                                step(n // 3 - 1)
                wait_m(m0 + 3)
                for i in range(TILES):
                    mm(M[1][:, i * D:(i + 1) * D], dwT[:, N + i * P:N + (i + 1) * P], l3_b2[:, :], True, False)
                    last = mm(M[1][:, i * D:(i + 1) * D], x3_c[:, i * P:(i + 1) * P], ident[:, :], False, True)
                last.then_inc(m_full, 1)
                pe.wait_ge(l3_hid, 2 * c + 2)
                n = 0
                for i in range(TILES):
                    for g in range(E3 // 4):
                        j = E3 // 2 + i * (E3 // 4) + g
                        pe.wait_ge(y_free, y0 + j - 1)
                        for q in range(Q):
                            hid = gated[:, q // 2, (q % 2) * N + i * P:(q % 2) * N + (i + 1) * P]
                            last = mm(Y[j % 2][:, :], hid, l3_dn[:, q, 4 * g:4 * g + 4, :], q == 0, q == Q - 1)
                            if q == Q - 1:
                                last.then_inc(y_full, 1)
                            n += 1
                            if n % 3 != 0:
                                step(16 + n - n // 3 - 1)

            with pe.Fori(0, 2) as c:
                rnn_inputs(c + 2)
                l3(c, lambda s: rnn_step(c + 2, s))
            with pe.Fori(2, CHUNKS) as c:
                l3(c, lambda s: None)


_INS = ["x", "cond_1024", "fside_Bx1x1024x16_0", "L0_cond_router_W", "L0_cond_router_bias", "L0_cond_w1", "L0_cond_w3",
        "L0_cond_w2", "L0_cond_W1e", "L0_cond_W2e", "L0_ffn_router_w", "L0_ffn_w1", "L0_ffn_w2", "L1_cond_W_z",
        "L1_cond_U_z", "L1_cond_C_z", "L1_cond_b_z", "L1_cond_W_r", "L1_cond_U_r", "L1_cond_C_r", "L1_cond_b_r",
        "L1_cond_W", "L1_cond_U", "L1_cond_C", "L1_cond_b", "L1_ffn_W1", "L1_ffn_b1", "L1_ffn_W2", "L1_ffn_b2",
        "L1_ffn_gate_w", "L1_ffn_gate_b", "L1_ffn_temperature", "L2_cond_W", "L2_cond_fc_bias", "L2_ffn_gate_w",
        "L2_ffn_gate_b", "L2_ffn_w1", "L2_ffn_b1", "L2_ffn_w2", "L2_ffn_b2", "L3_cond_Wx", "L3_cond_Wh", "L3_cond_b",
        "L3_ffn_P_w", "L3_ffn_U1", "L3_ffn_U2", "L3_ffn_U3", "L3_ffn_W1", "L3_ffn_W2", "L3_ffn_b2"]


def kernel(**inputs):
    import numpy as np
    import concourse.bacc as bacc
    from concourse.bass_utils import run_bass_kernel_spmd

    nc = bacc.Bacc("TRN2", target_bir_lowering=False, num_devices=1, dynamic_dma_scratch_size=1024)
    arrays, aps = {}, {}
    for name in _INS:
        arr = np.atleast_1d(np.ascontiguousarray(inputs[name]))
        arrays[name + "_dram"] = arr
        aps[name] = nc.dram_tensor(name + "_dram", arr.shape, F32, kind="ExternalInput").ap()
    out = nc.dram_tensor("out_dram", (B, T, D), F32, kind="ExternalOutput").ap()
    adaln_ffn_program(nc, aps, out)
    result = run_bass_kernel_spmd(nc, [arrays], core_ids=[0])
    return result.results[0]["out_dram"]
```

```python
from contextlib import ExitStack

import concourse.bass as bass
from concourse import mybir

F32 = mybir.dt.float32
ALU = mybir.AluOpType
ACT = mybir.ActivationFunctionType
AX = mybir.AxisListType

P = 128
B, T, D = 8, 128, 128
CT = 32
CHUNKS = T // CT
N = CT * B
TILES = N // P
E = 8
E3 = 12
NR3 = 3
F = 512
Q = F // P
R = 16
DA = 64
LU = E * Q // 2
RSQRT2 = 0.5 ** 0.5

L0_FIRST = [("C", i) for i in range(6)]
L0_BOTH = [("C", 0), ("C", 1), ("F", 0), ("C", 2), ("F", 1), ("C", 3),
           ("F", 2), ("C", 4), ("F", 3), ("C", 5), ("F", 4), ("F", 5)]
L0_LAST = [("F", i) for i in range(6)]
L12_FIRST = [(0, e) for e in range(E)]
L12_BOTH = [(0, 0), (0, 1), (1, 0), (0, 2), (1, 1), (0, 3), (1, 2), (0, 4),
            (1, 3), (0, 5), (1, 4), (0, 6), (0, 7), (1, 5), (1, 6), (1, 7)]
L12_LAST = [(1, e) for e in range(E)]

X_FIRST = ["logits0", "w0", "b0"] + [f"t{e}" for e in range(E3)] + ["sum0", "z", "pre"]
X_BOTH = ["logits0", "logits1", "w0", "b0", "w1", "b1", "sum0", "z", "sum1", "pre"]
X_LAST = ["logits1", "w1", "b1", "addr", "score", "dw", "sum1"]

GRU_L0 = len(L0_BOTH) + 1
M_PRO, M_MID, M_BOTH, M_END, M_L3 = 2, 3, 3, E3 + 1, 4
U_X, Y_L3 = 2, 2 * E3 // 4


def u_l0(k):
    return U_X + 6 + (k - 1) * 12 if not isinstance(k, int) or k else U_X


def y_l0(k):
    return 5 + (k - 1) * 11 if not isinstance(k, int) or k else 0


def ga_l0(k):
    return 4 + (k - 1) * 10 if not isinstance(k, int) or k else 0


def m_l0(k):
    return M_PRO + 2 + M_MID + (k - 1) * M_BOTH if not isinstance(k, int) or k else M_PRO


def hid_l12(k):
    return LU + (k - 1) * 2 * LU if not isinstance(k, int) or k else 0


U0_L12 = u_l0(CHUNKS) + 6
Y0_L12 = y_l0(CHUNKS) + 6
M0_L12 = m_l0(CHUNKS) + M_END


def y_l12(k):
    return Y0_L12 + (E + (k - 1) * 2 * E if not isinstance(k, int) or k else 0)


def m_l12(k):
    return M0_L12 + (len(X_FIRST) + (k - 1) * len(X_BOTH) if not isinstance(k, int) or k else 0)


def soft_l12(k):
    return 2 * k if not isinstance(k, int) or k else 1


U0_L3 = U0_L12 + 2 * LU * CHUNKS
Y0_L3 = y_l12(CHUNKS) + E
M0_L3 = m_l12(CHUNKS) + len(X_LAST)


def at(start, n):
    return slice(start, start + n) if isinstance(start, int) else bass.ds(start, n)


def made_by_act(units, n):
    return sum(stream == "F" or i > 1 for stream, i in units[:n + 1])


class OwnOrder:

    def __init__(self, engine, sem):
        self.engine, self.sem, self.base, self.n = engine, sem, 0, 0

    def __call__(self, instruction):
        instruction.then_inc(self.sem, 1)
        self.n += 1
        self.engine.wait_ge(self.sem, self.base + self.n)

    def enter(self, k, per):
        self.start = self.base + self.n
        self.base, self.n = self.start + k * per, 0

    def leave(self, count, per):
        assert self.n == per, (self.n, per)
        self.base, self.n = self.start + count * per, 0


def adaln_ffn_program(nc, a, out):
    with ExitStack() as ctx:
        def sb(name, shape):
            return ctx.enter_context(nc.sbuf_tensor(name, shape, F32))

        def psum(name):
            return ctx.enter_context(nc.psum_tensor(name, [P, 512], F32))

        def sem(name):
            return ctx.enter_context(nc.semaphore(name))

        ident = sb("ident", [P, P])
        sel_batch = sb("sel_batch", [B, N])
        rank_mask = sb("rank_mask", [P, B])
        earlier8 = sb("earlier8", [P, E, E])
        earlier12 = sb("earlier12", [P, E3, E3])
        ones_row = sb("ones_row", [1, N])
        rows = sb("rows", [1, 3 * E + 1])
        gru_b_row = sb("gru_b_row", [1, 3 * D])
        rnn_b_row = sb("rnn_b_row", [1, D])
        cond = sb("cond", [B, D])
        l0_rw = sb("l0_rw", [P, 2, E])
        l0f_rw_in = sb("l0f_rw_in", [E, D])
        l0_w13 = sb("l0_w13", [P, 2, 2 * P])
        l0_w2 = sb("l0_w2", [P, 2, D])
        l0_up = sb("l0_up", [P, E, P])
        l0_dn = sb("l0_dn", [P, E, D])
        l0f_up = sb("l0f_up", [P, 12 * P])
        l0f_dn = sb("l0f_dn", [P, 12, D])
        gru_w = sb("gru_w", [P, 3, D])
        gru_u = sb("gru_u", [P, 3, D])
        gru_c = sb("gru_c", [P, 3 * D])
        up = [sb(f"l{l}_up", [P, E, F]) for l in (1, 2)]
        dn = [sb(f"l{l}_dn", [P, E, Q, D]) for l in (1, 2)]
        b1_in = sb("b1_in", [2 * E * Q, P])
        b2 = [sb(f"l{l}_b2", [E, D]) for l in (1, 2)]
        gate_w = sb("gate_w", [P, 2, E])
        l2_v = sb("l2_v", [P, B * R])
        l2_w_in = sb("l2_w_in", [P, P])
        fc_bias = sb("fc_bias", [P, 1])
        rnn_w = sb("rnn_w", [P, 2, D])
        l3_p_in = sb("l3_p_in", [DA, D])
        l3_u_in = sb("l3_u_in", [NR3 * E3, DA])
        l3_b2 = sb("l3_b2", [E3, D])
        l3_up = sb("l3_up", [P, E3, F])
        l3_dn = sb("l3_dn", [P, Q, E3, D])
        stage = sb("stage", [P, E3 * F])

        condT = sb("condT", [D, B])
        cond_tok = sb("cond_tok", [D, P])
        bc = sb("bc", [P, 3 * E + 1])
        inv_temp = sb("inv_temp", [P, 1])
        b1T = sb("b1T", [P, 2 * E * Q])
        l2_uT = sb("l2_uT", [B * R, P])
        l2_wT = sb("l2_wT", [P, P])
        l0f_rw = sb("l0f_rw", [P, E])
        l3_pT = sb("l3_pT", [P, DA])
        l3_uT = sb("l3_uT", [DA, NR3 * E3])
        gru_vb = sb("gru_vb", [B, 3 * D])
        l2_fb = sb("l2_fb", [P, B])

        h3 = sb("h3", [P, B + T * B])
        xT = h3[:, B:]
        x3 = sb("x3", [P, T * B])
        x_in = x3[:, :].rearrange("p (b d) -> p b d", b=B)
        x1 = sb("x1", [P, T * B])
        h_gru = sb("h_gru", [P, (CT + 1) * B])
        l1_in = sb("l1_in", [P, N])
        l2_in = sb("l2_in", [P, N])
        c0 = l1_in
        z1m = sb("z1m", [P, N])
        l2_pre = sb("l2_pre", [P, N])
        silu = sb("silu", [P, 512])
        act = sb("act", [P, 512])
        relu = sb("relu", [P, 2, 512])
        gated = sb("gated", [P, 4, 512])
        acc_a = sb("acc_a", [P, TILES, D])
        acc_b = sb("acc_b", [P, TILES, D])
        zr_s = sb("zr_s", [P, 2, B])
        rh = sb("rh", [P, B])
        zh = sb("zh", [P, B])
        keep = sb("keep", [P, B])
        cand = sb("cand", [P, B])
        fresh = sb("fresh", [P, B])
        l3_in = l0f_up[:, 0:N]
        x3_c = l0f_up[:, N:2 * N]
        addr = l0f_up[0:DA, 2 * N:3 * N]
        dwT = l0f_up[0:E3, 3 * N:5 * N]
        sel_expert = l0f_dn[0:E3, :, :]
        l3_cmp_a = l0_up[:, :, :].rearrange("p e h -> p (e h)")
        l3_cmp_b = l0_dn[:, :, :].rearrange("p e h -> p (e h)")
        scaled = stage[:, 0:E3 * N].rearrange("p (e n) -> p e n", e=E3)

        NG = TILES * NR3 * E3
        score = sb("score", [P, NG])
        sig_a = sb("sig_a", [P, NG])
        sig_b = sb("sig_b", [P, NG])
        cmp_a = sb("cmp_a", [P, TILES * E * E])
        cmp_b = sb("cmp_b", [P, TILES * E * E])
        rank = sb("rank", [P, NG])
        mask = sb("mask", [P, NG])
        gap = sb("gap", [P, NG])
        comb = sb("comb", [P, NG])
        comb_x = sb("comb_x", [P, T * B // P * E])
        comb_a = sb("comb_a", [P, TILES * E])
        comb_b = sb("comb_b", [P, TILES * E])
        mix2 = sb("mix2", [P, TILES, E3])
        top = sb("top", [P, E])
        den = sb("den", [P, E])
        okay = sb("okay", [P, E])
        combT_a = sb("combT_a", [E, N])
        combT_b = sb("combT_b", [E, N])

        U = [psum("U0"), psum("U1")]
        Y = [psum("Y0"), psum("Y1")]
        M = [psum("M0"), psum("M1")]
        ZR = psum("ZR")
        HH = psum("HH")

        consts = sem("consts")
        ld_first, ld_l0f = sem("ld_first"), sem("ld_l0f")
        ld_x, ld_small, ld_l0, ld_gru = sem("ld_x"), sem("ld_small"), sem("ld_l0"), sem("ld_gru")
        ld_l1, ld_l2, ld_w1, ld_w2 = sem("ld_l1"), sem("ld_l2"), sem("ld_w1"), sem("ld_w2")
        u_full, u_free = sem("u_full"), sem("u_free")
        y_full, y_free = sem("y_full"), sem("y_free")
        m_full, m_free = sem("m_full"), sem("m_free")
        e_full, ga_full, gd_full = sem("e_full"), sem("ga_full"), sem("gd_full")
        hid_full, l3_hid = sem("hid_full"), sem("l3_hid")
        set_up = sem("set_up")
        acc_third, l0_sig, silu_done = sem("acc_third"), sem("l0_sig"), sem("silu_done")
        gru_zr, gru_gates, gru_rh = sem("gru_zr"), sem("gru_gates"), sem("gru_rh")
        gru_hh, gru_cand, gru_h = sem("gru_hh"), sem("gru_cand"), sem("gru_h")
        h_moved = sem("h_moved")
        soft_gap, soft_tanh, comb_ready = sem("soft_gap"), sem("soft_tanh"), sem("comb_ready")
        l2_ready, b_full, b_free = sem("l2_ready"), sem("b_full"), sem("b_free")
        relu_done = sem("relu_done")
        rnn_pre, rnn_h = sem("rnn_pre"), sem("rnn_h")
        l3_consts, l3_ready, out_done = sem("l3_consts"), sem("l3_ready"), sem("out_done")
        dve_own, pool_own = sem("dve_own"), sem("pool_own")

        L0_LOADS, L0F_LOADS, GRU_LOADS, L12_LOADS = 5, 2, 6, 2
        first_loads = [
            (cond[:, :], a["cond_1024"]),
            (rows[:, 0:E], a["L0_cond_router_bias"].unsqueeze(0)),
            (rows[:, E:2 * E], a["L1_ffn_gate_b"].unsqueeze(0)),
            (rows[:, 2 * E:3 * E], a["L2_ffn_gate_b"].unsqueeze(0)),
            (rows[:, 3 * E:], a["L1_ffn_temperature"].unsqueeze(0)),
            (l0_rw[:, :, :], a["L0_cond_router_W"].rearrange("(h d) e -> d h e", h=2)),
            (l0f_rw_in[:, :], a["L0_ffn_router_w"]),
        ]
        small_loads = [
            (gru_b_row[:, 0:D], a["L1_cond_b_z"].unsqueeze(0)),
            (gru_b_row[:, D:2 * D], a["L1_cond_b_r"].unsqueeze(0)),
            (gru_b_row[:, 2 * D:], a["L1_cond_b"].unsqueeze(0)),
            (rnn_b_row[:, :], a["L3_cond_b"].unsqueeze(0)),
            (fc_bias[:, :], a["L2_cond_fc_bias"].unsqueeze(1)),
            (gru_c[:, 0:D], a["L1_cond_C_z"]),
            (gru_c[:, D:2 * D], a["L1_cond_C_r"]),
            (gru_c[:, 2 * D:], a["L1_cond_C"]),
            (b1_in[0:E * Q, :], a["L1_ffn_b1"].rearrange("e (q p) -> (e q) p", p=P)),
            (b1_in[E * Q:, :], a["L2_ffn_b1"].rearrange("e (q p) -> (e q) p", p=P)),
            (b2[0][:, :], a["L1_ffn_b2"]),
            (b2[1][:, :], a["L2_ffn_b2"]),
            (gate_w[:, 0, :], a["L1_ffn_gate_w"]),
            (gate_w[:, 1, :], a["L2_ffn_gate_w"]),
            (l2_v[:, :].rearrange("i (b r) -> i b r", b=B), a["fside_Bx1x1024x16_0"].rearrange("b o i r -> (o i) b r")),
            (l2_w_in[:, :], a["L2_cond_W"]),
            (l3_p_in[:, :], a["L3_ffn_P_w"]),
            (l3_u_in[0:E3, :], a["L3_ffn_U1"]),
            (l3_u_in[E3:2 * E3, :], a["L3_ffn_U2"]),
            (l3_u_in[2 * E3:, :], a["L3_ffn_U3"]),
            (l3_b2[:, :], a["L3_ffn_b2"]),
            (rnn_w[:, 0, :], a["L3_cond_Wx"]),
            (rnn_w[:, 1, :], a["L3_cond_Wh"]),
        ]
        FIRST, SMALL = len(first_loads), len(small_loads)

        def bank_of(exchanges, name):
            return M[(exchanges.index(name) + 1) % 2]

        block = ctx.enter_context(nc.Block())

        @block.sync
        def _(sp):
            sp.dma_start(x_in, a["x"].rearrange("b t d -> t b d")).then_inc(ld_x, 16)
            for dst, src in first_loads:
                sp.dma_start(dst, src).then_inc(ld_first, 16)
            sp.dma_start(l0_w13[:, 0, :], a["L0_cond_w1"]).then_inc(ld_l0, 16)
            sp.dma_start(l0_w13[:, 1, :], a["L0_cond_w3"]).then_inc(ld_l0, 16)
            sp.dma_start(l0_up[:, :, :], a["L0_cond_W1e"].rearrange("e c h -> c e h")).then_inc(ld_l0, 16)
            sp.dma_start(l0_w2[:, :, :], a["L0_cond_w2"].rearrange("(q p) d -> p q d", p=P)).then_inc(ld_l0, 16)
            sp.dma_start(l0_dn[:, :, :], a["L0_cond_W2e"].rearrange("e h c -> h e c")).then_inc(ld_l0, 16)
            sp.dma_start(l0f_up[:, :], a["L0_ffn_w1"]).then_inc(ld_l0f, 16)
            sp.dma_start(l0f_dn[:, :, :], a["L0_ffn_w2"].rearrange("(q p) d -> p q d", p=P)).then_inc(ld_l0f, 16)
            for dst, src in small_loads:
                sp.dma_start(dst, src).then_inc(ld_small, 16)
            for g, s in enumerate(("_z", "_r", "")):
                sp.dma_start(gru_w[:, g, :], a["L1_cond_W" + s]).then_inc(ld_gru, 16)
                sp.dma_start(gru_u[:, g, :], a["L1_cond_U" + s]).then_inc(ld_gru, 16)
            sp.dma_start(stage[:, :].rearrange("p (e q d) -> p e q d", e=E3, q=Q),
                         a["L3_ffn_W1"].rearrange("e (q p) d -> p e q d", p=P)).then_inc(ld_w1, 16)
            sp.dma_start(up[0][:, :, :], a["L1_ffn_W1"].rearrange("e d f -> d e f")).then_inc(ld_l1, 16)
            sp.dma_start(dn[0][:, :, :, :], a["L1_ffn_W2"].rearrange("e (q p) d -> p e q d", p=P)).then_inc(ld_l1, 16)
            sp.dma_start(up[1][:, :, :], a["L2_ffn_w1"].rearrange("e d f -> d e f")).then_inc(ld_l2, 16)
            sp.dma_start(dn[1][:, :, :, :], a["L2_ffn_w2"].rearrange("e (q p) d -> p e q d", p=P)).then_inc(ld_l2, 16)
            sp.wait_ge(m_full, m_l0(CHUNKS) + E3)
            sp.dma_start(stage[:, :].rearrange("o (e h) -> o e h", e=E3),
                         a["L3_ffn_W2"].rearrange("e o h -> o e h")).then_inc(ld_w2, 16)
            with sp.Fori(0, CHUNKS) as c:
                for i in range(TILES):
                    sp.wait_ge(y_free, Y0_L3 + c * Y_L3 + (i + 1) * E3 // 4)
                    for b in range(P // CT):
                        sp.dma_start(out[i * (P // CT) + b, bass.ds(c * CT, CT), :],
                                     acc_a[b * CT:(b + 1) * CT, i, :]).then_inc(out_done, 16)
            sp.wait_ge(out_done, CHUNKS * B * 16)

        @block.gpsimd
        def _(pool):
            own = OwnOrder(pool, pool_own)
            own(pool.memset(ident[:, :], 0.0))
            own(pool.memset(sel_batch[:, :], 0.0))
            own(pool.memset(rank_mask[:, :], 1.0 / (D * R)))
            own(pool.memset(earlier8[:, :, :], 1.0))
            own(pool.memset(earlier12[:, :, :], 1.0))
            pool.memset(ones_row[:, :], 1.0).then_inc(consts, 1)
            pool.memset(h_gru[:, 0:B], 0.0).then_inc(consts, 1)
            pool.affine_select(out=ident[:, :], in_=ident[:, :], compare_op=ALU.not_equal, fill=1.0,
                               base=0, pattern=[[-1, P]], channel_multiplier=1).then_inc(consts, 1)
            sbv = sel_batch[:, :].rearrange("p (t b) -> p t b", b=B)
            pool.affine_select(out=sbv, in_=sbv, compare_op=ALU.not_equal, fill=1.0,
                               base=0, pattern=[[0, CT], [-1, B]], channel_multiplier=1).then_inc(consts, 1)
            rm = rank_mask[:, 0:B]
            own(pool.affine_select(out=rm, in_=rm, compare_op=ALU.is_ge, fill=0.0,
                                   base=0, pattern=[[-R, B]], channel_multiplier=1))
            pool.affine_select(out=rm, in_=rm, compare_op=ALU.is_ge, fill=0.0,
                               base=R - 1, pattern=[[R, B]], channel_multiplier=-1).then_inc(consts, 1)
            for t, n in ((earlier8, E), (earlier12, E3)):
                pool.affine_select(out=t[:, :, :], in_=t[:, :, :], compare_op=ALU.is_gt, fill=0.0,
                                   base=0, pattern=[[1, n], [-1, n]], channel_multiplier=0).then_inc(consts, 1)

            pool.wait_ge(h_moved, 1)
            own(pool.memset(sel_expert, 0.0))
            pool.affine_select(out=sel_expert, in_=sel_expert, compare_op=ALU.not_equal, fill=1.0,
                               base=0, pattern=[[-1, E3], [0, P]], channel_multiplier=1).then_inc(l3_consts, 1)

        @block.scalar
        def _(sc):
            sc.wait_ge(m_free, M_PRO)
            nc.scalar.activation(sig_a[:, 0:T * B // P * E], score[:, 0:T * B // P * E], ACT.Sigmoid).then_inc(l0_sig, 1)

            def gru_gates_of(chunk, t):
                sc.wait_ge(gru_zr, chunk * CT + t + 1)
                zr = ZR[:, :].rearrange("p (g n) -> p g n", g=2)[:, :, at(t * B, B)]
                nc.scalar.activation(zr_s[:, :, :], zr, ACT.Tanh, scale=0.5).then_inc(gru_gates, 1)

            def gru_cand_of(chunk, t):
                sc.wait_ge(gru_hh, chunk * CT + t + 1)
                nc.scalar.activation(cand[:, :], HH[:, at(t * B, B)], ACT.Tanh).then_inc(gru_cand, 1)

            def rnn_step(chunk, t):
                step = chunk * CT + t
                sc.wait_ge(rnn_pre, step + 1)
                nc.scalar.activation(h3[:, at((step + 1) * B, B)], ZR[:, t * B:(t + 1) * B], ACT.Tanh).then_inc(rnn_h, 1)

            def l0(k, units, gates, cands):
                def hidden(n):
                    stream, i = units[n]
                    if stream == "C" and i != 1:
                        sc.wait_ge(u_full, u_l0(k) + n + 1)
                        if i == 0:
                            nc.scalar.activation(act[:, :], U[n % 2][:, :], ACT.Tanh, scale=0.5).then_inc(e_full, 1)
                        else:
                            nc.scalar.activation(gated[:, n % 4, :], U[n % 2][:, :], ACT.Gelu).then_inc(ga_full, 1)
                    if stream == "F":
                        sc.wait_ge(u_full, u_l0(k) + n + 1)
                        nc.scalar.activation(relu[:, i % 2, :], U[n % 2][:, :], ACT.Relu).then_inc(relu_done, 1)
                        sc.wait_ge(relu_done, (k - 1) * 6 + i + 1)
                        nc.scalar.activation(gated[:, n % 4, :], relu[:, i % 2, :], ACT.Square).then_inc(ga_full, 1)

                for n in range(len(units)):
                    gates(n)
                    if n == 0 and ("F", 0) in units:
                        sc.wait_ge(m_free, m_l0(k) if isinstance(k, int) and k == 1 else m_l0(k) - 1)
                        nc.scalar.activation(sig_a[:, 0:TILES * E], score[:, 0:TILES * E], ACT.Sigmoid).then_inc(l0_sig, 1)
                    if n:
                        hidden(n - 1)
                    cands(n)
                hidden(len(units) - 1)
                if len(units) == len(L0_BOTH):
                    gates(len(units))
                    cands(len(units))

            def idle(n):
                pass

            l0(0, L0_FIRST, idle, idle)
            l0(1, L0_BOTH, idle, idle)
            with sc.Fori(2, CHUNKS) as k:
                l0(k, L0_BOTH, lambda n: gru_gates_of(0, (k - 2) * GRU_L0 + n), lambda n: gru_cand_of(0, (k - 2) * GRU_L0 + n))
            l0(CHUNKS, L0_LAST, lambda n: gru_gates_of(0, 2 * GRU_L0 + n), lambda n: gru_cand_of(0, 2 * GRU_L0 + n))

            def softmax_tanh(count, n):
                sc.wait_ge(soft_gap, count)
                nc.scalar.activation(sig_a[:, 0:n], gap[:, 0:n], ACT.Tanh, scale=0.5).then_inc(soft_tanh, 1)

            def l12(k, blocks, steps):
                first_layer = 0 if (0, 0) in blocks else 1
                if (1, 0) in blocks:
                    sc.wait_ge(m_free, m_l12(k))
                    nc.scalar.activation(l2_in[:, :], l2_pre[:, :], ACT.Gelu).then_inc(l2_ready, 1)

                def hidden(u):
                    layer, e = blocks[u // 2]
                    sc.wait_ge(u_full, U0_L12 + hid_l12(k) + u + 1)
                    sc.wait_ge(y_full, y_l12(k) + max(u // 2 - 1, 0))
                    for h in range(2):
                        col = (layer * E + e) * Q + 2 * (u % 2) + h
                        last = nc.scalar.activation(gated[:, u % 4, h * N:(h + 1) * N], U[u % 2][:, h * N:(h + 1) * N],
                                                    ACT.Gelu, bias=b1T[:, col:col + 1])
                    last.then_inc(hid_full, 1)

                for u in range(2 * len(blocks)):
                    steps[0](u)
                    if u:
                        hidden(u - 1)
                    if u == 1:
                        softmax_tanh(soft_l12(k), TILES * E)
                    if u == 4 and len(blocks) > E:
                        softmax_tanh(soft_l12(k) + 1, TILES * E)
                    if u == 12 and first_layer == 1:
                        softmax_tanh(2 * CHUNKS + 1, TILES * NR3 * E3)
                    for step in steps[1:]:
                        step(u)
                hidden(2 * len(blocks) - 1)

            l12(0, L12_FIRST, [lambda u: gru_gates_of(1, 2 * u), lambda u: gru_cand_of(1, 2 * u),
                               lambda u: gru_gates_of(1, 2 * u + 1), lambda u: gru_cand_of(1, 2 * u + 1)])
            with sc.Fori(1, CHUNKS - 1) as k:
                l12(k, L12_BOTH, [lambda u: gru_gates_of(k + 1, u), lambda u: gru_cand_of(k + 1, u)])
            l12(CHUNKS - 1, L12_BOTH, [lambda u: rnn_step(2 * u // CT, 2 * u % CT),
                                       lambda u: rnn_step((2 * u + 1) // CT, (2 * u + 1) % CT)])
            l12(CHUNKS, L12_LAST, [lambda u: rnn_step(2, 2 * u), lambda u: rnn_step(2, 2 * u + 1)])

            def l3(c, step, route_next):
                for half in range(2):
                    for s in range(8):
                        step(half * 8 + s)
                    if half == 0 and route_next:
                        softmax_tanh(2 * CHUNKS + c + 2, TILES * NR3 * E3)
                    sc.wait_ge(u_full, U0_L3 + c * 2 + half + 1)
                    sc.wait_ge(y_full, Y0_L3 + c * Y_L3)
                    nc.scalar.activation(gated[:, half, :], U[half][:, :], ACT.Gelu).then_inc(l3_hid, 1)
                for s in range(16, CT):
                    step(s)

            l3(0, lambda s: rnn_step(CHUNKS - 1, s), True)
            with sc.Fori(1, CHUNKS - 1) as c:
                l3(c, idle, True)
            l3(CHUNKS - 1, idle, False)

        @block.vector
        def _(dve):
            own = OwnOrder(dve, dve_own)
            v = nc.vector

            def tt(out, in0, in1, op):
                return v.tensor_tensor(out=out, in0=in0, in1=in1, op=op)

            def ts(out, in0, s1, op0, s2=None, op1=None):
                if op1 is None:
                    return v.tensor_scalar(out, in0, s1, None, op0)
                return v.tensor_scalar(out, in0, s1, s2, op0, op1)

            def stt(out, in0, scalar, in1, op0, op1):
                return v.scalar_tensor_tensor(out=out, in0=in0, scalar=scalar, in1=in1, op0=op0, op1=op1)

            def grp(t, g, n):
                return t[:, 0:g * n].rearrange("p (g n) -> p g n", g=g)

            def over(t, g, n):
                return t[:, 0:g].unsqueeze(2).to_broadcast([P, g, n])

            def by_tile(bank):
                return bank[:, 0:TILES * D].rearrange("p (i d) -> p i d", i=TILES)

            def top_mask(scores, g, n, k, room):
                s = grp(scores, g, n)
                ca, cb = [t[:, 0:g * n * n].rearrange("p (g a b) -> p g a b", g=g, a=n) for t in room]
                other = s.unsqueeze(2).to_broadcast([P, g, n, n])
                mine = s.unsqueeze(3).to_broadcast([P, g, n, n])
                earlier = earlier8 if n == E else earlier12
                tt(ca, other, mine, ALU.is_gt)
                own(tt(cb, other, mine, ALU.is_equal))
                own(tt(cb, cb, earlier[:, :, :].unsqueeze(1).to_broadcast([P, g, n, n]), ALU.mult))
                own(tt(ca, ca, cb, ALU.add))
                own(v.tensor_reduce(out=grp(rank, g, n), in_=ca, axis=AX.X, op=ALU.add))
                own(ts(mask[:, 0:g * n], rank[:, 0:g * n], k - 0.5, ALU.is_lt))

            def softmax_gaps(g, n):
                own(v.tensor_reduce(out=top[:, 0:g], in_=grp(score, g, n), axis=AX.X, op=ALU.max))
                tt(grp(gap, g, n), grp(score, g, n), over(top, g, n), ALU.subtract).then_inc(soft_gap, 1)

            def softmax_combine(count, g, n, comb_to):
                m = g * n
                dve.wait_ge(soft_tanh, count)
                own(ts(sig_b[:, 0:m], sig_a[:, 0:m], -1.0, ALU.mult, 1.0, ALU.add))
                own(v.reciprocal(sig_b[:, 0:m], sig_b[:, 0:m]))
                own(stt(sig_a[:, 0:m], sig_a[:, 0:m], 1.0, sig_b[:, 0:m], ALU.add, ALU.mult))
                own(tt(sig_a[:, 0:m], sig_a[:, 0:m], mask[:, 0:m], ALU.mult))
                own(v.tensor_reduce(out=den[:, 0:g], in_=grp(sig_a, g, n), axis=AX.X, op=ALU.add))
                own(v.reciprocal(den[:, 0:g], den[:, 0:g]))
                tt(grp(comb_to, g, n), grp(sig_a, g, n), over(den, g, n), ALU.mult).then_inc(comb_ready, 1)

            def gru_reset(chunk, t):
                step = chunk * CT + t
                h = h_gru[:, at(t * B, B)]
                dve.wait_ge(gru_gates, step + 1)
                if not isinstance(step, int) or step:
                    dve.wait_ge(gru_h, step)
                stt(rh[:, :], zr_s[:, 1, :], 1.0, h, ALU.add, ALU.mult).then_inc(gru_rh, 1)
                own(stt(zh[:, :], zr_s[:, 0, :], 1.0, h, ALU.add, ALU.mult))
                own(stt(keep[:, :], zh[:, :], -0.5, h, ALU.mult, ALU.add))

            def gru_update(chunk, t):
                dve.wait_ge(gru_cand, chunk * CT + t + 1)
                own(stt(fresh[:, :], zr_s[:, 0, :], 1.0, cand[:, :], ALU.add, ALU.mult))
                stt(h_gru[:, at((t + 1) * B, B)], fresh[:, :], 0.5, keep[:, :], ALU.mult, ALU.add).then_inc(gru_h, 1)

            for i in range(2):
                dve.wait_ge(u_full, i + 1)
                v.tensor_copy(xT.rearrange("d (t b) -> d b t", b=B)[:, 4 * i:4 * i + 4, :],
                              U[i][:, :].rearrange("d (b t) -> d b t", b=4)).then_inc(u_free, 1)
            dve.wait_ge(m_full, 1)
            own(v.tensor_copy(condT[:, :], M[0][:, 0:B]))
            v.tensor_copy(cond_tok[:, :].rearrange("d (t b) -> d t b", b=B),
                          condT[:, :].unsqueeze(1).to_broadcast([P, P // B, B])).then_inc(set_up, 1)
            own(v.tensor_copy(bc[:, :], M[0][:, B:B + 3 * E + 1]))
            v.tensor_copy(l0f_rw[:, :], M[0][:, 64:64 + E]).then_inc(m_free, 1)
            own(v.reciprocal(inv_temp[:, :], bc[:, 3 * E:]))
            v.tensor_copy(h3[:, 0:B], condT[:, :]).then_inc(set_up, 1)
            dve.wait_ge(consts, 7)

            GX = T * B // P
            SX = GX * E
            dve.wait_ge(m_full, M_PRO)
            v.tensor_copy(score[:, 0:SX], M[1][:, 0:SX]).then_inc(m_free, 1)
            dve.wait_ge(l0_sig, 1)
            own(tt(grp(gap, GX, E), grp(sig_a, GX, E), bc[:, 0:E].unsqueeze(1).to_broadcast([P, GX, E]), ALU.add))
            top_mask(gap, GX, E, 2, (gated[:, 2, :], gated[:, 3, :]))
            own(tt(comb_x[:, :], sig_a[:, 0:SX], mask[:, 0:SX], ALU.mult))
            own(v.tensor_reduce(out=den[:, 0:GX], in_=grp(comb_x, GX, E), axis=AX.X, op=ALU.add))
            own(ts(okay[:, 0:GX], den[:, 0:GX], 1e-9, ALU.is_gt))
            own(ts(den[:, 0:GX], den[:, 0:GX], 1e-9, ALU.add))
            own(v.reciprocal(den[:, 0:GX], den[:, 0:GX]))
            own(tt(den[:, 0:GX], den[:, 0:GX], okay[:, 0:GX], ALU.mult))
            own(tt(grp(comb_x, GX, E), grp(comb_x, GX, E), over(den, GX, E), ALU.mult))
            own(ts(okay[:, 0:GX], okay[:, 0:GX], -0.5, ALU.mult, 0.5, ALU.add))
            own(tt(grp(mask, GX, E), grp(mask, GX, E), over(okay, GX, E), ALU.mult))
            own(tt(comb_x[:, :], comb_x[:, :], mask[:, 0:SX], ALU.add))

            def add_experts(count, bank, pieces, acc, comb, first=False):
                dve.wait_ge(y_full, count)
                for n, (col, i, e) in enumerate(pieces):
                    src = Y[bank][:, col:col + D]
                    weight = comb[:, i * E + e:i * E + e + 1]
                    if first and n < TILES:
                        ins = ts(acc[:, i, :], src, weight, ALU.mult)
                    else:
                        ins = stt(acc[:, i, :], src, weight, acc[:, i, :], ALU.mult, ALU.add)
                    if n == len(pieces) - 1:
                        ins.then_inc(y_free, 1)
                        dve.wait_ge(y_free, count)
                    elif n % TILES == TILES - 1:
                        own(ins)

            S = TILES * E

            def f_router_mask(k):
                dve.wait_ge(l0_sig, k + 1)
                top_mask(sig_a, TILES, E, 2, (cmp_a, cmp_b))

            def f_router_weights():
                own(tt(comb_b[:, :], sig_a[:, 0:S], mask[:, 0:S], ALU.mult))
                own(v.tensor_reduce(out=den[:, 0:TILES], in_=grp(comb_b, TILES, E), axis=AX.X, op=ALU.add))
                own(ts(den[:, 0:TILES], den[:, 0:TILES], 1e-20, ALU.add))
                own(v.reciprocal(den[:, 0:TILES], den[:, 0:TILES]))
                own(tt(grp(comb_b, TILES, E), grp(comb_b, TILES, E), over(den, TILES, E), ALU.mult))

            PAIR = [((i * 2 + e2) * D, e2, i) for e2 in range(2) for i in range(TILES)]

            def l0(k, units, reset, update, copies):
                u0, y0, m0 = u_l0(k), y_l0(k), m_l0(k)
                size = len(units)
                with_c, with_f = ("C", 0) in units, ("F", 0) in units
                down_of = {n: j for j, n in enumerate(n for n in range(size) if units[n] != ("C", 0))}

                def finish(n):
                    stream, i = units[n]
                    if stream == "C" and i == 0:
                        dve.wait_ge(e_full, k + 1)
                        stt(silu[:, :], act[:, :], 1.0, U[n % 2][:, :], ALU.add, ALU.mult).then_inc(silu_done, 1)
                    elif stream == "C" and i == 1:
                        dve.wait_ge(u_full, u0 + n + 1)
                        dve.wait_ge(silu_done, k + 1)
                        stt(gated[:, n % 4, :], silu[:, :], 0.5, U[n % 2][:, :], ALU.mult, ALU.mult).then_inc(gd_full, 1)

                def add(n):
                    stream, i = units[n]
                    j = down_of[n]
                    count = y0 + j + 1
                    if (stream, i) == ("C", 1):
                        dve.wait_ge(y_full, count)
                        v.tensor_copy(comb_a[:, :], comb_x[:, at(k * S, S)])
                        v.tensor_copy(acc_a[:, :, :], by_tile(Y[j % 2])).then_inc(y_free, 1)
                        dve.wait_ge(y_free, count)
                    elif stream == "C":
                        add_experts(count, j % 2, [(c, t, 2 * (i - 2) + e2) for c, e2, t in PAIR], acc_a, comb_a)
                        if i == 5:
                            ts(acc_a[:, :, :], acc_a[:, :, :], 1.0 / 3.0, ALU.mult).then_inc(acc_third, 1)
                    elif i < 2:
                        add_experts(count, j % 2, [(c, t, 2 * i + e2) for c, e2, t in PAIR], acc_b, comb_b, first=i == 0)
                    else:
                        add_experts(count, j % 2, [(t * D, t, 2 + i) for t in range(TILES)], acc_b, comb_b)

                for n in range(size):
                    reset(n)
                    if n:
                        finish(n - 1)
                    if with_f and n == (2 if with_c else 0):
                        f_router_mask(k)
                    if with_f and n == (3 if with_c else 1):
                        f_router_weights()
                    if n >= 3 and n - 3 in down_of:
                        add(n - 3)
                    update(n)
                    copies(n)
                finish(size - 1)
                add(size - 3)
                if with_c and with_f:
                    reset(size)
                add(size - 2)
                if not with_f:
                    add(size - 1)
                if with_c:
                    dve.wait_ge(m_full, m0 + 1)
                    v.tensor_copy(c0[:, :], M[1][:, 0:N]).then_inc(m_free, 1)
                if with_f:
                    add(size - 1)
                if with_c and with_f:
                    update(size)
                if with_c:
                    dve.wait_ge(m_full, m0 + 2)
                    v.tensor_copy(score[:, 0:S], M[0][:, 0:S]).then_inc(m_free, 1)
                if with_f:
                    dve.wait_ge(m_full, m0 + (M_BOTH if with_c else M_END))
                    tt(x1[:, at((k - 1) * N, N)], xT[:, at((k - 1) * N, N)], M[1 if with_c else 0][:, 0:N], ALU.add).then_inc(m_free, 1)

            def idle(n):
                pass

            def copy_up(e):
                idx = m_l0(CHUNKS) + e
                dve.wait_ge(m_full, idx + 1)
                v.tensor_copy(l3_up[:, e, :], M[e % 2][:, :]).then_inc(m_free, 1)

            def copy_down(e):
                dve.wait_ge(m_full, M0_L12 + X_FIRST.index(f"t{e}") + 1)
                v.tensor_copy(l3_dn[:, :, e, :], bank_of(X_FIRST, f"t{e}")[:, :].rearrange("p (q d) -> p q d", q=Q)).then_inc(m_free, 1)

            l0(0, L0_FIRST, idle, idle, idle)

            m_mid = M_PRO + 2
            dve.wait_ge(ld_small, 16 * SMALL)
            own(ts(l2_fb[:, :], condT[:, :], fc_bias[:, 0:1], ALU.add))
            dve.wait_ge(m_full, m_mid + 1)
            v.tensor_copy(l2_uT[:, :], M[1][:, 0:P])
            v.tensor_copy(l2_wT[:, :], M[1][:, P:2 * P]).then_inc(m_free, 1)
            dve.wait_ge(m_full, m_mid + 2)
            v.tensor_copy(gru_vb[:, :], M[0][0:B, 0:3 * D]).then_inc(m_free, 1)
            dve.wait_ge(m_full, m_mid + 3)
            v.tensor_copy(b1T[:, :], M[1][:, 0:2 * E * Q])
            v.tensor_copy(l3_pT[:, :], M[1][:, 128:128 + DA])
            v.tensor_copy(l3_uT[:, :], M[1][0:DA, 256:256 + NR3 * E3]).then_inc(m_free, 1)
            dve.wait_ge(ld_gru, 16 * GRU_LOADS)
            ts(gru_u[:, 2, :], gru_u[:, 2, :], 0.5, ALU.mult).then_inc(set_up, 1)
            l0(1, L0_BOTH, idle, idle, idle)
            L0_OWN = 55
            with dve.Fori(2, CHUNKS) as k:
                own.enter(k - 2, L0_OWN)
                l0(k, L0_BOTH, lambda n: gru_reset(0, (k - 2) * GRU_L0 + n), lambda n: gru_update(0, (k - 2) * GRU_L0 + n), idle)
                own.leave(CHUNKS - 2, L0_OWN)

            def copy_two(n):
                copy_up(2 * n)
                copy_up(2 * n + 1)

            l0(CHUNKS, L0_LAST, lambda n: gru_reset(0, 2 * GRU_L0 + n), lambda n: gru_update(0, 2 * GRU_L0 + n), copy_two)

            def l12(k, blocks, exchanges, steps, more):
                m0, y0 = m_l12(k), y_l12(k)
                count = len(blocks)
                accs, combs, combTs = (acc_a, acc_b), (comb_a, comb_b), (combT_a, combT_b)
                layers = sorted({layer for layer, e in blocks})

                def taken(name):
                    dve.wait_ge(m_full, m0 + exchanges.index(name) + 1)
                    return bank_of(exchanges, name)

                def scores(layer):
                    tt(grp(score, TILES, E), grp(taken(f"logits{layer}"), TILES, E),
                       bc[:, (1 + layer) * E:(2 + layer) * E].unsqueeze(1).to_broadcast([P, TILES, E]), ALU.add).then_inc(m_free, 1)
                    dve.wait_ge(m_free, m0 + exchanges.index(f"logits{layer}") + 1)
                    if layer == 0:
                        own(ts(score[:, 0:S], score[:, 0:S], inv_temp[:, 0:1], ALU.mult))
                    softmax_gaps(TILES, E)

                def add(b):
                    layer, e = blocks[b]
                    add_experts(y0 + b + 1, b % 2, [(i * D, i, e) for i in range(TILES)], accs[layer], combs[layer])

                def routing(u):
                    for n, layer in enumerate(layers):
                        at_unit = u - 3 * n
                        if at_unit == 0:
                            if n:
                                scores(layer)
                            top_mask(score, TILES, E, 2, (cmp_a, cmp_b))
                        if at_unit == 2:
                            softmax_combine(soft_l12(k) + n, TILES, E, combs[layer])
                        if at_unit == (4 if n == 0 else 5):
                            v.tensor_copy(combTs[layer][:, :], taken(f"w{layer}")[0:E, 0:N]).then_inc(m_free, 1)
                        if at_unit == (5 if n == 0 else 6):
                            v.tensor_copy(accs[layer][:, :, :], by_tile(taken(f"b{layer}"))).then_inc(m_free, 1)
                            dve.wait_ge(m_free, m0 + exchanges.index(f"b{layer}") + 1)

                if 0 in layers:
                    dve.wait_ge(gru_h, (k + 1) * CT)
                    v.tensor_copy(l1_in[:, :], h_gru[:, B:])
                    v.tensor_copy(h_gru[:, 0:B], h_gru[:, CT * B:]).then_inc(h_moved, 1)
                    dve.wait_ge(h_moved, k + 1)
                scores(layers[0])
                for u in range(2 * count):
                    steps[0](u)
                    routing(u)
                    if u >= 6 and u % 2 == 0:
                        add((u - 6) // 2)
                    steps[1](u)
                    more(u)
                b = count - 3

                def sum0():
                    tt(x1[:, at(k * N, N)], x1[:, at(k * N, N)], taken("sum0")[:, 0:N], ALU.add).then_inc(m_free, 1)

                def low_rank():
                    tt(z1m[:, :].rearrange("p (t b) -> p t b", b=B), taken("z")[:, 0:N].rearrange("p (t b) -> p t b", b=B),
                       rank_mask[:, 0:B].unsqueeze(1).to_broadcast([P, CT, B]), ALU.mult).then_inc(m_free, 1)

                if layers == [0, 1]:
                    sum0()
                add(b)
                add(b + 1)
                if layers == [0, 1]:
                    low_rank()
                add(b + 2)
                if layers == [0]:
                    sum0()
                    low_rank()
                if 1 in layers:
                    tt(x3[:, at((k - 1) * N, N)], x1[:, at((k - 1) * N, N)], taken("sum1")[:, 0:N], ALU.add).then_inc(m_free, 1)
                if 0 in layers:
                    tt(l2_pre[:, :].rearrange("p (t b) -> p t b", b=B), taken("pre")[:, 0:N].rearrange("p (t b) -> p t b", b=B),
                       l2_fb[:, :].unsqueeze(1).to_broadcast([P, CT, B]), ALU.add).then_inc(m_free, 1)

            def second_steps(u):
                gru_update(1, 2 * u)
                gru_reset(1, 2 * u + 1)
                if u >= 5:
                    copy_down(u - 5)
                gru_update(1, 2 * u + 1)
                if u == LU - 1:
                    copy_down(E3 - 1)

            l12(0, L12_FIRST, X_FIRST, [lambda u: gru_reset(1, 2 * u), second_steps], idle)
            L12_OWN = 121
            with dve.Fori(1, CHUNKS - 1) as k:
                own.enter(k - 1, L12_OWN)
                l12(k, L12_BOTH, X_BOTH, [lambda u: gru_reset(k + 1, u), lambda u: gru_update(k + 1, u)], idle)
                own.leave(CHUNKS - 2, L12_OWN)
            l12(CHUNKS - 1, L12_BOTH, X_BOTH, [idle, idle], idle)

            GR = TILES * NR3

            def l3_gather(c):
                dve.wait_ge(rnn_h, (c + 1) * CT)
                v.tensor_copy(l3_in.rearrange("p (b t) -> p b t", b=B),
                              h3[:, at(c * N + B, N)].rearrange("p (t b) -> p b t", b=B)).then_inc(l3_ready, 1)

            def l3_residual(c):
                v.tensor_copy(x3_c.rearrange("p (b t) -> p b t", b=B),
                              x3[:, at(c * N, N)].rearrange("p (t b) -> p b t", b=B)).then_inc(l3_ready, 1)

            def l3_address(idx, bank):
                dve.wait_ge(m_full, idx + 1)
                v.tensor_copy(addr, bank[0:DA, 0:N]).then_inc(m_free, 1)

            def l3_scores(idx, bank):
                dve.wait_ge(m_full, idx + 1)
                v.tensor_copy(score[:, :], bank[:, 0:GR * E3]).then_inc(m_free, 1)
                dve.wait_ge(m_free, idx + 1)
                softmax_gaps(GR, E3)
                top_mask(score, GR, E3, 3, (l3_cmp_a, l3_cmp_b))

            def l3_weights(idx, bank):
                dve.wait_ge(m_full, idx + 1)
                v.tensor_copy(dwT, bank[0:E3, :]).then_inc(m_free, 1)

            def l3_scale(c, j):
                dve.wait_ge(b_full, c * (E3 // 2) + j + 1)
                bank = (HH, U[1])[j % 2]
                tt(scaled[:, 2 * j:2 * j + 2, :], bank[:, :].rearrange("p (e n) -> p e n", e=2),
                   l3_in.unsqueeze(1).to_broadcast([P, 2, N]), ALU.mult).then_inc(b_free, 1)

            m_last = m_l12(CHUNKS)

            def first_route(u):
                if u == 7:
                    l3_gather(0)
                    l3_residual(0)
                if u == 9:
                    l3_address(m_last + X_LAST.index("addr"), bank_of(X_LAST, "addr"))
                if u == 10:
                    l3_scores(m_last + X_LAST.index("score"), bank_of(X_LAST, "score"))
                if u == 12:
                    softmax_combine(2 * CHUNKS + 1, GR, E3, comb)
                if u == 14:
                    l3_weights(m_last + X_LAST.index("dw"), bank_of(X_LAST, "dw"))

            l12(CHUNKS, L12_LAST, X_LAST, [idle, idle], first_route)
            for j in range(E3 // 2):
                l3_scale(0, j)

            def l3(c, route_next):
                m0, y0 = M0_L3 + c * M_L3, Y0_L3 + c * Y_L3
                own(v.tensor_copy(mix2[:, :, :], comb[:, :].rearrange("p (i r e) -> p i r e", i=TILES, r=NR3)[:, :, 1, :]))
                if route_next:
                    l3_gather(c + 1)
                    l3_address(m0, M[0])
                    l3_scores(m0 + 1, M[1])
                    softmax_combine(2 * CHUNKS + 2 + c, GR, E3, comb)
                sums = m0 + 2 if route_next else m0
                dve.wait_ge(m_full, sums + 1)
                if not isinstance(c, int) or c:
                    dve.wait_ge(out_done, c * (B * 16))
                v.tensor_copy(acc_a[:, :, :], by_tile(M[0])).then_inc(m_free, 1)
                dve.wait_ge(m_free, sums + 1)
                if route_next:
                    l3_residual(c + 1)
                    l3_weights(m0 + 3, M[1])
                for i in range(TILES):
                    for g in range(E3 // 4):
                        j = i * (E3 // 4) + g
                        dve.wait_ge(y_full, y0 + j + 1)
                        for e4 in range(4):
                            e = 4 * g + e4
                            ins = stt(acc_a[:, i, :], Y[j % 2][:, e4 * D:(e4 + 1) * D], mix2[:, i, e:e + 1], acc_a[:, i, :],
                                      ALU.mult, ALU.add)
                            if e4 < 3:
                                own(ins)
                            else:
                                ins.then_inc(y_free, 1)
                                dve.wait_ge(y_free, y0 + j + 1)
                        if route_next:
                            l3_scale(c + 1, j)

            l3(0, True)
            L3_OWN = 31
            with dve.Fori(1, CHUNKS - 1) as c:
                own.enter(c - 1, L3_OWN)
                l3(c, True)
                own.leave(CHUNKS - 2, L3_OWN)
            l3(CHUNKS - 1, False)

        @block.tensor
        def _(pe):
            def mm(out, lhsT, rhs, start=True, stop=True, shared=False):
                return nc.tensor.matmul(out, lhsT, rhs, start=start, stop=stop, skip_group_check=shared)

            def tiles(t):
                return [t[:, i * P:(i + 1) * P] for i in range(TILES)]

            def wait_m(idx):
                pe.wait_ge(m_free, idx - 1)

            def transpose_tiles(bank, acc):
                for i in range(TILES):
                    last = nc.tensor.transpose(bank[:, i * P:(i + 1) * P], acc[:, i, :], ident[:, :])
                last.then_inc(m_full, 1)

            pe.wait_ge(consts, 7)
            pe.wait_ge(ld_x, 16)
            for i in range(2):
                for b in range(4):
                    last = nc.tensor.transpose(U[i][:, b * T:(b + 1) * T], x_in[:, 4 * i + b, :], ident[:, :])
                last.then_inc(u_full, 1)
            pe.wait_ge(ld_first, 16 * FIRST)
            mm(M[0][:, 0:B], cond[:, :], ident[0:B, 0:B])
            mm(M[0][:, B:B + 3 * E + 1], ones_row[:, 0:P], rows[:, :])
            mm(M[0][:, 64:64 + E], l0f_rw_in[:, :], ident[0:E, 0:E]).then_inc(m_full, 1)
            pe.wait_ge(u_free, U_X)
            pe.wait_ge(set_up, 1)
            for i in range(T * B // P):
                mm(M[1][:, i * E:(i + 1) * E], xT[:, i * P:(i + 1) * P], l0_rw[:, 0, :], True, False)
                last = mm(M[1][:, i * E:(i + 1) * E], cond_tok[:, :], l0_rw[:, 1, :], False, True)
            last.then_inc(m_full, 1)

            def later_set_up():
                m_mid = M_PRO + 2
                pe.wait_ge(ld_small, 16 * SMALL)
                wait_m(m_mid)
                nc.tensor.transpose(M[1][:, 0:P], l2_v[:, :], ident[:, :])
                nc.tensor.transpose(M[1][:, P:2 * P], l2_w_in[:, :], ident[:, :]).then_inc(m_full, 1)
                wait_m(m_mid + 1)
                pe.wait_ge(set_up, 2)
                mm(M[0][0:B, 0:3 * D], condT[:, :], gru_c[:, :], stop=False)
                mm(M[0][0:B, 0:3 * D], ones_row[:, 0:B], gru_b_row[:, :], start=False).then_inc(m_full, 1)
                wait_m(m_mid + 2)
                mm(M[1][:, 0:2 * E * Q], b1_in[:, :], ident[0:2 * E * Q, 0:2 * E * Q])
                mm(M[1][:, 128:128 + DA], l3_p_in[:, :], ident[0:DA, 0:DA])
                mm(M[1][0:DA, 256:256 + NR3 * E3], l3_u_in[:, :], ident[0:NR3 * E3, 0:NR3 * E3]).then_inc(m_full, 1)

            def gru_inputs(chunk):
                for g, bank in ((0, ZR[:, 0:N]), (1, ZR[:, N:2 * N]), (2, HH[:, 0:N])):
                    mm(bank, gru_w[:, g, :], x1[:, at(chunk * N, N)], g != 1, False, True)
                    mm(bank, gru_vb[:, g * D:(g + 1) * D], sel_batch[:, :], False, False, True)

            def gru_gates_of(chunk, t):
                step = chunk * CT + t
                if not isinstance(step, int) or step:
                    pe.wait_ge(gru_h, step)
                for g in range(2):
                    last = mm(ZR[:, at(g * N + t * B, B)], gru_u[:, g, :], h_gru[:, at(t * B, B)], False, False, True)
                last.then_inc(gru_zr, 1)

            def gru_cand_of(chunk, t):
                pe.wait_ge(gru_rh, chunk * CT + t + 1)
                mm(HH[:, at(t * B, B)], gru_u[:, 2, :], rh[:, :], False, False, True).then_inc(gru_hh, 1)

            def rnn_inputs(c):
                if c:
                    pe.wait_ge(rnn_h, c * CT)
                mm(ZR[:, 0:N], rnn_w[:, 0, :], x3[:, c * N:(c + 1) * N], True, False, True)
                mm(ZR[:, 0:N], rnn_b_row[:, :], ones_row[:, :], False, False, True)

            def rnn_step(c, t):
                step = c * CT + t
                if step:
                    pe.wait_ge(rnn_h, step)
                mm(ZR[:, t * B:(t + 1) * B], rnn_w[:, 1, :], h3[:, step * B:(step + 1) * B], False, False, True).then_inc(rnn_pre, 1)

            def l0(k, units, gates, cands, more):
                y0, m0, ga0 = y_l0(k), m_l0(k), ga_l0(k)
                size = len(units)
                with_c, with_f = ("C", 0) in units, ("F", 0) in units
                down_of = {n: j for j, n in enumerate(n for n in range(size) if units[n] != ("C", 0))}

                def wait_hidden(n):
                    stream, i = units[n]
                    if (stream, i) == ("C", 0):
                        pe.wait_ge(silu_done, k + 1)
                    elif (stream, i) == ("C", 1):
                        pe.wait_ge(gd_full, k + 1)
                    else:
                        pe.wait_ge(ga_full, ga0 + made_by_act(units, n))

                def project(n):
                    stream, i = units[n]
                    if n >= 2:
                        wait_hidden(n - 2)
                    for h in range(2):
                        if stream == "F":
                            w = l0f_up[:, (2 * i + h) * P:(2 * i + h + 1) * P]
                        elif i < 2:
                            w = l0_w13[:, i, h * P:(h + 1) * P]
                        else:
                            w = l0_up[:, 2 * (i - 2) + h, :]
                        x = c0[:, :] if stream == "F" else xT[:, at(k * N, N)]
                        last = mm(U[n % 2][:, h * N:(h + 1) * N], w, x)
                    last.then_inc(u_full, 1)

                def down(n):
                    stream, i = units[n]
                    j = down_of[n]
                    wait_hidden(n)
                    if j >= 2:
                        pe.wait_ge(y_free, y0 + j - 1)
                    y = Y[j % 2]
                    for t in range(TILES):
                        for h in range(2):
                            hid = gated[:, n % 4, h * N + t * P:h * N + (t + 1) * P]
                            if stream == "C" and i == 1:
                                last = mm(y[:, t * D:(t + 1) * D], hid, l0_w2[:, h, :], h == 0, h == 1)
                            elif stream == "C":
                                last = mm(y[:, (2 * t + h) * D:(2 * t + h + 1) * D], hid, l0_dn[:, 2 * (i - 2) + h, :])
                            elif i < 2:
                                last = mm(y[:, (2 * t + h) * D:(2 * t + h + 1) * D], hid, l0f_dn[:, 2 * i + h, :])
                            else:
                                last = mm(y[:, t * D:(t + 1) * D], hid, l0f_dn[:, 2 * i + h, :], h == 0, h == 1)
                    last.then_inc(y_full, 1)

                def conditioned():
                    pe.wait_ge(acc_third, k + 1)
                    pe.wait_ge(m_free, m0)
                    transpose_tiles(M[1], acc_a)

                for n in range(size):
                    gates(n)
                    project(n)
                    cands(n)
                    if n - 2 in down_of:
                        down(n - 2)
                    more(n)
                down(size - 2)
                if with_f and with_c:
                    gates(size)
                    conditioned()
                down(size - 1)
                if with_f and with_c:
                    cands(size)
                if with_c:
                    if not with_f:
                        conditioned()
                    pe.wait_ge(m_free, m0 + 1)
                    for i, x in enumerate(tiles(c0)):
                        last = mm(M[0][:, i * E:(i + 1) * E], x, l0f_rw[:, :])
                    last.then_inc(m_full, 1)
                if with_f:
                    pe.wait_ge(y_free, y0 + len(down_of))
                    wait_m(m0 + (M_BOTH if with_c else M_END) - 1)
                    transpose_tiles(M[1 if with_c else 0], acc_b)

            def idle(n):
                pass

            def transpose_up(n):
                if n == 0:
                    pe.wait_ge(ld_w1, 16)
                for e in (2 * n, 2 * n + 1):
                    wait_m(m_l0(CHUNKS) + e)
                    for q in range(Q):
                        last = nc.tensor.transpose(M[e % 2][:, q * P:(q + 1) * P],
                                                   stage[:, e * F + q * P:e * F + (q + 1) * P], ident[:, :])
                    last.then_inc(m_full, 1)

            def transpose_down(e):
                if e == 0:
                    pe.wait_ge(ld_w2, 16)
                wait_m(M0_L12 + X_FIRST.index(f"t{e}"))
                for q in range(Q):
                    last = nc.tensor.transpose(bank_of(X_FIRST, f"t{e}")[:, q * P:(q + 1) * P],
                                               stage[:, e * F + q * P:e * F + (q + 1) * P], ident[:, :])
                last.then_inc(m_full, 1)

            pe.wait_ge(ld_l0, 16 * L0_LOADS)
            l0(0, L0_FIRST, idle, idle, idle)
            later_set_up()
            pe.wait_ge(ld_l0f, 16 * L0F_LOADS)
            l0(1, L0_BOTH, idle, idle, idle)
            pe.wait_ge(ld_gru, 16 * GRU_LOADS)
            pe.wait_ge(set_up, 3)
            pe.wait_ge(m_free, m_l0(2))
            gru_inputs(0)
            with pe.Fori(2, CHUNKS) as k:
                l0(k, L0_BOTH, lambda n: gru_gates_of(0, (k - 2) * GRU_L0 + n), lambda n: gru_cand_of(0, (k - 2) * GRU_L0 + n), idle)
            l0(CHUNKS, L0_LAST, lambda n: gru_gates_of(0, 2 * GRU_L0 + n), lambda n: gru_cand_of(0, 2 * GRU_L0 + n), transpose_up)

            def l12(k, blocks, exchanges, before, between, after):
                m0, y0, h0 = m_l12(k), y_l12(k), hid_l12(k)
                count = len(blocks)
                units = 2 * count
                layers = sorted({layer for layer, e in blocks})
                combs, combTs, ins = (comb_a, comb_b), (combT_a, combT_b), (l1_in, l2_in)

                def bank(name):
                    wait_m(m0 + exchanges.index(name))
                    return bank_of(exchanges, name)

                def logits(layer):
                    if layer:
                        pe.wait_ge(l2_ready, k)
                    m = bank(f"logits{layer}")
                    for i, x in enumerate(tiles(ins[layer])):
                        last = mm(m[:, i * E:(i + 1) * E], x, gate_w[:, layer, :])
                    last.then_inc(m_full, 1)

                def weights(layer):
                    pe.wait_ge(comb_ready, soft_l12(k) + layers.index(layer))
                    m = bank(f"w{layer}")
                    for i in range(TILES):
                        last = mm(m[0:E, i * P:(i + 1) * P], combs[layer][:, i * E:(i + 1) * E], ident[:, :])
                    last.then_inc(m_full, 1)

                def biases(layer):
                    pe.wait_ge(m_free, m0 + exchanges.index(f"w{layer}") + 1)
                    m = bank(f"b{layer}")
                    for i in range(TILES):
                        last = mm(m[:, i * D:(i + 1) * D], combTs[layer][:, i * P:(i + 1) * P], b2[layer][:, :])
                    last.then_inc(m_full, 1)

                def project(u):
                    layer, e = blocks[u // 2]
                    if u >= 2:
                        pe.wait_ge(hid_full, h0 + u - 1)
                    for h in range(2):
                        col = (2 * (u % 2) + h) * P
                        last = mm(U[u % 2][:, h * N:(h + 1) * N], up[layer][:, e, col:col + P], ins[layer][:, :])
                    last.then_inc(u_full, 1)

                def down(d):
                    b, i = d // 2, d % 2
                    layer, e = blocks[b]
                    if i == 0:
                        pe.wait_ge(hid_full, h0 + 2 * b + 2)
                        pe.wait_ge(y_free, y0 + b - 1)
                    for q in range(Q):
                        hid = gated[:, (2 * b + q // 2) % 4, (q % 2) * N + i * P:(q % 2) * N + (i + 1) * P]
                        last = mm(Y[b % 2][:, i * D:(i + 1) * D], hid, dn[layer][:, e, q, :], q == 0, q == Q - 1)
                    if i == TILES - 1:
                        last.then_inc(y_full, 1)

                def layer_sum(layer):
                    done = max(b for b in range(count) if blocks[b][0] == layer) + 1
                    pe.wait_ge(y_free, y0 + done)
                    transpose_tiles(bank(f"sum{layer}"), (acc_a, acc_b)[layer])

                def low_rank():
                    pe.wait_ge(m_free, m0 + exchanges.index("sum0") + 1)
                    mm(bank("z")[:, 0:N], l2_v[:, :], x1[:, at(k * N, N)]).then_inc(m_full, 1)

                def layer2_input():
                    m = bank("pre")
                    mm(m[:, 0:N], l2_wT[:, :], x1[:, at(k * N, N)], True, False)
                    pe.wait_ge(m_free, m0 + exchanges.index("z") + 1)
                    mm(m[:, 0:N], l2_uT[:, :], z1m[:, :], False, True).then_inc(m_full, 1)

                logits(layers[0])
                for u in range(units):
                    before(u)
                    if u == 2 and len(layers) > 1:
                        logits(1)
                    project(u)
                    between(u)
                    if u >= 3:
                        down(u - 3)
                    if u == 3:
                        weights(layers[0])
                    if u == 4:
                        biases(layers[0])
                    if u == 7 and len(layers) > 1:
                        weights(1)
                    if u == 8 and len(layers) > 1:
                        biases(1)
                    after(u)
                if layers == [0, 1]:
                    layer_sum(0)
                down(units - 3)
                down(units - 2)
                if layers == [0, 1]:
                    low_rank()
                down(units - 1)
                if layers == [0]:
                    layer_sum(0)
                    low_rank()
                if 1 in layers:
                    layer_sum(1)
                if 0 in layers:
                    layer2_input()

            def second_steps(u):
                gru_gates_of(1, 2 * u + 1)
                if u >= 5:
                    transpose_down(u - 5)
                gru_cand_of(1, 2 * u + 1)
                if u == LU - 1:
                    transpose_down(E3 - 1)

            pe.wait_ge(ld_l1, 16 * L12_LOADS)
            pe.wait_ge(ld_l2, 16 * L12_LOADS)
            pe.wait_ge(m_free, M0_L12)
            pe.wait_ge(h_moved, 1)
            gru_inputs(1)
            l12(0, L12_FIRST, X_FIRST, lambda u: gru_gates_of(1, 2 * u), lambda u: gru_cand_of(1, 2 * u), second_steps)
            with pe.Fori(1, CHUNKS - 1) as k:
                pe.wait_ge(h_moved, k + 1)
                gru_inputs(k + 1)
                l12(k, L12_BOTH, X_BOTH, lambda u: gru_gates_of(k + 1, u), lambda u: gru_cand_of(k + 1, u), idle)

            def rnn_early(s):
                if s % CT == 0:
                    rnn_inputs(s // CT)
                rnn_step(s // CT, s % CT)

            pe.wait_ge(h_moved, CHUNKS)
            l12(CHUNKS - 1, L12_BOTH, X_BOTH, lambda u: rnn_early(2 * u), lambda u: rnn_early(2 * u + 1), idle)

            def l3_address(c, idx, bank):
                pe.wait_ge(l3_ready, 2 * c + 1)
                wait_m(idx)
                mm(bank[0:DA, 0:N], l3_pT[:, :], l3_in).then_inc(m_full, 1)

            def l3_scores(idx, bank):
                pe.wait_ge(m_free, idx)
                for i in range(TILES):
                    last = mm(bank[:, i * NR3 * E3:(i + 1) * NR3 * E3], addr[:, i * P:(i + 1) * P], l3_uT[:, :])
                last.then_inc(m_full, 1)

            def l3_weights(c, idx, bank):
                pe.wait_ge(comb_ready, 2 * CHUNKS + 1 + c)
                wait_m(idx)
                for half, r in enumerate((0, 2)):
                    for i in range(TILES):
                        w = (i * NR3 + r) * E3
                        last = mm(bank[0:E3, half * N + i * P:half * N + (i + 1) * P], comb[:, w:w + E3], ident[:, :])
                last.then_inc(m_full, 1)

            def l3_broadcast(c, j):
                if not isinstance(c, int) or c or j >= 2:
                    pe.wait_ge(b_free, c * (E3 // 2) + j - 1)
                for h in range(2):
                    last = mm((HH, U[1])[j % 2][:, h * N:(h + 1) * N], sel_expert[:, 2 * j + h, :], dwT[:, 0:N])
                last.then_inc(b_full, 1)

            m_last = m_l12(CHUNKS)

            def first_route(u):
                if u == 8:
                    l3_address(0, m_last + X_LAST.index("addr"), bank_of(X_LAST, "addr"))
                if u == 10:
                    l3_scores(m_last + X_LAST.index("score"), bank_of(X_LAST, "score"))
                if u == 13:
                    l3_weights(0, m_last + X_LAST.index("dw"), bank_of(X_LAST, "dw"))

            pe.wait_ge(m_free, m_last)
            rnn_inputs(2)
            l12(CHUNKS, L12_LAST, X_LAST, lambda u: rnn_step(2, 2 * u), lambda u: rnn_step(2, 2 * u + 1), first_route)
            pe.wait_ge(l3_consts, 1)
            for j in range(E3 // 2):
                l3_broadcast(0, j)
            pe.wait_ge(m_free, M0_L3)
            rnn_inputs(CHUNKS - 1)

            def l3(c, step, route_next):
                m0, y0 = M0_L3 + c * M_L3, Y0_L3 + c * Y_L3
                n = 0
                for half in range(2):
                    for h in range(2):
                        for e in range(E3):
                            if half == h == 0 and e % 2 == 0:
                                pe.wait_ge(b_free, c * (E3 // 2) + e // 2 + 1)
                            q = 2 * half + h
                            last = mm(U[half][:, h * N:(h + 1) * N], l3_up[:, e, q * P:(q + 1) * P], scaled[:, e, :],
                                      e == 0, e == E3 - 1)
                            if h == 1 and e == E3 - 1:
                                last.then_inc(u_full, 1)
                            n += 1
                            if n % 3 == 0:
                                step(n // 3 - 1)
                            if n == 8 and route_next:
                                l3_address(c + 1, m0, M[0])
                            if n == 14 and route_next:
                                l3_scores(m0 + 1, M[1])
                pe.wait_ge(l3_ready, 2 * c + 2)
                wait_m(m0 + 2 if route_next else m0)
                for i in range(TILES):
                    mm(M[0][:, i * D:(i + 1) * D], dwT[:, N + i * P:N + (i + 1) * P], l3_b2[:, :], True, False)
                    last = mm(M[0][:, i * D:(i + 1) * D], x3_c[:, i * P:(i + 1) * P], ident[:, :], False, True)
                last.then_inc(m_full, 1)
                if route_next:
                    l3_weights(c + 1, m0 + 3, M[1])
                pe.wait_ge(l3_hid, 2 * c + 2)
                n = 0
                for i in range(TILES):
                    for g in range(E3 // 4):
                        j = i * (E3 // 4) + g
                        pe.wait_ge(y_free, y0 + j - 1)
                        for q in range(Q):
                            hid = gated[:, q // 2, (q % 2) * N + i * P:(q % 2) * N + (i + 1) * P]
                            last = mm(Y[j % 2][:, :], hid, l3_dn[:, q, 4 * g:4 * g + 4, :], q == 0, q == Q - 1)
                            if q == Q - 1:
                                last.then_inc(y_full, 1)
                            n += 1
                            if n % 3 != 0:
                                step(16 + n - n // 3 - 1)
                        if route_next:
                            if j == 0:
                                pe.wait_ge(m_free, m0 + 4)
                            l3_broadcast(c + 1, j)

            l3(0, lambda s: rnn_step(CHUNKS - 1, s), True)
            with pe.Fori(1, CHUNKS - 1) as c:
                l3(c, idle, True)
            l3(CHUNKS - 1, idle, False)


_INS = ["x", "cond_1024", "fside_Bx1x1024x16_0", "L0_cond_router_W", "L0_cond_router_bias", "L0_cond_w1", "L0_cond_w3",
        "L0_cond_w2", "L0_cond_W1e", "L0_cond_W2e", "L0_ffn_router_w", "L0_ffn_w1", "L0_ffn_w2", "L1_cond_W_z",
        "L1_cond_U_z", "L1_cond_C_z", "L1_cond_b_z", "L1_cond_W_r", "L1_cond_U_r", "L1_cond_C_r", "L1_cond_b_r",
        "L1_cond_W", "L1_cond_U", "L1_cond_C", "L1_cond_b", "L1_ffn_W1", "L1_ffn_b1", "L1_ffn_W2", "L1_ffn_b2",
        "L1_ffn_gate_w", "L1_ffn_gate_b", "L1_ffn_temperature", "L2_cond_W", "L2_cond_fc_bias", "L2_ffn_gate_w",
        "L2_ffn_gate_b", "L2_ffn_w1", "L2_ffn_b1", "L2_ffn_w2", "L2_ffn_b2", "L3_cond_Wx", "L3_cond_Wh", "L3_cond_b",
        "L3_ffn_P_w", "L3_ffn_U1", "L3_ffn_U2", "L3_ffn_U3", "L3_ffn_W1", "L3_ffn_W2", "L3_ffn_b2"]


def kernel(**inputs):
    import numpy as np
    import concourse.bacc as bacc
    from concourse.bass_utils import run_bass_kernel_spmd

    nc = bacc.Bacc("TRN2", target_bir_lowering=False, num_devices=1, dynamic_dma_scratch_size=1024)
    arrays, aps = {}, {}
    for name in _INS:
        arr = np.atleast_1d(np.ascontiguousarray(inputs[name]))
        arrays[name + "_dram"] = arr
        aps[name] = nc.dram_tensor(name + "_dram", arr.shape, F32, kind="ExternalInput").ap()
    out = nc.dram_tensor("out_dram", (B, T, D), F32, kind="ExternalOutput").ap()
    adaln_ffn_program(nc, aps, out)
    result = run_bass_kernel_spmd(nc, [arrays], core_ids=[0])
    return result.results[0]["out_dram"]
```

```python
from contextlib import ExitStack

import concourse.bass as bass
from concourse import mybir

F32 = mybir.dt.float32
F32R = mybir.dt.float32r
ALU = mybir.AluOpType
ACT = mybir.ActivationFunctionType
AX = mybir.AxisListType

P = 128
B, T, D = 8, 128, 128
CT = 32
CHUNKS = T // CT
N = CT * B
TILES = N // P
E = 8
E3 = 12
NR3 = 3
F = 512
Q = F // P
R = 16
DA = 64
LU = E * Q // 2
RSQRT2 = 0.5 ** 0.5

L0_EARLY = "C0 C1 C2 C3 F0 F1 F2 F3 F4 F5 C4 C5".split()
L0_LATE = "C0 C1 C2 C3 F0 F1 C4 C5 F2 F3 F4 F5".split()
L0_UNITS = [("C", i, 0) for i in range(6)]
for k in range(1, CHUNKS):
    for u in L0_LATE if k == CHUNKS - 1 else L0_EARLY:
        L0_UNITS += [(u[0], int(u[1]), k if u[0] == "C" else k - 1)]
L0_UNITS += [("F", i, CHUNKS - 1) for i in range(6)]
L0_SLOTS = len(L0_UNITS) + 4
L0_DOWNS = [n for n, u in enumerate(L0_UNITS) if u[:2] != ("C", 0)]
MID_SLOT = 12
W1_EARLY, W1_SLOT = 9, 8
W1_SLOTS = [W1_SLOT + e if e < W1_EARLY else len(L0_UNITS) + e - W1_EARLY for e in range(E3)]
X_L0 = []
for n in range(L0_SLOTS):
    X_L0 += [("c", c) for s, i, c in L0_UNITS[max(n - 4, 0):max(n - 3, 0)] if (s, i) == ("C", 5)]
    X_L0 += [("f", c) for s, i, c in L0_UNITS[max(n - 4, 0):max(n - 3, 0)] if (s, i) == ("F", 5)]
    X_L0 += [("logits", c) for s, i, c in L0_UNITS[max(n - 5, 0):max(n - 4, 0)] if (s, i) == ("C", 5)]
    X_L0 += [("mid", m) for m in range(3) if n == MID_SLOT]
    X_L0 += [("up", e) for e in range(E3) if W1_SLOTS[e] == n]
X_BODY = ["w0", "b0", "sum0", "z", "pre", "logits1", "w1", "b1", "logits0", "sum1"]
X_END = (["w0"] + [f"t{e}" for e in range(E, E3)] + ["b0", "sum0", "z", "pre", "logits1", "addr", "w1", "score", "b1"]
         + [f"t{e}" for e in range(E)] + ["dw", "sum1"])

GRU_SLOT = L0_UNITS.index(("F", 5, 0)) + 5
LATE = 3
M_PRO, M_L3 = 2, 4
U_X, Y_L3 = 2, 2 * E3 // 4


def m_l0(*name):
    return M_PRO + X_L0.index(name)


U0_L12 = U_X + len(L0_UNITS)
Y0_L12 = len(L0_DOWNS)
M_START = M_PRO + len(X_L0)
M0_L12 = M_START + 1
U0_L3 = U0_L12 + 2 * LU * CHUNKS
Y0_L3 = Y0_L12 + CHUNKS * 2 * E
M0_L3 = M0_L12 + (CHUNKS - 1) * len(X_BODY) + len(X_END)


def steps_l0(n):
    first, last = n - GRU_SLOT, L0_SLOTS - 1 - GRU_SLOT
    return [] if first < 0 else [first] if first < last else list(range(first, CT))


def w2_beside(l, u):
    return [E + u - 8] if l == 0 and 8 <= u < 8 + E3 - E else [u - 6] if l == 1 and 6 <= u < 6 + E else []


def at(start, n):
    return slice(start, start + n) if isinstance(start, int) else bass.ds(start, n)


def made_by_act(n):
    return sum(stream == "F" or i > 1 for stream, i, c in L0_UNITS[:n + 1])


class OwnOrder:

    def __init__(self, engine, sem):
        self.engine, self.sem, self.base, self.n = engine, sem, 0, 0

    def __call__(self, instruction):
        instruction.then_inc(self.sem, 1)
        self.n += 1
        self.engine.wait_ge(self.sem, self.base + self.n)

    def enter(self, k, per):
        self.start = self.base + self.n
        self.base, self.n = self.start + k * per, 0

    def leave(self, count, per):
        assert self.n == per, (self.n, per)
        self.base, self.n = self.start + count * per, 0


def adaln_ffn_program(nc, a, out):
    with ExitStack() as ctx:
        def sb(name, shape, dtype=F32, scope=ctx):
            return scope.enter_context(nc.sbuf_tensor(name, shape, dtype))

        def parts(name, shape):
            return sb(name + "_hi", shape, F32R), sb(name + "_lo", shape, F32R)

        def psum(name):
            return ctx.enter_context(nc.psum_tensor(name, [P, 512], F32))

        def sem(name):
            return ctx.enter_context(nc.semaphore(name))

        ident = sb("ident", [P, P])
        sel_batch = sb("sel_batch", [B, N])
        rank_mask = sb("rank_mask", [P, B])
        earlier8 = sb("earlier8", [P, E, E])
        earlier12 = sb("earlier12", [P, E3, E3])
        ones_row = sb("ones_row", [1, N])
        rows = sb("rows", [1, 3 * E + 1])
        rnn_b_row = sb("rnn_b_row", [1, D])
        cond = sb("cond", [B, D])
        l0_rw = sb("l0_rw", [P, 2, E])
        b2 = [sb(f"l{l}_b2", [E, D]) for l in (1, 2)]
        gate_w = sb("gate_w", [P, 2, E])
        l2_v = sb("l2_v", [P, B * R])
        fc_bias = sb("fc_bias", [1, P])
        rnn_w = sb("rnn_w", [P, 2, D])
        l3_u_in = sb("l3_u_in", [NR3 * E3, DA])
        l3_b2 = sb("l3_b2", [E3, D])

        condT = sb("condT", [D, B])
        cond_tok = sb("cond_tok", [D, P])
        bc = sb("bc", [P, 3 * E + 1])
        inv_temp = sb("inv_temp", [P, 1])
        b1T = sb("b1T", [P, 2 * E * Q])
        l2_uT = sb("l2_uT", [B * R, P])
        l2_wT = sb("l2_wT", [P, P])
        l0f_rw = sb("l0f_rw", [P, E])
        l3_pT = sb("l3_pT", [P, DA])
        l3_uT = sb("l3_uT", [DA, NR3 * E3])

        h3 = sb("h3", [P, B + T * B])
        xT = h3[:, B:]
        x3 = sb("x3", [P, T * B])
        x_in = x3[:, :].rearrange("p (b d) -> p b d", b=B)
        x1 = sb("x1", [P, T * B])
        h_gru = sb("h_gru", [P, (CT + 1) * B])
        l1_in = sb("l1_in", [P, N])
        l2_in = sb("l2_in", [P, N])
        c0 = (l1_in, l2_in)
        z1m = sb("z1m", [P, N])
        gated = sb("gated", [P, 4, 512])
        acc_a = sb("acc_a", [P, TILES, D])
        acc_b = sb("acc_b", [P, TILES, D])
        zr_s = sb("zr_s", [P, 2, B])
        rh = sb("rh", [P, B])
        zh = sb("zh", [P, B])
        keep = sb("keep", [P, B])
        cand = sb("cand", [P, B])
        fresh = sb("fresh", [P, B])
        NG = TILES * NR3 * E3
        up, dn = [None, sb("l2_up", [P, E, F])], [None, sb("l2_dn", [P, E, Q, D])]
        l3_cmp_a = sb("l3_cmp_a", [P, NG * E3])
        l3_up = parts("l3_up", [P, E3, F])
        with ExitStack() as early:
            l0f_up = sb("l0f_up", [P, 12 * P], scope=early)
            l0f_dn = sb("l0f_dn", [P, 12, D], scope=early)
            l0_up = sb("l0_up", [P, E, P], scope=early)
            l0_dn = sb("l0_dn", [P, E, D], scope=early)
            l0_w13 = sb("l0_w13", [P, 2, 2 * P], scope=early)
            l0_w2 = sb("l0_w2", [P, 2, D], scope=early)
            gru_w = sb("gru_w", [P, 3, D], scope=early)
            gru_u = sb("gru_u", [P, 3, D], scope=early)
            gru_c = sb("gru_c", [P, 3 * D], scope=early)
            gru_vb = sb("gru_vb", [B, 3 * D], scope=early)
            gru_b_row = sb("gru_b_row", [1, 3 * D], scope=early)
            l0f_rw_in = sb("l0f_rw_in", [E, D], scope=early)
            b1_in = sb("b1_in", [2 * E * Q, P], scope=early)
            l2_w_in = sb("l2_w_in", [P, P], scope=early)
            l3_p_in = sb("l3_p_in", [DA, D], scope=early)
            silu = sb("silu", [P, 512], scope=early)
            act = sb("act", [P, 512], scope=early)
            relu = sb("relu", [P, 2, 512], scope=early)
            up[0] = sb("l1_up", [P, E, F], scope=early)
            dn[0] = sb("l1_dn", [P, E, Q, D], scope=early)
            stage = sb("stage", [P, E3 * F], scope=early)
        sel_expert = sb("sel_expert", [E3, E3, P], F32R)
        l3_in, x3_c, addr = sb("l3_in", [P, N])[:, :], sb("x3_c", [P, N])[:, :], sb("addr", [DA, N])[:, :]
        dwT, dwT_third = parts("dwT", [E3, N]), sb("dwT_third", [E3, N])
        l3_dn = [None, None, parts("l3_dn2", [P, Q, 4, D])]
        l3_cmp_b = sb("l3_cmp_b", [P, NG * E3])
        sb("room", [P, 2 * E * P + 4 * P + 2 * D + 15 * D + 4 * D - 2 * Q * 4 * D - NG * E3])
        hid3 = parts("hid3", [P, 2, 512])
        l3_dn[0], l3_dn[1] = parts("l3_dn0", [P, Q, 4, D]), parts("l3_dn1", [P, Q, 4, D])
        scaled = parts("scaled", [P, E3, N])
        weighted = gated[:, 2:4, :]

        score = sb("score", [P, NG])
        sig_a = sb("sig_a", [P, NG])
        sig_b = sb("sig_b", [P, NG])
        cmp_a = sb("cmp_a", [P, TILES * E * E])
        cmp_b = sb("cmp_b", [P, TILES * E * E])
        rank = sb("rank", [P, NG])
        mask = sb("mask", [P, NG])
        gap = sb("gap", [P, NG])
        table = sb("table", [P, 1])
        comb = sb("comb", [P, NG])
        comb_x = sb("comb_x", [P, T * B // P * E])
        comb_a = sb("comb_a", [P, TILES * E])
        comb_b = sb("comb_b", [P, TILES * E])
        mix2 = sb("mix2", [P, TILES, E3])
        top = sb("top", [P, E])
        den = sb("den", [P, E])
        okay = sb("okay", [P, E])
        combT_a = sb("combT_a", [E, N])
        combT_b = sb("combT_b", [E, N])

        U = [psum("U0"), psum("U1")]
        Y = [psum("Y0"), psum("Y1")]
        M = [psum("M0"), psum("M1")]
        ZR = psum("ZR")
        HH = psum("HH")

        consts = sem("consts")
        ld_first, ld_l0f = sem("ld_first"), sem("ld_l0f")
        ld_x, ld_small, ld_l0, ld_gru = sem("ld_x"), sem("ld_small"), sem("ld_l0"), sem("ld_gru")
        ld_l1, ld_l2, ld_w1, ld_w2 = sem("ld_l1"), sem("ld_l2"), sem("ld_w1"), sem("ld_w2")
        u_full, u_free = sem("u_full"), sem("u_free")
        y_full, y_free = sem("y_full"), sem("y_free")
        m_full, m_free = sem("m_full"), sem("m_free")
        e_full, ga_full, gd_full = sem("e_full"), sem("ga_full"), sem("gd_full")
        hid_full, l3_hid = sem("hid_full"), sem("l3_hid")
        set_up = sem("set_up")
        acc_third, l0_sig, silu_done = sem("acc_third"), sem("l0_sig"), sem("silu_done")
        gru_zr, gru_gates, gru_rh = sem("gru_zr"), sem("gru_gates"), sem("gru_rh")
        gru_hh, gru_cand, gru_h = sem("gru_hh"), sem("gru_cand"), sem("gru_h")
        h_moved = sem("h_moved")
        soft_gap, soft_tanh, comb_ready = sem("soft_gap"), sem("soft_tanh"), sem("comb_ready")
        b_full, b_free = sem("b_full"), sem("b_free")
        scaled_hi, scaled_all = sem("scaled_hi"), sem("scaled_all")
        l3_hid_hi, l3_hid_all = sem("l3_hid_hi"), sem("l3_hid_all")
        relu_done = sem("relu_done")
        rnn_pre, rnn_h = sem("rnn_pre"), sem("rnn_h")
        l3_consts, l3_ready, out_done = sem("l3_consts"), sem("l3_ready"), sem("out_done")
        dve_own, pool_own = sem("dve_own"), sem("pool_own")

        L0_LOADS, L0F_LOADS, GRU_LOADS, L12_LOADS = 5, 2, 6, 2
        first_loads = [
            (cond[:, :], a["cond_1024"]),
            (rows[:, 0:E], a["L0_cond_router_bias"].unsqueeze(0)),
            (rows[:, E:2 * E], a["L1_ffn_gate_b"].unsqueeze(0)),
            (rows[:, 2 * E:3 * E], a["L2_ffn_gate_b"].unsqueeze(0)),
            (rows[:, 3 * E:], a["L1_ffn_temperature"].unsqueeze(0)),
            (l0_rw[:, :, :], a["L0_cond_router_W"].rearrange("(h d) e -> d h e", h=2)),
            (l0f_rw_in[:, :], a["L0_ffn_router_w"]),
        ]
        small_loads = [
            (gru_b_row[:, 0:D], a["L1_cond_b_z"].unsqueeze(0)),
            (gru_b_row[:, D:2 * D], a["L1_cond_b_r"].unsqueeze(0)),
            (gru_b_row[:, 2 * D:], a["L1_cond_b"].unsqueeze(0)),
            (rnn_b_row[:, :], a["L3_cond_b"].unsqueeze(0)),
            (fc_bias[:, :], a["L2_cond_fc_bias"].unsqueeze(0)),
            (gru_c[:, 0:D], a["L1_cond_C_z"]),
            (gru_c[:, D:2 * D], a["L1_cond_C_r"]),
            (gru_c[:, 2 * D:], a["L1_cond_C"]),
            (b1_in[0:E * Q, :], a["L1_ffn_b1"].rearrange("e (q p) -> (e q) p", p=P)),
            (b1_in[E * Q:, :], a["L2_ffn_b1"].rearrange("e (q p) -> (e q) p", p=P)),
            (b2[0][:, :], a["L1_ffn_b2"]),
            (b2[1][:, :], a["L2_ffn_b2"]),
            (gate_w[:, 0, :], a["L1_ffn_gate_w"]),
            (gate_w[:, 1, :], a["L2_ffn_gate_w"]),
            (l2_v[:, :].rearrange("i (b r) -> i b r", b=B), a["fside_Bx1x1024x16_0"].rearrange("b o i r -> (o i) b r")),
            (l2_w_in[:, :], a["L2_cond_W"]),
            (l3_p_in[:, :], a["L3_ffn_P_w"]),
            (l3_u_in[0:E3, :], a["L3_ffn_U1"]),
            (l3_u_in[E3:2 * E3, :], a["L3_ffn_U2"]),
            (l3_u_in[2 * E3:, :], a["L3_ffn_U3"]),
            (l3_b2[:, :], a["L3_ffn_b2"]),
            (rnn_w[:, 0, :], a["L3_cond_Wx"]),
            (rnn_w[:, 1, :], a["L3_cond_Wh"]),
        ]
        FIRST, SMALL = len(first_loads), len(small_loads)

        def bank_of(exchanges, name):
            return U[0] if name == "z" else M[(M0_L12 + exchanges.index(name if name != "pre" else "z")) % 2]

        block = ctx.enter_context(nc.Block())

        @block.sync
        def _(sp):
            sp.dma_start(x_in, a["x"].rearrange("b t d -> t b d")).then_inc(ld_x, 16)
            for dst, src in first_loads:
                sp.dma_start(dst, src).then_inc(ld_first, 16)
            sp.dma_start(l0_w13[:, 0, :], a["L0_cond_w1"]).then_inc(ld_l0, 16)
            sp.dma_start(l0_w13[:, 1, :], a["L0_cond_w3"]).then_inc(ld_l0, 16)
            sp.dma_start(l0_up[:, :, :], a["L0_cond_W1e"].rearrange("e c h -> c e h")).then_inc(ld_l0, 16)
            sp.dma_start(l0_w2[:, :, :], a["L0_cond_w2"].rearrange("(q p) d -> p q d", p=P)).then_inc(ld_l0, 16)
            sp.dma_start(l0_dn[:, :, :], a["L0_cond_W2e"].rearrange("e h c -> h e c")).then_inc(ld_l0, 16)
            sp.dma_start(l0f_up[:, :], a["L0_ffn_w1"]).then_inc(ld_l0f, 16)
            sp.dma_start(l0f_dn[:, :, :], a["L0_ffn_w2"].rearrange("(q p) d -> p q d", p=P)).then_inc(ld_l0f, 16)
            sp.dma_start(stage[:, :].rearrange("p (e q d) -> p e q d", e=E3, q=Q),
                         a["L3_ffn_W1"].rearrange("e (q p) d -> p e q d", p=P)).then_inc(ld_w1, 16)
            for dst, src in small_loads:
                sp.dma_start(dst, src).then_inc(ld_small, 16)
            for g, s in enumerate(("_z", "_r", "")):
                sp.dma_start(gru_w[:, g, :], a["L1_cond_W" + s]).then_inc(ld_gru, 16)
                sp.dma_start(gru_u[:, g, :], a["L1_cond_U" + s]).then_inc(ld_gru, 16)
            sp.dma_start(up[0][:, :, :], a["L1_ffn_W1"].rearrange("e d f -> d e f")).then_inc(ld_l1, 16)
            sp.dma_start(dn[0][:, :, :, :], a["L1_ffn_W2"].rearrange("e (q p) d -> p e q d", p=P)).then_inc(ld_l1, 16)
            sp.dma_start(up[1][:, :, :], a["L2_ffn_w1"].rearrange("e d f -> d e f")).then_inc(ld_l2, 16)
            sp.dma_start(dn[1][:, :, :, :], a["L2_ffn_w2"].rearrange("e (q p) d -> p e q d", p=P)).then_inc(ld_l2, 16)
            sp.wait_ge(m_full, m_l0("up", E3 - 1) + 1)
            sp.dma_start(stage[:, :].rearrange("o (e h) -> o e h", e=E3),
                         a["L3_ffn_W2"].rearrange("e o h -> o e h")).then_inc(ld_w2, 16)
            with sp.Fori(0, CHUNKS) as c:
                for i in range(TILES):
                    sp.wait_ge(y_free, Y0_L3 + c * Y_L3 + (i + 1) * E3 // 4)
                    for b in range(P // CT):
                        sp.dma_start(out[i * (P // CT) + b, bass.ds(c * CT, CT), :],
                                     acc_a[b * CT:(b + 1) * CT, i, :]).then_inc(out_done, 16)
            sp.wait_ge(out_done, CHUNKS * B * 16)

        @block.gpsimd
        def _(pool):
            own = OwnOrder(pool, pool_own)
            own(pool.memset(ident[:, :], 0.0))
            own(pool.memset(sel_batch[:, :], 0.0))
            own(pool.memset(rank_mask[:, :], 1.0 / (D * R)))
            own(pool.memset(earlier8[:, :, :], 1.0))
            own(pool.memset(earlier12[:, :, :], 1.0))
            pool.memset(ones_row[:, :], 1.0).then_inc(consts, 1)
            pool.memset(h_gru[:, 0:B], 0.0).then_inc(consts, 1)
            pool.affine_select(out=ident[:, :], in_=ident[:, :], compare_op=ALU.not_equal, fill=1.0,
                               base=0, pattern=[[-1, P]], channel_multiplier=1).then_inc(consts, 1)
            sbv = sel_batch[:, :].rearrange("p (t b) -> p t b", b=B)
            pool.affine_select(out=sbv, in_=sbv, compare_op=ALU.not_equal, fill=1.0,
                               base=0, pattern=[[0, CT], [-1, B]], channel_multiplier=1).then_inc(consts, 1)
            rm = rank_mask[:, 0:B]
            own(pool.affine_select(out=rm, in_=rm, compare_op=ALU.is_ge, fill=0.0,
                                   base=0, pattern=[[-R, B]], channel_multiplier=1))
            pool.affine_select(out=rm, in_=rm, compare_op=ALU.is_ge, fill=0.0,
                               base=R - 1, pattern=[[R, B]], channel_multiplier=-1).then_inc(consts, 1)
            for t, n in ((earlier8, E), (earlier12, E3)):
                pool.affine_select(out=t[:, :, :], in_=t[:, :, :], compare_op=ALU.is_gt, fill=0.0,
                                   base=0, pattern=[[1, n], [-1, n]], channel_multiplier=0).then_inc(consts, 1)

            pool.wait_ge(h_moved, 2)
            own(pool.memset(sel_expert[:, :, :].bitcast(F32), 0.0))
            pool.affine_select(out=sel_expert[:, :, :], in_=sel_expert[:, :, :], compare_op=ALU.not_equal, fill=1.0,
                               base=0, pattern=[[-1, E3], [0, P]], channel_multiplier=1).then_inc(l3_consts, 1)

            def scaled_low(c, j):
                pool.wait_ge(scaled_hi, c * (E3 // 2) + j + 1)
                nc.gpsimd.tensor_tensor(out=scaled[1][:, 2 * j:2 * j + 2, :].rearrange("p e n -> p (e n)"),
                                        in0=weighted[:, j % 2, :],
                                        in1=scaled[0][:, 2 * j:2 * j + 2, :].rearrange("p e n -> p (e n)"),
                                        op=ALU.subtract).then_inc(scaled_all, 1)

            def hidden_low(c, half):
                pool.wait_ge(l3_hid_hi, 2 * c + half + 1)
                nc.gpsimd.tensor_tensor(out=hid3[1][:, half, :], in0=gated[:, half, :], in1=hid3[0][:, half, :],
                                        op=ALU.subtract).then_inc(l3_hid_all, 1)

            for j in range(E3 // 2):
                scaled_low(0, j)
            with pool.Fori(0, CHUNKS - 1) as c:
                for half in range(2):
                    hidden_low(c, half)
                for j in range(E3 // 2):
                    scaled_low(c + 1, j)
            for half in range(2):
                hidden_low(CHUNKS - 1, half)

        @block.scalar
        def _(sc):
            sc.wait_ge(m_free, M_PRO)
            nc.scalar.activation(sig_a[:, 0:T * B // P * E], score[:, 0:T * B // P * E], ACT.Sigmoid).then_inc(l0_sig, 1)

            def gru_gates_of(chunk, t):
                sc.wait_ge(gru_zr, chunk * CT + t + 1)
                zr = ZR[:, :].rearrange("p (g n) -> p g n", g=2)[:, :, at(t * B, B)]
                nc.scalar.activation(zr_s[:, :, :], zr, ACT.Tanh, scale=0.5).then_inc(gru_gates, 1)

            def gru_cand_of(chunk, t):
                sc.wait_ge(gru_hh, chunk * CT + t + 1)
                nc.scalar.activation(cand[:, :], HH[:, at(t * B, B)], ACT.Tanh).then_inc(gru_cand, 1)

            def rnn_step(chunk, t):
                step = chunk * CT + t
                sc.wait_ge(rnn_pre, step + 1)
                nc.scalar.activation(h3[:, at((step + 1) * B, B)], ZR[:, t * B:(t + 1) * B], ACT.Tanh).then_inc(rnn_h, 1)

            def hidden_l0(n):
                stream, i, k = L0_UNITS[n]
                if (stream, i) == ("C", 1):
                    return
                sc.wait_ge(u_full, U_X + n + 1)
                if (stream, i) == ("C", 0):
                    nc.scalar.activation(act[:, :], U[n % 2][:, :], ACT.Tanh, scale=0.5).then_inc(e_full, 1)
                elif stream == "C":
                    nc.scalar.activation(gated[:, n % 4, :], U[n % 2][:, :], ACT.Gelu).then_inc(ga_full, 1)
                else:
                    nc.scalar.activation(relu[:, i % 2, :], U[n % 2][:, :], ACT.Relu).then_inc(relu_done, 1)

            def square_l0(n):
                stream, i, k = L0_UNITS[n]
                if stream == "F":
                    sc.wait_ge(relu_done, k * 6 + i + 1)
                    nc.scalar.activation(gated[:, n % 4, :], relu[:, i % 2, :], ACT.Square).then_inc(ga_full, 1)

            def gru_step(step):
                gru_gates_of(step // CT, step % CT)
                gru_cand_of(step // CT, step % CT)

            def idle(*_):
                pass

            for n in range(L0_SLOTS):
                steps = steps_l0(n)
                for step in steps[:1]:
                    gru_step(step)
                if n < len(L0_UNITS):
                    hidden_l0(n)
                if 5 <= n < len(L0_UNITS) + 5 and L0_UNITS[n - 5][:2] == ("C", 5):
                    sc.wait_ge(m_free, m_l0("logits", L0_UNITS[n - 5][2]) + 1)
                    nc.scalar.activation(sig_a[:, 0:TILES * E], score[:, 0:TILES * E], ACT.Sigmoid).then_inc(l0_sig, 1)
                for step in steps[1:]:
                    gru_gates_of(step // CT, step % CT)
                if n < len(L0_UNITS):
                    square_l0(n)
                for step in steps[1:]:
                    gru_cand_of(step // CT, step % CT)

            def softmax_tanh(count, n):
                sc.wait_ge(soft_gap, count)
                nc.scalar.activation(sig_a[:, 0:n], gap[:, 0:n], ACT.Tanh, scale=0.5).then_inc(soft_tanh, 1)

            def l12(k, exchanges, steps, between):
                for l in range(2):
                    y0 = Y0_L12 + (2 * k + l) * E

                    def hidden(u):
                        sc.wait_ge(u_full, U0_L12 + (2 * k + l) * LU + u + 1)
                        sc.wait_ge(y_full, y0 + u // 2 - 1)
                        for h in range(2):
                            col = l * E * Q + 2 * u + h
                            last = nc.scalar.activation(gated[:, u % 4, h * N:(h + 1) * N], U[u % 2][:, h * N:(h + 1) * N],
                                                        ACT.Gelu, bias=b1T[:, col:col + 1])
                        last.then_inc(hid_full, 1)

                    for u in range(LU):
                        steps(l, u)
                        hidden(u)
                        if u == 1:
                            softmax_tanh(2 * k + l + 1, TILES * E)
                        if u == 8 and l == 1 and "score" in exchanges:
                            softmax_tanh(2 * CHUNKS + 1, TILES * NR3 * E3)
                    if l == 0:
                        between[0](0)
                        between[1](0)
                        between[0](1)
                        between[1](1)
                        between[0](2)
                        idx = M0_L12 + k * len(X_BODY) + exchanges.index("pre")
                        sc.wait_ge(m_full, idx + 1)
                        nc.scalar.activation(l2_in[:, :], bank_of(exchanges, "pre")[:, 0:N], ACT.Gelu).then_inc(m_free, 1)
                        between[1](2)

            def gru_beside(chunk):
                def step(t):
                    gru_gates_of(chunk, t)
                    gru_cand_of(chunk, t)

                def steps(l, u):
                    if l == 0 or u >= LATE:
                        step(l * LU + u)

                between = (lambda n: gru_gates_of(chunk, LU + n), lambda n: gru_cand_of(chunk, LU + n))
                return steps, between

            def rnn_beside(l, u):
                for s in (0, 1):
                    rnn_step(l, 2 * u + s)

            with sc.Fori(0, CHUNKS - 1) as k:
                nc.scalar.activation(table[:, :], inv_temp[:, :], ACT.Gelu)
                l12(k, X_BODY, *gru_beside(k + 1))
            l12(CHUNKS - 1, X_END, rnn_beside, (idle, idle))

            def l3(c, step, route_next):
                for half in range(2):
                    for s in range(8):
                        step(half * 8 + s)
                    if half == 0 and route_next:
                        softmax_tanh(2 * CHUNKS + c + 2, TILES * NR3 * E3)
                    sc.wait_ge(u_full, U0_L3 + c * 2 + half + 1)
                    sc.wait_ge(y_full, Y0_L3 + c * Y_L3)
                    nc.scalar.activation(gated[:, half, :], U[half][:, :], ACT.Gelu).then_inc(l3_hid, 1)
                    sc.wait_ge(l3_hid, 2 * c + half + 1)
                    nc.scalar.activation(hid3[0][:, half, :], gated[:, half, :], ACT.Copy).then_inc(l3_hid_hi, 1)
                for s in range(16, CT):
                    step(s)

            with sc.Fori(0, 2) as c:
                l3(c, lambda s: rnn_step(c + 2, s), True)
            l3(2, idle, True)
            l3(CHUNKS - 1, idle, False)

        @block.vector
        def _(dve):
            own = OwnOrder(dve, dve_own)
            v = nc.vector

            def tt(out, in0, in1, op):
                return v.tensor_tensor(out=out, in0=in0, in1=in1, op=op)

            def ts(out, in0, s1, op0, s2=None, op1=None):
                if op1 is None:
                    return v.tensor_scalar(out, in0, s1, None, op0)
                return v.tensor_scalar(out, in0, s1, s2, op0, op1)

            def stt(out, in0, scalar, in1, op0, op1):
                return v.scalar_tensor_tensor(out=out, in0=in0, scalar=scalar, in1=in1, op0=op0, op1=op1)

            def grp(t, g, n):
                return t[:, 0:g * n].rearrange("p (g n) -> p g n", g=g)

            def over(t, g, n):
                return t[:, 0:g].unsqueeze(2).to_broadcast([P, g, n])

            def by_tile(bank):
                return bank[:, 0:TILES * D].rearrange("p (i d) -> p i d", i=TILES)

            def rank_compare(scores, g, n, room):
                s = grp(scores, g, n)
                ca, cb = [t[:, 0:g * n * n].rearrange("p (g a b) -> p g a b", g=g, a=n) for t in room]
                other = s.unsqueeze(2).to_broadcast([P, g, n, n])
                mine = s.unsqueeze(3).to_broadcast([P, g, n, n])
                earlier = earlier8 if n == E else earlier12
                tt(ca, other, mine, ALU.is_gt)
                own(tt(cb, other, mine, ALU.is_equal))
                own(tt(cb, cb, earlier[:, :, :].unsqueeze(1).to_broadcast([P, g, n, n]), ALU.mult))

            def rank_mask_top(g, n, k, room):
                ca, cb = [t[:, 0:g * n * n].rearrange("p (g a b) -> p g a b", g=g, a=n) for t in room]
                own(tt(ca, ca, cb, ALU.add))
                own(v.tensor_reduce(out=grp(rank, g, n), in_=ca, axis=AX.X, op=ALU.add))
                own(ts(mask[:, 0:g * n], rank[:, 0:g * n], k - 0.5, ALU.is_lt))

            def top_mask(scores, g, n, k, room):
                rank_compare(scores, g, n, room)
                rank_mask_top(g, n, k, room)

            def softmax_gaps(g, n):
                own(v.tensor_reduce(out=top[:, 0:g], in_=grp(score, g, n), axis=AX.X, op=ALU.max))
                tt(grp(gap, g, n), grp(score, g, n), over(top, g, n), ALU.subtract).then_inc(soft_gap, 1)

            def softmax_terms(count, g, n):
                m = g * n
                dve.wait_ge(soft_tanh, count)
                own(ts(sig_b[:, 0:m], sig_a[:, 0:m], -1.0, ALU.mult, 1.0, ALU.add))
                own(v.reciprocal(sig_b[:, 0:m], sig_b[:, 0:m]))
                own(stt(sig_a[:, 0:m], sig_a[:, 0:m], 1.0, sig_b[:, 0:m], ALU.add, ALU.mult))

            def softmax_combine(g, n, comb_to):
                m = g * n
                own(tt(sig_a[:, 0:m], sig_a[:, 0:m], mask[:, 0:m], ALU.mult))
                own(v.tensor_reduce(out=den[:, 0:g], in_=grp(sig_a, g, n), axis=AX.X, op=ALU.add))
                own(v.reciprocal(den[:, 0:g], den[:, 0:g]))
                tt(grp(comb_to, g, n), grp(sig_a, g, n), over(den, g, n), ALU.mult).then_inc(comb_ready, 1)

            def gru_reset(chunk, t):
                step = chunk * CT + t
                h = h_gru[:, at(t * B, B)]
                dve.wait_ge(gru_gates, step + 1)
                if not isinstance(step, int) or step:
                    dve.wait_ge(gru_h, step)
                stt(rh[:, :], zr_s[:, 1, :], 1.0, h, ALU.add, ALU.mult).then_inc(gru_rh, 1)
                own(stt(zh[:, :], zr_s[:, 0, :], 1.0, h, ALU.add, ALU.mult))
                own(stt(keep[:, :], zh[:, :], -0.5, h, ALU.mult, ALU.add))

            def gru_update(chunk, t):
                dve.wait_ge(gru_cand, chunk * CT + t + 1)
                own(stt(fresh[:, :], zr_s[:, 0, :], 1.0, cand[:, :], ALU.add, ALU.mult))
                stt(h_gru[:, at((t + 1) * B, B)], fresh[:, :], 0.5, keep[:, :], ALU.mult, ALU.add).then_inc(gru_h, 1)

            for i in range(2):
                dve.wait_ge(u_full, i + 1)
                v.tensor_copy(xT.rearrange("d (t b) -> d b t", b=B)[:, 4 * i:4 * i + 4, :],
                              U[i][:, :].rearrange("d (b t) -> d b t", b=4)).then_inc(u_free, 1)
            dve.wait_ge(m_full, 1)
            own(v.tensor_copy(condT[:, :], M[0][:, 0:B]))
            v.tensor_copy(cond_tok[:, :].rearrange("d (t b) -> d t b", b=B),
                          condT[:, :].unsqueeze(1).to_broadcast([P, P // B, B])).then_inc(set_up, 1)
            own(v.tensor_copy(bc[:, :], M[0][:, B:B + 3 * E + 1]))
            v.tensor_copy(l0f_rw[:, :], M[0][:, 64:64 + E]).then_inc(m_free, 1)
            own(v.reciprocal(inv_temp[:, :], bc[:, 3 * E:]))
            v.tensor_copy(h3[:, 0:B], condT[:, :]).then_inc(set_up, 1)
            dve.wait_ge(consts, 7)

            GX = T * B // P
            SX = GX * E
            dve.wait_ge(m_full, M_PRO)
            v.tensor_copy(score[:, 0:SX], M[1][:, 0:SX]).then_inc(m_free, 1)

            def route_c():
                dve.wait_ge(l0_sig, 1)
                own(tt(grp(gap, GX, E), grp(sig_a, GX, E), bc[:, 0:E].unsqueeze(1).to_broadcast([P, GX, E]), ALU.add))
                top_mask(gap, GX, E, 2, (relu[:, 0, :], relu[:, 1, :]))
                own(tt(comb_x[:, :], sig_a[:, 0:SX], mask[:, 0:SX], ALU.mult))
                own(v.tensor_reduce(out=den[:, 0:GX], in_=grp(comb_x, GX, E), axis=AX.X, op=ALU.add))
                own(ts(okay[:, 0:GX], den[:, 0:GX], 1e-9, ALU.is_gt))
                own(ts(den[:, 0:GX], den[:, 0:GX], 1e-9, ALU.add))
                own(v.reciprocal(den[:, 0:GX], den[:, 0:GX]))
                own(tt(den[:, 0:GX], den[:, 0:GX], okay[:, 0:GX], ALU.mult))
                own(tt(grp(comb_x, GX, E), grp(comb_x, GX, E), over(den, GX, E), ALU.mult))
                own(ts(okay[:, 0:GX], okay[:, 0:GX], -0.5, ALU.mult, 0.5, ALU.add))
                own(tt(grp(mask, GX, E), grp(mask, GX, E), over(okay, GX, E), ALU.mult))
                own(tt(comb_x[:, :], comb_x[:, :], mask[:, 0:SX], ALU.add))

            def add_experts(count, bank, pieces, acc, comb, first=False, part=range(2 * TILES)):
                dve.wait_ge(y_full, count)
                for n, (col, i, e) in enumerate(pieces):
                    if n not in part:
                        continue
                    src = Y[bank][:, col:col + D]
                    weight = comb[:, i * E + e:i * E + e + 1]
                    if first and n < TILES:
                        ins = ts(acc[:, i, :], src, weight, ALU.mult)
                    else:
                        ins = stt(acc[:, i, :], src, weight, acc[:, i, :], ALU.mult, ALU.add)
                    if n == len(pieces) - 1:
                        ins.then_inc(y_free, 1)
                        dve.wait_ge(y_free, count)
                    elif n % TILES == TILES - 1:
                        own(ins)

            S = TILES * E

            def f_router_compare(k):
                dve.wait_ge(l0_sig, k + 1)
                rank_compare(sig_a, TILES, E, (cmp_a, cmp_b))

            def f_router_weights():
                own(tt(comb_b[:, :], sig_a[:, 0:S], mask[:, 0:S], ALU.mult))
                own(v.tensor_reduce(out=den[:, 0:TILES], in_=grp(comb_b, TILES, E), axis=AX.X, op=ALU.add))
                own(ts(den[:, 0:TILES], den[:, 0:TILES], 1e-20, ALU.add))
                own(v.reciprocal(den[:, 0:TILES], den[:, 0:TILES]))
                own(tt(grp(comb_b, TILES, E), grp(comb_b, TILES, E), over(den, TILES, E), ALU.mult))

            PAIR = [((i * 2 + e2) * D, e2, i) for e2 in range(2) for i in range(TILES)]

            def finish(n):
                stream, i, k = L0_UNITS[n]
                if (stream, i) == ("C", 0):
                    dve.wait_ge(e_full, k + 1)
                    stt(silu[:, :], act[:, :], 1.0, U[n % 2][:, :], ALU.add, ALU.mult).then_inc(silu_done, 1)
                if (stream, i) == ("C", 1):
                    dve.wait_ge(u_full, U_X + n + 1)
                    dve.wait_ge(silu_done, k + 1)
                    stt(gated[:, n % 4, :], silu[:, :], 0.5, U[n % 2][:, :], ALU.mult, ALU.mult).then_inc(gd_full, 1)

            def add_l0(n, half):
                if not 0 <= n < len(L0_UNITS) or n not in L0_DOWNS:
                    return
                stream, i, k = L0_UNITS[n]
                j, part = L0_DOWNS.index(n), range(half * TILES, (half + 1) * TILES)
                if (stream, i) == ("C", 1):
                    if half == 0:
                        return
                    dve.wait_ge(y_full, j + 1)
                    v.tensor_copy(comb_a[:, :], comb_x[:, k * S:(k + 1) * S])
                    v.tensor_copy(acc_a[:, :, :], by_tile(Y[j % 2])).then_inc(y_free, 1)
                    dve.wait_ge(y_free, j + 1)
                elif stream == "C":
                    add_experts(j + 1, j % 2, [(c, t, 2 * (i - 2) + e2) for c, e2, t in PAIR], acc_a, comb_a, part=part)
                    if i == 5 and half == 1:
                        ts(acc_a[:, :, :], acc_a[:, :, :], 1.0 / 3.0, ALU.mult).then_inc(acc_third, 1)
                elif i == 0:
                    if half == 1:
                        add_experts(j + 1, j % 2, [(c, t, e2) for c, e2, t in PAIR], acc_b, comb_b, first=True)
                elif i == 1:
                    add_experts(j + 1, j % 2, [(c, t, 2 + e2) for c, e2, t in PAIR], acc_b, comb_b, part=part)
                elif half == 0:
                    add_experts(j + 1, j % 2, [(t * D, t, 2 + i) for t in range(TILES)], acc_b, comb_b)

            def taken_l0(*name):
                idx = m_l0(*name)
                dve.wait_ge(m_full, idx + 1)
                return M[idx % 2]

            def later_set_up():
                m = taken_l0("mid", 0)
                v.tensor_copy(l2_uT[:, :], m[:, 0:P])
                v.tensor_copy(l2_wT[:, :], m[:, P:2 * P]).then_inc(m_free, 1)
                m = taken_l0("mid", 1)
                v.tensor_copy(cond[:, :], m[0:B, 3 * D:])
                v.tensor_copy(gru_vb[:, :], m[0:B, 0:3 * D]).then_inc(m_free, 1)
                m = taken_l0("mid", 2)
                v.tensor_copy(b1T[:, :], m[:, 0:2 * E * Q])
                v.tensor_copy(l3_pT[:, :], m[:, 128:128 + DA])
                v.tensor_copy(l3_uT[:, :], m[0:DA, 256:256 + NR3 * E3]).then_inc(m_free, 1)
                dve.wait_ge(ld_gru, 16 * GRU_LOADS)
                ts(gru_u[:, 2, :], gru_u[:, 2, :], 0.5, ALU.mult).then_inc(set_up, 1)

            def gru_moved(k):
                dve.wait_ge(gru_h, (k + 1) * CT)
                v.tensor_copy(l1_in[:, :], h_gru[:, B:])
                v.tensor_copy(h_gru[:, 0:B], h_gru[:, CT * B:]).then_inc(h_moved, 1)
                dve.wait_ge(h_moved, k + 1)

            def take_sums(n):
                if n == MID_SLOT + 1:
                    later_set_up()
                for e in [e for e in range(E3) if W1_SLOTS[e] == n - 1]:
                    w = taken_l0("up", e)
                    own(v.tensor_copy(l3_up[0][:, e, :], w[:, :]))
                    tt(l3_up[1][:, e, :], w[:, :], l3_up[0][:, e, :], ALU.subtract).then_inc(m_free, 1)
                for back in (4, 5):
                    stream, i, k = L0_UNITS[n - back] if 0 <= n - back < len(L0_UNITS) else ("", 0, 0)
                    if back == 4 and (stream, i) == ("C", 5):
                        v.tensor_copy(c0[k % 2][:, :], taken_l0("c", k)[:, 0:N]).then_inc(m_free, 1)
                    if back == 4 and (stream, i) == ("F", 5):
                        tt(x1[:, k * N:(k + 1) * N], xT[:, k * N:(k + 1) * N], taken_l0("f", k)[:, 0:N], ALU.add).then_inc(m_free, 1)
                    if back == 5 and (stream, i) == ("C", 5):
                        v.tensor_copy(score[:, 0:S], taken_l0("logits", k)[:, 0:S]).then_inc(m_free, 1)

            def route_f(n):
                for back in (6, 7, 8):
                    stream, i, k = L0_UNITS[n - back] if 0 <= n - back < len(L0_UNITS) else ("", 0, 0)
                    if (stream, i) == ("C", 5):
                        if back == 6:
                            f_router_compare(k + 1)
                        elif back == 7:
                            rank_mask_top(TILES, E, 2, (cmp_a, cmp_b))
                        else:
                            f_router_weights()

            def idle(*_):
                pass

            for n in range(L0_SLOTS):
                steps = steps_l0(n)
                if steps:
                    gru_reset(0, steps[0])
                if 0 < n <= len(L0_UNITS):
                    finish(n - 1)
                if n == 2:
                    route_c()
                add_l0(n - 3, 0)
                if steps:
                    gru_update(0, steps[0])
                route_f(n)
                for step in steps[1:]:
                    gru_reset(0, step)
                take_sums(n)
                add_l0(n - 3, 1)
                for step in steps[1:]:
                    gru_update(0, step)
                if CT - 1 in steps:
                    gru_moved(0)

            def routing_scores(l, idx, bank):
                dve.wait_ge(m_full, idx + 1)
                tt(grp(score, TILES, E), grp(bank, TILES, E),
                   bc[:, (1 + l) * E:(2 + l) * E].unsqueeze(1).to_broadcast([P, TILES, E]), ALU.add).then_inc(m_free, 1)
                dve.wait_ge(m_free, idx + 1)
                if l == 0:
                    own(ts(score[:, 0:S], score[:, 0:S], inv_temp[:, 0:1], ALU.mult))
                softmax_gaps(TILES, E)

            def layer(k, exchanges, l):
                m0, y0 = M0_L12 + k * len(X_BODY), Y0_L12 + (2 * k + l) * E
                acc, comb_l, combT = ((acc_a, comb_a, combT_a), (acc_b, comb_b, combT_b))[l]

                def taken(name):
                    dve.wait_ge(m_full, m0 + exchanges.index(name) + 1)
                    return bank_of(exchanges, name)

                def add(e):
                    if e == 0:
                        dve.wait_ge(comb_ready, 2 * k + l + 1)
                    add_experts(y0 + e + 1, e % 2, [(i * D, i, e) for i in range(TILES)], acc, comb_l, e == 0)

                def routing(u):
                    n = u + l
                    if n == 1:
                        rank_compare(score, TILES, E, (cmp_a, cmp_b))
                    if n == 2:
                        rank_mask_top(TILES, E, 2, (cmp_a, cmp_b))
                    if n == 3:
                        softmax_terms(2 * k + l + 1, TILES, E)
                    if n == 4:
                        softmax_combine(TILES, E, comb_l)
                    if n == 6:
                        v.tensor_copy(combT[:, :], taken(f"w{l}")[0:E, 0:N]).then_inc(m_free, 1)
                    if (l, u) == (1, 7):
                        biases()

                def biases():
                    tt(acc[:, :, :], acc[:, :, :], by_tile(taken(f"b{l}")), ALU.add).then_inc(m_free, 1)
                    dve.wait_ge(m_free, m0 + exchanges.index(f"b{l}") + 1)

                def total():
                    out = (x1, x3)[l]
                    tt(out[:, at(k * N, N)], x1[:, at(k * N, N)], taken(f"sum{l}")[:, 0:N], ALU.add).then_inc(m_free, 1)

                return add, routing, total, taken, biases

            def head(c, steps, more, idx, bank, last_of=None):
                reset, update, _ = steps
                routing = layer(c, X_BODY, 0)[1]
                if last_of:
                    last_of[0](E - 2)
                for u in range(2):
                    reset(0, u)
                    if last_of and u == 1:
                        last_of[0](E - 1)
                    update(0, u)
                    if u == 0:
                        routing_scores(0, idx, bank)
                    routing(u)
                    more(0, u)
                if last_of:
                    last_of[2]()

            def rest(k, exchanges, steps, more):
                m0 = M0_L12 + k * len(X_BODY)
                reset, update, between = steps
                for l in range(2):
                    add, routing, total, taken, biases = layer(k, exchanges, l)
                    if l == 1:
                        routing_scores(1, m0 + exchanges.index("logits1"), bank_of(exchanges, "logits1"))
                    for u in range(2 - 2 * l, LU):
                        reset(l, u)
                        update(l, u)
                        if u >= 5 and u % 2 == 1:
                            add((u - 5) // 2)
                        routing(u)
                        more(l, u)
                    if l == 0:
                        add(E - 2)
                        between[0](0)
                        biases()
                        between[1](0)
                        add(E - 1)
                        between[0](1)
                        total()
                        between[1](1)
                        tt(z1m[:, :].rearrange("p (t b) -> p t b", b=B), taken("z")[:, 0:N].rearrange("p (t b) -> p t b", b=B),
                           rank_mask[:, 0:B].unsqueeze(1).to_broadcast([P, CT, B]), ALU.mult).then_inc(m_free, 1)
                        between[0](2)
                        between[1](2)

            def gru_beside(chunk):
                def at_step(do):
                    def steps(l, u):
                        if l == 0 or u >= LATE:
                            do(chunk, l * LU + u)
                    return steps
                between = (lambda n: gru_reset(chunk, LU + n), lambda n: gru_update(chunk, LU + n))
                return at_step(gru_reset), at_step(gru_update), between

            def next_head(k, steps, more):
                gru_moved(k + 1)
                head(k + 1, steps, more, M0_L12 + k * len(X_BODY) + X_BODY.index("logits0"), bank_of(X_BODY, "logits0"),
                     layer(k, X_BODY, 1))

            head(0, gru_beside(1), idle, M_START, M[M_START % 2])
            L12_OWN = 121
            with dve.Fori(0, CHUNKS - 2) as k:
                own.enter(k, L12_OWN)
                rest(k, X_BODY, gru_beside(k + 1), idle)
                next_head(k, gru_beside(k + 2), idle)
                own.leave(CHUNKS - 2, L12_OWN)
            rest(CHUNKS - 2, X_BODY, gru_beside(CHUNKS - 1), idle)

            GR = TILES * NR3

            def l3_gather(c):
                dve.wait_ge(rnn_h, (c + 1) * CT)
                v.tensor_copy(l3_in.rearrange("p (b t) -> p b t", b=B),
                              h3[:, at(c * N + B, N)].rearrange("p (t b) -> p b t", b=B)).then_inc(l3_ready, 1)

            def l3_residual(c):
                v.tensor_copy(x3_c.rearrange("p (b t) -> p b t", b=B),
                              x3[:, at(c * N, N)].rearrange("p (t b) -> p b t", b=B)).then_inc(l3_ready, 1)

            def l3_address(idx, bank):
                dve.wait_ge(m_full, idx + 1)
                v.tensor_copy(addr, bank[0:DA, 0:N]).then_inc(m_free, 1)

            def l3_scores(idx, bank):
                dve.wait_ge(m_full, idx + 1)
                v.tensor_copy(score[:, :], bank[:, 0:GR * E3]).then_inc(m_free, 1)
                dve.wait_ge(m_free, idx + 1)
                softmax_gaps(GR, E3)

            def l3_compare():
                rank_compare(score, GR, E3, (l3_cmp_a, l3_cmp_b))

            def l3_mask():
                rank_mask_top(GR, E3, 3, (l3_cmp_a, l3_cmp_b))

            def l3_weights(idx, bank):
                dve.wait_ge(m_full, idx + 1)
                own(v.tensor_copy(dwT[0][:, :], bank[0:E3, 0:N]))
                tt(dwT[1][:, :], bank[0:E3, 0:N], dwT[0][:, :], ALU.subtract)
                v.tensor_copy(dwT_third[:, :], bank[0:E3, N:]).then_inc(m_free, 1)

            def l3_scale(c, j):
                dve.wait_ge(b_full, c * (E3 // 2) + j + 1)
                bank = (HH, U[1])[j % 2]
                done = c * (E3 // 2) + j
                if not isinstance(c, int) or c or j >= 2:
                    dve.wait_ge(scaled_all, done - 1)
                tt(weighted[:, j % 2, :].rearrange("p (e n) -> p e n", e=2), bank[:, :].rearrange("p (e n) -> p e n", e=2),
                   l3_in.unsqueeze(1).to_broadcast([P, 2, N]), ALU.mult).then_inc(b_free, 1)
                dve.wait_ge(b_free, done + 1)
                v.tensor_copy(scaled[0][:, 2 * j:2 * j + 2, :].rearrange("p e n -> p (e n)"),
                              weighted[:, j % 2, :]).then_inc(scaled_hi, 1)

            m_last = M0_L12 + (CHUNKS - 1) * len(X_BODY)

            def take_w2(e):
                dve.wait_ge(m_full, m_last + X_END.index(f"t{e}") + 1)
                w = bank_of(X_END, f"t{e}")[:, :].rearrange("p (q d) -> p q d", q=Q)
                hi, lo = [half[:, :, e % 4, :] for half in l3_dn[e // 4]]
                own(v.tensor_copy(hi, w))
                tt(lo, w, hi, ALU.subtract).then_inc(m_free, 1)

            def beside_last(l, u):
                def exchange(name):
                    return m_last + X_END.index(name), bank_of(X_END, name)

                if l == 1:
                    if u == 1:
                        l3_gather(0)
                        l3_residual(0)
                    if u == 3:
                        l3_address(*exchange("addr"))
                    if u == 6:
                        l3_scores(*exchange("score"))
                    if u == 8:
                        l3_compare()
                    if u == 10:
                        l3_mask()
                    if u == 12:
                        softmax_terms(2 * CHUNKS + 1, GR, E3)
                        softmax_combine(GR, E3, comb)
                for e in w2_beside(l, u - 1):
                    take_w2(e)
                if (l, u) == (1, 14):
                    l3_weights(*exchange("dw"))

            beside = (idle, idle, (idle, idle))
            next_head(CHUNKS - 2, beside, beside_last)
            rest(CHUNKS - 1, X_END, beside, beside_last)
            add, _, total, _, _ = layer(CHUNKS - 1, X_END, 1)
            add(E - 2)
            add(E - 1)
            for j in range(E3 // 2):
                l3_scale(0, j)
                if j == 1:
                    total()

            def l3(c, route_next):
                m0, y0 = M0_L3 + c * M_L3, Y0_L3 + c * Y_L3
                own(v.tensor_copy(mix2[:, :, :], comb[:, :].rearrange("p (i r e) -> p i r e", i=TILES, r=NR3)[:, :, 1, :]))
                if route_next:
                    l3_gather(c + 1)
                    l3_address(m0, M[0])
                    l3_scores(m0 + 1, M[1])
                    l3_compare()
                    l3_mask()
                    softmax_terms(2 * CHUNKS + 2 + c, GR, E3)
                    softmax_combine(GR, E3, comb)
                sums = m0 + 2 if route_next else m0
                dve.wait_ge(m_full, sums + 1)
                if not isinstance(c, int) or c:
                    dve.wait_ge(out_done, c * (B * 16))
                v.tensor_copy(acc_a[:, :, :], by_tile(M[0])).then_inc(m_free, 1)
                dve.wait_ge(m_free, sums + 1)
                if route_next:
                    l3_residual(c + 1)
                    l3_weights(m0 + 3, M[1])
                for i in range(TILES):
                    for g in range(E3 // 4):
                        j = i * (E3 // 4) + g
                        dve.wait_ge(y_full, y0 + j + 1)
                        for e4 in range(4):
                            e = 4 * g + e4
                            ins = stt(acc_a[:, i, :], Y[j % 2][:, e4 * D:(e4 + 1) * D], mix2[:, i, e:e + 1], acc_a[:, i, :],
                                      ALU.mult, ALU.add)
                            if e4 < 3:
                                own(ins)
                            else:
                                ins.then_inc(y_free, 1)
                                dve.wait_ge(y_free, y0 + j + 1)
                        if route_next:
                            l3_scale(c + 1, j)

            l3(0, True)
            L3_OWN = 32
            with dve.Fori(1, CHUNKS - 1) as c:
                own.enter(c - 1, L3_OWN)
                l3(c, True)
                own.leave(CHUNKS - 2, L3_OWN)
            l3(CHUNKS - 1, False)

        @block.tensor
        def _(pe):
            def mm(out, lhsT, rhs, start=True, stop=True, shared=False):
                return nc.tensor.matmul(out, lhsT, rhs, start=start, stop=stop, skip_group_check=shared)

            def mm3(out, lhsT, rhs, first, last):
                mm(out, lhsT[0], rhs[0], first, False)
                mm(out, lhsT[1], rhs[0], False, False)
                return mm(out, lhsT[0], rhs[1], False, last)

            def tiles(t):
                return [t[:, i * P:(i + 1) * P] for i in range(TILES)]

            def wait_m(idx):
                pe.wait_ge(m_free, idx - 1)

            def transpose_tiles(bank, acc):
                for i in range(TILES):
                    last = nc.tensor.transpose(bank[:, i * P:(i + 1) * P], acc[:, i, :], ident[:, :])
                last.then_inc(m_full, 1)

            pe.wait_ge(consts, 7)
            pe.wait_ge(ld_x, 16)
            for i in range(2):
                for b in range(4):
                    last = nc.tensor.transpose(U[i][:, b * T:(b + 1) * T], x_in[:, 4 * i + b, :], ident[:, :])
                last.then_inc(u_full, 1)
            pe.wait_ge(ld_first, 16 * FIRST)
            mm(M[0][:, 0:B], cond[:, :], ident[0:B, 0:B])
            mm(M[0][:, B:B + 3 * E + 1], ones_row[:, 0:P], rows[:, :])
            mm(M[0][:, 64:64 + E], l0f_rw_in[:, :], ident[0:E, 0:E]).then_inc(m_full, 1)
            pe.wait_ge(u_free, U_X)
            pe.wait_ge(set_up, 1)
            for i in range(T * B // P):
                mm(M[1][:, i * E:(i + 1) * E], xT[:, i * P:(i + 1) * P], l0_rw[:, 0, :], True, False)
                last = mm(M[1][:, i * E:(i + 1) * E], cond_tok[:, :], l0_rw[:, 1, :], False, True)
            last.then_inc(m_full, 1)

            def bank_l0(*name):
                idx = m_l0(*name)
                wait_m(idx)
                return M[idx % 2]

            def later_set_up():
                pe.wait_ge(ld_small, 16 * SMALL)
                m = bank_l0("mid", 0)
                nc.tensor.transpose(m[:, 0:P], l2_v[:, :], ident[:, :])
                nc.tensor.transpose(m[:, P:2 * P], l2_w_in[:, :], ident[:, :]).then_inc(m_full, 1)
                m = bank_l0("mid", 1)
                pe.wait_ge(set_up, 2)
                mm(m[0:B, 0:3 * D], condT[:, :], gru_c[:, :], stop=False)
                mm(m[0:B, 0:3 * D], ones_row[:, 0:B], gru_b_row[:, :], start=False)
                mm(m[0:B, 3 * D:], ident[0:B, 0:B], cond[:, :], stop=False)
                mm(m[0:B, 3 * D:], ones_row[:, 0:B], fc_bias[:, :], start=False).then_inc(m_full, 1)
                m = bank_l0("mid", 2)
                mm(m[:, 0:2 * E * Q], b1_in[:, :], ident[0:2 * E * Q, 0:2 * E * Q])
                mm(m[:, 128:128 + DA], l3_p_in[:, :], ident[0:DA, 0:DA])
                mm(m[0:DA, 256:256 + NR3 * E3], l3_u_in[:, :], ident[0:NR3 * E3, 0:NR3 * E3]).then_inc(m_full, 1)

            def gru_inputs(chunk):
                for g, bank in ((0, ZR[:, 0:N]), (1, ZR[:, N:2 * N]), (2, HH[:, 0:N])):
                    mm(bank, gru_w[:, g, :], x1[:, at(chunk * N, N)], g != 1, False, True)
                    mm(bank, gru_vb[:, g * D:(g + 1) * D], sel_batch[:, :], False, False, True)

            def gru_gates_of(chunk, t):
                step = chunk * CT + t
                if not isinstance(step, int) or step:
                    pe.wait_ge(gru_h, step)
                for g in range(2):
                    last = mm(ZR[:, at(g * N + t * B, B)], gru_u[:, g, :], h_gru[:, at(t * B, B)], False, False, True)
                last.then_inc(gru_zr, 1)

            def gru_cand_of(chunk, t):
                pe.wait_ge(gru_rh, chunk * CT + t + 1)
                mm(HH[:, at(t * B, B)], gru_u[:, 2, :], rh[:, :], False, False, True).then_inc(gru_hh, 1)

            def rnn_inputs(c):
                if not isinstance(c, int) or c:
                    pe.wait_ge(rnn_h, c * CT)
                mm(ZR[:, 0:N], rnn_w[:, 0, :], x3[:, at(c * N, N)], True, False, True)
                mm(ZR[:, 0:N], rnn_b_row[:, :], ones_row[:, :], False, False, True)

            def rnn_step(c, t):
                step = c * CT + t
                if not isinstance(step, int) or step:
                    pe.wait_ge(rnn_h, step)
                mm(ZR[:, t * B:(t + 1) * B], rnn_w[:, 1, :], h3[:, at(step * B, B)], False, False, True).then_inc(rnn_pre, 1)

            def wait_hidden(n):
                stream, i, k = L0_UNITS[n]
                if (stream, i) == ("C", 0):
                    pe.wait_ge(silu_done, k + 1)
                elif (stream, i) == ("C", 1):
                    pe.wait_ge(gd_full, k + 1)
                else:
                    pe.wait_ge(ga_full, made_by_act(n))

            def project_l0(n):
                stream, i, k = L0_UNITS[n]
                if n == 0:
                    pe.wait_ge(ld_l0, 16 * L0_LOADS)
                if (stream, i, k) == ("F", 0, 0):
                    pe.wait_ge(ld_l0f, 16 * L0F_LOADS)
                if (stream, i) == ("F", 0):
                    pe.wait_ge(m_free, m_l0("c", k) + 1)
                if n >= 2:
                    wait_hidden(n - 2)
                for h in range(2):
                    if stream == "F":
                        w = l0f_up[:, (2 * i + h) * P:(2 * i + h + 1) * P]
                    elif i < 2:
                        w = l0_w13[:, i, h * P:(h + 1) * P]
                    else:
                        w = l0_up[:, 2 * (i - 2) + h, :]
                    x = c0[k % 2][:, :] if stream == "F" else xT[:, k * N:(k + 1) * N]
                    last = mm(U[n % 2][:, h * N:(h + 1) * N], w, x)
                last.then_inc(u_full, 1)

            def down_l0(n):
                if n not in L0_DOWNS:
                    return
                stream, i, k = L0_UNITS[n]
                j = L0_DOWNS.index(n)
                wait_hidden(n)
                if j >= 2:
                    pe.wait_ge(y_free, j - 1)
                y = Y[j % 2]
                for t in range(TILES):
                    for h in range(2):
                        hid = gated[:, n % 4, h * N + t * P:h * N + (t + 1) * P]
                        if stream == "C" and i == 1:
                            last = mm(y[:, t * D:(t + 1) * D], hid, l0_w2[:, h, :], h == 0, h == 1)
                        elif stream == "C":
                            last = mm(y[:, (2 * t + h) * D:(2 * t + h + 1) * D], hid, l0_dn[:, 2 * (i - 2) + h, :])
                        elif i < 2:
                            last = mm(y[:, (2 * t + h) * D:(2 * t + h + 1) * D], hid, l0f_dn[:, 2 * i + h, :])
                        else:
                            last = mm(y[:, t * D:(t + 1) * D], hid, l0f_dn[:, 2 * i + h, :], h == 0, h == 1)
                last.then_inc(y_full, 1)

            def sums_l0(n):
                for back in (4, 5):
                    stream, i, k = L0_UNITS[n - back] if 0 <= n - back < len(L0_UNITS) else ("", 0, 0)
                    if back == 4 and (stream, i) == ("C", 5):
                        pe.wait_ge(acc_third, k + 1)
                        transpose_tiles(bank_l0("c", k), acc_a)
                    if back == 5 and (stream, i) == ("C", 5):
                        pe.wait_ge(m_free, m_l0("c", k) + 1)
                        m = bank_l0("logits", k)
                        for t, x in enumerate(tiles(c0[k % 2])):
                            last = mm(m[:, t * E:(t + 1) * E], x, l0f_rw[:, :])
                        last.then_inc(m_full, 1)
                    if back == 4 and (stream, i) == ("F", 5):
                        pe.wait_ge(y_free, L0_DOWNS.index(n - 4) + 1)
                        transpose_tiles(bank_l0("f", k), acc_b)

            def transpose_w1(n):
                for e in [e for e in range(E3) if W1_SLOTS[e] == n]:
                    if e == 0:
                        pe.wait_ge(ld_w1, 16)
                    m = bank_l0("up", e)
                    for q in range(Q):
                        last = nc.tensor.transpose(m[:, q * P:(q + 1) * P],
                                                   stage[:, e * F + q * P:e * F + (q + 1) * P], ident[:, :])
                    last.then_inc(m_full, 1)

            def idle(*_):
                pass

            def gates_of(step):
                if step == 0:
                    pe.wait_ge(set_up, 3)
                    pe.wait_ge(m_free, m_l0("f", 0) + 1)
                    gru_inputs(0)
                gru_gates_of(0, step)

            for n in range(L0_SLOTS):
                steps = steps_l0(n)
                for step in steps[:1]:
                    gates_of(step)
                if n < len(L0_UNITS):
                    project_l0(n)
                for step in steps[:1]:
                    gru_cand_of(0, step)
                for step in steps[1:]:
                    gates_of(step)
                sums_l0(n)
                if 0 <= n - 2 < len(L0_UNITS):
                    down_l0(n - 2)
                if n == MID_SLOT:
                    later_set_up()
                transpose_w1(n)
                for step in steps[1:]:
                    gru_cand_of(0, step)

            def layer(k, exchanges, l):
                m0, y0, h0 = M0_L12 + k * len(X_BODY), Y0_L12 + (2 * k + l) * E, (2 * k + l) * LU
                x, comb_l, combT = ((l1_in, comb_a, combT_a), (l2_in, comb_b, combT_b))[l]

                def bank(name):
                    wait_m(m0 + exchanges.index(name))
                    return bank_of(exchanges, name)

                def project(u):
                    if u >= 2:
                        pe.wait_ge(hid_full, h0 + u - 1)
                    for h in range(2):
                        col = (2 * u + h) % Q * P
                        last = mm(U[u % 2][:, h * N:(h + 1) * N], up[l][:, u // 2, col:col + P], x[:, :])
                    last.then_inc(u_full, 1)

                def down(e, i):
                    if i == 0:
                        pe.wait_ge(hid_full, h0 + 2 * e + 2)
                        pe.wait_ge(y_free, y0 + e - 1)
                    for q in range(Q):
                        hid = gated[:, (2 * e + q // 2) % 4, (q % 2) * N + i * P:(q % 2) * N + (i + 1) * P]
                        last = mm(Y[e % 2][:, i * D:(i + 1) * D], hid, dn[l][:, e, q, :], q == 0, q == Q - 1)
                    if i == TILES - 1:
                        last.then_inc(y_full, 1)

                def routing(u):
                    if u == 5 - l:
                        pe.wait_ge(comb_ready, 2 * k + l + 1)
                        m = bank(f"w{l}")
                        for i in range(TILES):
                            last = mm(m[0:E, i * P:(i + 1) * P], comb_l[:, i * E:(i + 1) * E], ident[:, :])
                        last.then_inc(m_full, 1)
                    if (l, u) == (1, 6):
                        biases()

                def biases():
                    pe.wait_ge(m_free, m0 + exchanges.index(f"w{l}") + 1)
                    m = bank(f"b{l}")
                    for i in range(TILES):
                        last = mm(m[:, i * D:(i + 1) * D], combT[:, i * P:(i + 1) * P], b2[l][:, :])
                    last.then_inc(m_full, 1)

                def total():
                    pe.wait_ge(y_free, y0 + E)
                    transpose_tiles(bank(f"sum{l}"), (acc_a, acc_b)[l])

                return project, down, routing, total, biases

            def logits(l, idx, bank):
                wait_m(idx)
                for i, xi in enumerate(tiles((l1_in, l2_in)[l])):
                    last = mm(bank[:, i * E:(i + 1) * E], xi, gate_w[:, l, :])
                last.then_inc(m_full, 1)

            def head(c, steps, after, idx, bank, last_of=None):
                gates, cand, _ = steps
                project = layer(c, X_BODY, 0)[0]
                pe.wait_ge(h_moved, c + 1)
                for u in range(2):
                    gates(0, u)
                    if last_of:
                        last_of[1](E - 1, u)
                    cand(0, u)
                    if u == 0:
                        logits(0, idx, bank)
                    project(u)
                    after(0, u)
                if last_of:
                    last_of[3]()

            def rest(k, exchanges, steps, after):
                m0 = M0_L12 + k * len(X_BODY)
                gates, cand, between = steps
                for l in range(2):
                    project, down, routing, total, biases = layer(k, exchanges, l)
                    if l == 1:
                        pe.wait_ge(m_free, m0 + exchanges.index("pre") + 1)
                        logits(1, m0 + exchanges.index("logits1"), bank_of(exchanges, "logits1"))
                    for u in range(2 - 2 * l, LU):
                        gates(l, u)
                        project(u)
                        cand(l, u)
                        if u >= 2:
                            down((u - 2) // 2, u % 2)
                        routing(u)
                        after(l, u)
                    if l == 0:
                        between[0](0)
                        down(E - 1, 0)
                        biases()
                        between[1](0)
                        down(E - 1, 1)
                        between[0](1)
                        total()
                        between[1](1)
                        wait_m(m0 + exchanges.index("z"))
                        pre, z = bank_of(exchanges, "pre"), bank_of(exchanges, "z")
                        mm(pre[:, 0:N], cond[:, :], sel_batch[:, :], True, False, True)
                        pe.wait_ge(m_free, m0 + exchanges.index("sum0") + 1)
                        mm(z[:, 0:N], l2_v[:, :], x1[:, at(k * N, N)]).then_inc(m_full, 1)
                        mm(pre[:, 0:N], l2_wT[:, :], x1[:, at(k * N, N)], False, False, True)
                        between[0](2)
                        pe.wait_ge(m_free, m0 + exchanges.index("z") + 1)
                        mm(pre[:, 0:N], l2_uT[:, :], z1m[:, :], False, True, True).then_inc(m_full, 1)
                        between[1](2)

            def gru_beside(chunk):
                def at_step(do):
                    def steps(l, u):
                        if l == 0 or u >= LATE:
                            do(chunk, l * LU + u)
                    return steps
                between = (lambda n: gru_gates_of(chunk, LU + n), lambda n: gru_cand_of(chunk, LU + n))
                return at_step(gru_gates_of), at_step(gru_cand_of), between

            def next_head(k, steps, after):
                head(k + 1, steps, after, M0_L12 + k * len(X_BODY) + X_BODY.index("logits0"), bank_of(X_BODY, "logits0"),
                     layer(k, X_BODY, 1))

            pe.wait_ge(ld_l1, 16 * L12_LOADS)
            pe.wait_ge(ld_l2, 16 * L12_LOADS)
            pe.wait_ge(gru_h, CT)
            pe.wait_ge(m_free, m_l0("f", 1) + 1)
            gru_inputs(1)
            head(0, gru_beside(1), idle, M_START, M[M_START % 2])
            with pe.Fori(0, CHUNKS - 2) as k:
                rest(k, X_BODY, gru_beside(k + 1), idle)
                pe.wait_ge(gru_h, (k + 2) * CT)
                gru_inputs(k + 2)
                next_head(k, gru_beside(k + 2), idle)
            rest(CHUNKS - 2, X_BODY, gru_beside(CHUNKS - 1), idle)

            def rnn_first(l, u):
                if u == l == 0:
                    rnn_inputs(0)
                rnn_step(l, 2 * u)

            def rnn_second(l, u):
                rnn_step(l, 2 * u + 1)

            m_last = M0_L12 + (CHUNKS - 1) * len(X_BODY)

            def transpose_w2(e):
                if e == E:
                    pe.wait_ge(ld_w2, 16)
                idx, bank = m_last + X_END.index(f"t{e}"), bank_of(X_END, f"t{e}")
                wait_m(idx)
                for q in range(Q):
                    last = nc.tensor.transpose(bank[:, q * P:(q + 1) * P],
                                               stage[:, e * F + q * P:e * F + (q + 1) * P], ident[:, :])
                last.then_inc(m_full, 1)

            def between_last(n):
                if n == 1:
                    rnn_inputs(1)

            def beside_last(l, u):
                def exchange(name):
                    return m_last + X_END.index(name), bank_of(X_END, name)

                if l == 1:
                    if u == 2:
                        l3_address(0, *exchange("addr"))
                    if u == 5:
                        l3_scores(*exchange("score"))
                for e in w2_beside(l, u):
                    transpose_w2(e)
                if (l, u) == (1, 13):
                    l3_weights(0, *exchange("dw"))

            def l3_address(c, idx, bank):
                pe.wait_ge(l3_ready, 2 * c + 1)
                wait_m(idx)
                mm(bank[0:DA, 0:N], l3_pT[:, :], l3_in).then_inc(m_full, 1)

            def l3_scores(idx, bank):
                pe.wait_ge(m_free, idx)
                for i in range(TILES):
                    last = mm(bank[:, i * NR3 * E3:(i + 1) * NR3 * E3], addr[:, i * P:(i + 1) * P], l3_uT[:, :])
                last.then_inc(m_full, 1)

            def l3_weights(c, idx, bank):
                pe.wait_ge(comb_ready, 2 * CHUNKS + 1 + c)
                wait_m(idx)
                for half, r in enumerate((0, 2)):
                    for i in range(TILES):
                        w = (i * NR3 + r) * E3
                        last = mm(bank[0:E3, half * N + i * P:half * N + (i + 1) * P], comb[:, w:w + E3], ident[:, :])
                last.then_inc(m_full, 1)

            def l3_broadcast(c, j):
                if not isinstance(c, int) or c or j >= 2:
                    pe.wait_ge(b_free, c * (E3 // 2) + j - 1)
                for h in range(2):
                    for part in range(2):
                        last = mm((HH, U[1])[j % 2][:, h * N:(h + 1) * N], sel_expert[:, 2 * j + h, :], dwT[part][:, :],
                                  part == 0, part == 1)
                last.then_inc(b_full, 1)

            beside = (rnn_first, rnn_second, (between_last, idle))
            next_head(CHUNKS - 2, beside, beside_last)
            rest(CHUNKS - 1, X_END, beside, beside_last)
            _, down, _, total, _ = layer(CHUNKS - 1, X_END, 1)
            down(E - 1, 0)
            down(E - 1, 1)
            pe.wait_ge(l3_consts, 1)
            for j in range(E3 // 2):
                l3_broadcast(0, j)
                if j == 1:
                    total()

            def l3(c, step, route_next):
                m0, y0 = M0_L3 + c * M_L3, Y0_L3 + c * Y_L3
                n = 0
                for half in range(2):
                    for h in range(2):
                        for e in range(E3):
                            if half == h == 0 and e % 2 == 0:
                                pe.wait_ge(scaled_all, c * (E3 // 2) + e // 2 + 1)
                            q = 2 * half + h
                            last = mm3(U[half][:, h * N:(h + 1) * N], [w[:, e, q * P:(q + 1) * P] for w in l3_up],
                                       [x[:, e, :] for x in scaled], e == 0, e == E3 - 1)
                            if h == 1 and e == E3 - 1:
                                last.then_inc(u_full, 1)
                            n += 1
                            if n % 3 == 0:
                                step(n // 3 - 1)
                            if n == 8 and route_next:
                                l3_address(c + 1, m0, M[0])
                            if n == 14 and route_next:
                                l3_scores(m0 + 1, M[1])
                pe.wait_ge(l3_ready, 2 * c + 2)
                wait_m(m0 + 2 if route_next else m0)
                for i in range(TILES):
                    mm(M[0][:, i * D:(i + 1) * D], dwT_third[:, i * P:(i + 1) * P], l3_b2[:, :], True, False)
                    last = mm(M[0][:, i * D:(i + 1) * D], x3_c[:, i * P:(i + 1) * P], ident[:, :], False, True)
                last.then_inc(m_full, 1)
                if route_next:
                    l3_weights(c + 1, m0 + 3, M[1])
                n = 0
                for i in range(TILES):
                    for g in range(E3 // 4):
                        j = i * (E3 // 4) + g
                        pe.wait_ge(y_free, y0 + j - 1)
                        for q in range(2 * Q):
                            hid, w = (hid3[0], (0, 1)) if q < Q else (hid3[1], (0,))
                            if j == 0 and q % 2 == 0:
                                pe.wait_ge(l3_hid_hi if q < Q else l3_hid_all, 2 * c + q % Q // 2 + 1)
                            b = q % Q
                            hid = hid[:, b // 2, (b % 2) * N + i * P:(b % 2) * N + (i + 1) * P]
                            for side in w:
                                last = mm(Y[j % 2][:, :], hid, l3_dn[g][side][:, b, :, :], q == side == 0, q == 2 * Q - 1)
                            if q == 2 * Q - 1:
                                last.then_inc(y_full, 1)
                            if q % 2 == 1:
                                n += 1
                                if n % 3 != 0:
                                    step(16 + n - n // 3 - 1)
                        if route_next:
                            if j == 0:
                                pe.wait_ge(m_free, m0 + 4)
                            l3_broadcast(c + 1, j)

            with pe.Fori(0, 2) as c:
                rnn_inputs(c + 2)
                l3(c, lambda s: rnn_step(c + 2, s), True)
            l3(2, idle, True)
            l3(CHUNKS - 1, idle, False)


_INS = ["x", "cond_1024", "fside_Bx1x1024x16_0", "L0_cond_router_W", "L0_cond_router_bias", "L0_cond_w1", "L0_cond_w3",
        "L0_cond_w2", "L0_cond_W1e", "L0_cond_W2e", "L0_ffn_router_w", "L0_ffn_w1", "L0_ffn_w2", "L1_cond_W_z",
        "L1_cond_U_z", "L1_cond_C_z", "L1_cond_b_z", "L1_cond_W_r", "L1_cond_U_r", "L1_cond_C_r", "L1_cond_b_r",
        "L1_cond_W", "L1_cond_U", "L1_cond_C", "L1_cond_b", "L1_ffn_W1", "L1_ffn_b1", "L1_ffn_W2", "L1_ffn_b2",
        "L1_ffn_gate_w", "L1_ffn_gate_b", "L1_ffn_temperature", "L2_cond_W", "L2_cond_fc_bias", "L2_ffn_gate_w",
        "L2_ffn_gate_b", "L2_ffn_w1", "L2_ffn_b1", "L2_ffn_w2", "L2_ffn_b2", "L3_cond_Wx", "L3_cond_Wh", "L3_cond_b",
        "L3_ffn_P_w", "L3_ffn_U1", "L3_ffn_U2", "L3_ffn_U3", "L3_ffn_W1", "L3_ffn_W2", "L3_ffn_b2"]


def kernel(**inputs):
    import numpy as np
    import concourse.bacc as bacc
    from concourse.bass_utils import run_bass_kernel_spmd

    nc = bacc.Bacc("TRN2", target_bir_lowering=False, num_devices=1, dynamic_dma_scratch_size=1024)
    arrays, aps = {}, {}
    for name in _INS:
        arr = np.atleast_1d(np.ascontiguousarray(inputs[name]))
        arrays[name + "_dram"] = arr
        aps[name] = nc.dram_tensor(name + "_dram", arr.shape, F32, kind="ExternalInput").ap()
    out = nc.dram_tensor("out_dram", (B, T, D), F32, kind="ExternalOutput").ap()
    adaln_ffn_program(nc, aps, out)
    result = run_bass_kernel_spmd(nc, [arrays], core_ids=[0])
    return result.results[0]["out_dram"]
```
